# Optimizing a Trainium2 kernel written in Bass

```python
import numpy as np
import jax
import jax.numpy as jnp

def _softmax(x, axis=-1):
    return jax.nn.softmax(x, axis=axis)

def _gelu(x):
    return jax.nn.gelu(x, approximate=True)

def _silu(x):
    return jax.nn.silu(x)

def _sigmoid(x):
    return jax.nn.sigmoid(x)

def _layernorm(x, axis=-1, eps=1e-05):
    m = jnp.mean(x, axis=axis, keepdims=True)
    v = jnp.var(x, axis=axis, keepdims=True)
    return (x - m) / jnp.sqrt(v + eps)

def _scatter_add(tgt, idx, src, axis=0):
    return tgt.at[idx].add(src)

def _segment_sum(src, seg, n):
    return jax.ops.segment_sum(src, seg, n)
kernel_name = 'mk_xattn_ffn_d4_seqx_r4_4601e8'

def setup_inputs(seed: int=0):
    np.random.seed(seed)
    _w = jnp.asarray

    def _rec_inputs():
        import jax
        import jax.numpy as jnp
        _rk = jax.random.key(seed)
        x = 0.0002417 + 0.9998 * jax.random.normal(jax.random.fold_in(_rk, 1), (8, 512, 256), jnp.float32)
        _lenS = 512 - jax.random.randint(jax.random.fold_in(_rk, 7), (8,), 0, max(1, 512 // 4) + 1, jnp.int32)
        _lenS2 = 512 - jax.random.randint(jax.random.fold_in(_rk, 8), (8,), 0, max(1, 512 // 4) + 1, jnp.int32)
        _ctx_1024P = jax.random.normal(jax.random.fold_in(_rk, 11), (8, 16, 256), jnp.float32)
        _ctx_1024c = jax.random.dirichlet(jax.random.fold_in(_rk, 511), 0.3 * jnp.ones((16,), jnp.float32), (8, 512))
        _ctx_1024t = jnp.einsum('bsk,bkd->bsd', _ctx_1024c, _ctx_1024P)
        _ctx_1024t = _ctx_1024t * jax.lax.rsqrt(jnp.mean(jnp.square(_ctx_1024t)) + 1e-12) * 0.953939
        ctx_1024 = 7.22013e-05 + 1.00017 * (_ctx_1024t + 0.3 * jax.random.normal(jax.random.fold_in(_rk, 611), (8, 512, 256), jnp.float32))
        _validS = jnp.arange(512)[None, :] < _lenS[:, None]
        _validS2 = jnp.arange(512)[None, :] < _lenS2[:, None]
        _causal = jnp.tril(jnp.ones((512, 512), dtype=bool))
        mask_BxS2_if0 = jnp.where(jnp.ones((8, 512), dtype=bool), 0, 1).astype(jnp.int32)
        mask_Bx1x1xS2_bf1 = jnp.ones((8, 1, 1, 512), dtype=bool)
        return (x, ctx_1024, mask_BxS2_if0, mask_Bx1x1xS2_bf1)
    x, ctx_1024, mask_BxS2_if0, mask_Bx1x1xS2_bf1 = _rec_inputs()

    def _L0_xattn_setup():
        import jax, jax.numpy as jnp
        import numpy as np
        import math
        B, M, D, H, NK = (4, 512, 256, 16, 5)
        HD = D // H

        def _gather_pad0(x, idx):
            Bx, Hx, W, hd = x.shape
            valid = (idx >= 0) & (idx < W)
            idxc = jnp.clip(idx, 0, W - 1).reshape(Bx, Hx, -1)
            g = jnp.take_along_axis(x, idxc[..., None], axis=2)
            g = g.reshape(idx.shape + (hd,))
            return g * valid[..., None].astype(x.dtype)
        key = jax.random.key(seed)
        ks = jax.random.split(key, 9)
        w = lambda k, shape: jax.random.normal(k, shape, jnp.float32) * 0.02
        return {'k': jax.random.normal(ks[0], (B, M, D), jnp.float32), 'v': jax.random.normal(ks[1], (B, M, D), jnp.float32), 'q': jax.random.normal(ks[2], (B, M, D), jnp.float32), 'mask': jnp.zeros((B, M), jnp.int32), 'Wk': w(ks[3], (D, D)), 'bk': jnp.zeros((D,), jnp.float32), 'Wv': w(ks[4], (D, D)), 'bv': jnp.zeros((D,), jnp.float32), 'Wq': w(ks[5], (D, D)), 'bq': jnp.zeros((D,), jnp.float32), 'Woff': w(ks[6], (H * NK, D)), 'boff': jnp.zeros((H * NK,), jnp.float32), 'Wo': w(ks[7], (D, D)), 'bo': jnp.zeros((D,), jnp.float32)}
    _L0_xattn_all = _L0_xattn_setup()
    _L0_xattn_in = {k: v for k, v in _L0_xattn_all.items() if k in ('Wk', 'bk', 'Wv', 'bv', 'Wq', 'bq', 'Woff', 'boff', 'Wo', 'bo')}
    del _L0_xattn_all

    def _L0_ffn_setup():
        import jax, jax.numpy as jnp
        import numpy as np
        B, S, D, E, F = (2, 512, 256, 14, 512)
        key = jax.random.key(seed)
        k = jax.random.split(key, 4)
        h = jax.random.normal(k[0], (B, S, D), dtype=jnp.float32)
        router_w = jax.random.normal(k[1], (D, E), dtype=jnp.float32) * 0.02
        w1 = jax.random.uniform(k[2], (E, D, F), dtype=jnp.float32, minval=-1.0, maxval=1.0) * float(np.sqrt(6.0 / D))
        w2 = jax.random.uniform(k[3], (E, F, D), dtype=jnp.float32, minval=-1.0, maxval=1.0) * float(np.sqrt(6.0 / F))
        b1 = jnp.zeros((E, F), dtype=jnp.float32)
        b2 = jnp.zeros((E, D), dtype=jnp.float32)
        return {'h': h, 'router_w': router_w, 'w1': w1, 'b1': b1, 'w2': w2, 'b2': b2}
    _L0_ffn_all = _L0_ffn_setup()
    _L0_ffn_in = {k: v for k, v in _L0_ffn_all.items() if k in ('router_w', 'w1', 'b1', 'w2', 'b2')}
    del _L0_ffn_all

    def _L1_xattn_setup():
        import jax, jax.numpy as jnp
        import numpy as np
        H = 16
        key = jax.random.key(seed)
        ks = jax.random.split(key, 11)
        B, S, D = (2, 512, 256)
        sc = 0.02
        return {'q_in': jax.random.normal(ks[0], (B, S, D), jnp.float32), 'k_in': jax.random.normal(ks[1], (B, S, D), jnp.float32), 'v_in': jax.random.normal(ks[2], (B, S, D), jnp.float32), 'Wq': jax.random.normal(ks[3], (D, D), jnp.float32) * sc, 'bq': jax.random.normal(ks[4], (D,), jnp.float32) * sc, 'Wk': jax.random.normal(ks[5], (D, D), jnp.float32) * sc, 'bk': jax.random.normal(ks[6], (D,), jnp.float32) * sc, 'Wv': jax.random.normal(ks[7], (D, D), jnp.float32) * sc, 'bv': jax.random.normal(ks[8], (D,), jnp.float32) * sc, 'Wo': jax.random.normal(ks[9], (D, D), jnp.float32) * sc, 'bo': jax.random.normal(ks[10], (D,), jnp.float32) * sc}
    _L1_xattn_all = _L1_xattn_setup()
    _L1_xattn_in = {k: v for k, v in _L1_xattn_all.items() if k in ('Wq', 'bq', 'Wk', 'bk', 'Wv', 'bv', 'Wo', 'bo')}
    del _L1_xattn_all

    def _L1_ffn_setup():
        import jax, jax.numpy as jnp
        import numpy as np
        EPS = 1e-08

        def _ste(x, q):
            return x + jax.lax.stop_gradient(q - x)

        def quant_act_uint8(x):
            s = jax.lax.stop_gradient(jnp.maximum(jnp.max(x), EPS)) / 255.0
            q = jnp.clip(jnp.round(x / s), 0.0, 255.0) * s
            return (_ste(x, q), s)

        def quant_weight_int8_perchannel(w):
            s = jax.lax.stop_gradient(jnp.maximum(jnp.max(jnp.abs(w), axis=1, keepdims=True), EPS)) / 127.0
            q = jnp.clip(jnp.round(w / s), -128.0, 127.0) * s
            return (_ste(w, q), s[:, 0])

        def quant_bias_int32(b, s_in, s_w):
            s = jax.lax.stop_gradient(s_in * s_w)
            q = jnp.round(b / s) * s
            return _ste(b, q)

        def quant_linear(x, w, b):
            xq, s_in = quant_act_uint8(x)
            wq, s_w = quant_weight_int8_perchannel(w)
            bq = quant_bias_int32(b, s_in, s_w)
            return jnp.einsum('btd,fd->btf', xq, wq) + bq
        key = jax.random.key(seed)
        k1, k2, k3, k4, k5 = jax.random.split(key, 5)
        B, S, D, F = (4, 512, 256, 1024)
        return {'x': jax.random.normal(k1, (B, S, D), dtype=jnp.float32), 'w1': jax.random.normal(k2, (F, D), dtype=jnp.float32) * (1.0 / np.sqrt(D)), 'b1': jax.random.normal(k3, (F,), dtype=jnp.float32) * 0.01, 'w2': jax.random.normal(k4, (D, F), dtype=jnp.float32) * (1.0 / np.sqrt(F)), 'b2': jax.random.normal(k5, (D,), dtype=jnp.float32) * 0.01}
    _L1_ffn_all = _L1_ffn_setup()
    _L1_ffn_in = {k: v for k, v in _L1_ffn_all.items() if k in ('w1', 'b1', 'w2', 'b2')}
    del _L1_ffn_all

    def _L2_xattn_setup():
        import jax, jax.numpy as jnp
        import numpy as np
        D_MODEL = 256
        D_K = 64
        HEADS = 16
        key = jax.random.key(seed)
        k = jax.random.split(key, 7)
        b, s = (4, 512)
        scale = 1.0 / np.sqrt(D_MODEL)
        return {'input_Q': jax.random.normal(k[0], (b, s, D_MODEL), jnp.float32), 'input_K': jax.random.normal(k[1], (b, s, D_MODEL), jnp.float32), 'input_V': jax.random.normal(k[2], (b, s, D_MODEL), jnp.float32), 'W_Q': jax.random.normal(k[3], (D_MODEL, D_K * HEADS), jnp.float32) * scale, 'W_K': jax.random.normal(k[4], (D_MODEL, D_K * HEADS), jnp.float32) * scale, 'W_V': jax.random.normal(k[5], (D_MODEL, D_K * HEADS), jnp.float32) * scale, 'W_O': jax.random.normal(k[6], (D_K * HEADS, D_MODEL), jnp.float32) * scale}
    _L2_xattn_all = _L2_xattn_setup()
    _L2_xattn_in = {k: v for k, v in _L2_xattn_all.items() if k in ('W_Q', 'W_K', 'W_V', 'W_O')}
    del _L2_xattn_all

    def _L2_ffn_setup():
        import jax, jax.numpy as jnp
        import numpy as np
        DIM = 256

        def _reference_tuple_inner(x, W_r, W_k, W_v, mu_r, mu_k):
            B, T, C = x.shape
            x_prev = jnp.concatenate([jnp.zeros((B, 1, C), x.dtype), x[:, :-1, :]], axis=1)
            xr = mu_r * x + (1.0 - mu_r) * x_prev
            xk = mu_k * x + (1.0 - mu_k) * x_prev
            r = jax.nn.sigmoid(jnp.einsum('btc,dc->btd', xr, W_r))
            k = jnp.einsum('btc,dc->btd', xk, W_k)
            k_act = jnp.square(jax.nn.relu(k))
            out = r * jnp.einsum('btc,dc->btd', k_act, W_v)
            new_state = x[:, -1, :]
            return (out, new_state)
        key = jax.random.key(seed)
        ks = jax.random.split(key, 6)
        B, T, C = (8, 512, DIM)
        x = jax.random.normal(ks[0], (B, T, C), dtype=jnp.float32)
        s = 1.0 / np.sqrt(C)
        W_r = jax.random.uniform(ks[1], (C, C), jnp.float32, -s, s)
        W_k = jax.random.uniform(ks[2], (C, C), jnp.float32, -s, s)
        W_v = jax.random.uniform(ks[3], (C, C), jnp.float32, -s, s)
        mu_r = jax.random.uniform(ks[4], (C,), jnp.float32)
        mu_k = jax.random.uniform(ks[5], (C,), jnp.float32)
        return {'x': x, 'W_r': W_r, 'W_k': W_k, 'W_v': W_v, 'mu_r': mu_r, 'mu_k': mu_k}
    _L2_ffn_all = _L2_ffn_setup()
    _L2_ffn_in = {k: v for k, v in _L2_ffn_all.items() if k in ('W_r', 'W_k', 'W_v', 'mu_r', 'mu_k')}
    del _L2_ffn_all

    def _L3_xattn_setup():
        import jax, jax.numpy as jnp
        import numpy as np
        D_MODEL = 256
        NUM_HEADS = 16
        D_K = D_MODEL // NUM_HEADS
        B, S = (4, 512)
        key = jax.random.key(seed)
        ks = jax.random.split(key, 12)
        scale = 1.0 / np.sqrt(D_MODEL)
        inp = {'query': jax.random.normal(ks[0], (B, S, D_MODEL), jnp.float32), 'key': jax.random.normal(ks[1], (B, S, D_MODEL), jnp.float32), 'value': jax.random.normal(ks[2], (B, S, D_MODEL), jnp.float32), 'mask': jnp.ones((B, 1, 1, S), dtype=bool), 'Wq': jax.random.normal(ks[3], (D_MODEL, D_MODEL), jnp.float32) * scale, 'bq': jnp.zeros((D_MODEL,), jnp.float32), 'Wk': jax.random.normal(ks[4], (D_MODEL, D_MODEL), jnp.float32) * scale, 'bk': jnp.zeros((D_MODEL,), jnp.float32), 'Wv': jax.random.normal(ks[5], (D_MODEL, D_MODEL), jnp.float32) * scale, 'bv': jnp.zeros((D_MODEL,), jnp.float32), 'Wo': jax.random.normal(ks[6], (D_MODEL, D_MODEL), jnp.float32) * scale, 'bo': jnp.zeros((D_MODEL,), jnp.float32)}
        return inp
    _L3_xattn_all = _L3_xattn_setup()
    _L3_xattn_in = {k: v for k, v in _L3_xattn_all.items() if k in ('Wq', 'bq', 'Wk', 'bk', 'Wv', 'bv', 'Wo', 'bo')}
    del _L3_xattn_all

    def _L3_ffn_setup():
        import jax, jax.numpy as jnp
        import numpy as np
        import math
        B, S, D = (2, 512, 256)
        H = 16
        HD = D // H
        FFN = 512
        E = 8
        TOP_K = 2
        CAP_FACTOR = 1.25
        EPS = 1e-06
        BASE = 10000.0
        CAP = max(math.ceil(B * S * TOP_K * CAP_FACTOR / E), 1)

        def _rmsnorm(x, w):
            rms = jax.lax.rsqrt(jnp.mean(x * x, axis=-1, keepdims=True) + EPS)
            return w * x * rms

        def _rope(x, cos, sin):
            xr = x[..., 0::2]
            xi = x[..., 1::2]
            c = cos[None, None]
            s_ = sin[None, None]
            out_r = xr * c - xi * s_
            out_i = xr * s_ + xi * c
            return jnp.stack([out_r, out_i], axis=-1).reshape(x.shape)

        def _mha(x, w_qkv, w_o):
            b, s, d = x.shape
            qkv = x @ w_qkv
            q, k, v = jnp.split(qkv, 3, axis=-1)
            to_heads = lambda z: z.reshape(b, s, H, HD).transpose(0, 2, 1, 3)
            q, k, v = (to_heads(q), to_heads(k), to_heads(v))
            theta = BASE ** (-2.0 * (jnp.arange(HD // 2, dtype=jnp.float32) / HD))
            freqs = jnp.arange(s, dtype=jnp.float32)[:, None] * theta[None, :]
            cos, sin = (jnp.cos(freqs), jnp.sin(freqs))
            q = _rope(q, cos, sin)
            k = _rope(k, cos, sin)
            scores = jnp.einsum('bhqd,bhkd->bhqk', q, k) / jnp.sqrt(jnp.float32(HD))
            causal = jnp.tril(jnp.ones((s, s), dtype=bool))
            scores = jnp.where(causal, scores, -jnp.inf)
            attn = jax.nn.softmax(scores, axis=-1)
            y = jnp.einsum('bhqk,bhkd->bhqd', attn, v)
            y = y.transpose(0, 2, 1, 3).reshape(b, s, d)
            return y @ w_o

        def _moe(x, w_router, w1, w2):
            b, s, d = x.shape
            t = b * s
            xf = x.reshape(t, d)
            logits = xf.astype(jnp.float32) @ w_router.astype(jnp.float32)
            probs = jax.nn.softmax(logits, axis=-1)
            g, eidx = jax.lax.top_k(probs, TOP_K)
            fg = g.reshape(t * TOP_K)
            fe = eidx.reshape(t * TOP_K)
            tok_of = jnp.arange(t * TOP_K) // TOP_K
            masked = jnp.where(fe[None, :] == jnp.arange(E)[:, None], fg[None, :], -jnp.inf)
            vals, idx = jax.lax.top_k(masked, CAP)
            valid = jnp.isfinite(vals)
            gates = jnp.where(valid, vals, 0.0)
            tok = tok_of[idx]
            xe = xf[tok]
            h = jax.nn.relu(jnp.einsum('ecd,edf->ecf', xe, w1))
            ye = jnp.einsum('ecf,efd->ecd', h, w2) * gates[..., None]
            y = jnp.zeros_like(xf).at[tok.reshape(-1)].add(ye.reshape(-1, d))
            return y.reshape(b, s, d)
        key = jax.random.key(seed)
        ks = jax.random.split(key, 6)
        sd = 0.02
        return {'x': jax.random.normal(ks[0], (B, S, D), jnp.float32), 'g1': jnp.ones((D,), jnp.float32), 'w_qkv': jax.random.normal(ks[1], (D, 3 * D), jnp.float32) * sd, 'w_o': jax.random.normal(ks[2], (D, D), jnp.float32) * sd, 'g2': jnp.ones((D,), jnp.float32), 'w_router': jax.random.normal(ks[3], (D, E), jnp.float32) * sd, 'w1': jax.random.normal(ks[4], (E, D, FFN), jnp.float32) * sd, 'w2': jax.random.normal(ks[5], (E, FFN, D), jnp.float32) * sd}
    _L3_ffn_all = _L3_ffn_setup()
    _L3_ffn_in = {k: v for k, v in _L3_ffn_all.items() if k in ('g1', 'w_qkv', 'w_o', 'g2', 'w_router', 'w1', 'w2')}
    del _L3_ffn_all
    return {'x': x, 'ctx_1024': ctx_1024, 'mask_BxS2_if0': mask_BxS2_if0, 'mask_Bx1x1xS2_bf1': mask_Bx1x1xS2_bf1, 'L0_xattn_Wk': _L0_xattn_in['Wk'], 'L0_xattn_bk': _L0_xattn_in['bk'], 'L0_xattn_Wv': _L0_xattn_in['Wv'], 'L0_xattn_bv': _L0_xattn_in['bv'], 'L0_xattn_Wq': _L0_xattn_in['Wq'], 'L0_xattn_bq': _L0_xattn_in['bq'], 'L0_xattn_Woff': _L0_xattn_in['Woff'], 'L0_xattn_boff': _L0_xattn_in['boff'], 'L0_xattn_Wo': _L0_xattn_in['Wo'], 'L0_xattn_bo': _L0_xattn_in['bo'], 'L0_ffn_router_w': _L0_ffn_in['router_w'], 'L0_ffn_w1': _L0_ffn_in['w1'], 'L0_ffn_b1': _L0_ffn_in['b1'], 'L0_ffn_w2': _L0_ffn_in['w2'], 'L0_ffn_b2': _L0_ffn_in['b2'], 'L1_xattn_Wq': _L1_xattn_in['Wq'], 'L1_xattn_bq': _L1_xattn_in['bq'], 'L1_xattn_Wk': _L1_xattn_in['Wk'], 'L1_xattn_bk': _L1_xattn_in['bk'], 'L1_xattn_Wv': _L1_xattn_in['Wv'], 'L1_xattn_bv': _L1_xattn_in['bv'], 'L1_xattn_Wo': _L1_xattn_in['Wo'], 'L1_xattn_bo': _L1_xattn_in['bo'], 'L1_ffn_w1': _L1_ffn_in['w1'], 'L1_ffn_b1': _L1_ffn_in['b1'], 'L1_ffn_w2': _L1_ffn_in['w2'], 'L1_ffn_b2': _L1_ffn_in['b2'], 'L2_xattn_W_Q': _L2_xattn_in['W_Q'], 'L2_xattn_W_K': _L2_xattn_in['W_K'], 'L2_xattn_W_V': _L2_xattn_in['W_V'], 'L2_xattn_W_O': _L2_xattn_in['W_O'], 'L2_ffn_W_r': _L2_ffn_in['W_r'], 'L2_ffn_W_k': _L2_ffn_in['W_k'], 'L2_ffn_W_v': _L2_ffn_in['W_v'], 'L2_ffn_mu_r': _L2_ffn_in['mu_r'], 'L2_ffn_mu_k': _L2_ffn_in['mu_k'], 'L3_xattn_Wq': _L3_xattn_in['Wq'], 'L3_xattn_bq': _L3_xattn_in['bq'], 'L3_xattn_Wk': _L3_xattn_in['Wk'], 'L3_xattn_bk': _L3_xattn_in['bk'], 'L3_xattn_Wv': _L3_xattn_in['Wv'], 'L3_xattn_bv': _L3_xattn_in['bv'], 'L3_xattn_Wo': _L3_xattn_in['Wo'], 'L3_xattn_bo': _L3_xattn_in['bo'], 'L3_ffn_g1': _L3_ffn_in['g1'], 'L3_ffn_w_qkv': _L3_ffn_in['w_qkv'], 'L3_ffn_w_o': _L3_ffn_in['w_o'], 'L3_ffn_g2': _L3_ffn_in['g2'], 'L3_ffn_w_router': _L3_ffn_in['w_router'], 'L3_ffn_w1': _L3_ffn_in['w1'], 'L3_ffn_w2': _L3_ffn_in['w2']}

def reference(x, ctx_1024, mask_BxS2_if0, mask_Bx1x1xS2_bf1, L0_xattn_Wk, L0_xattn_bk, L0_xattn_Wv, L0_xattn_bv, L0_xattn_Wq, L0_xattn_bq, L0_xattn_Woff, L0_xattn_boff, L0_xattn_Wo, L0_xattn_bo, L0_ffn_router_w, L0_ffn_w1, L0_ffn_b1, L0_ffn_w2, L0_ffn_b2, L1_xattn_Wq, L1_xattn_bq, L1_xattn_Wk, L1_xattn_bk, L1_xattn_Wv, L1_xattn_bv, L1_xattn_Wo, L1_xattn_bo, L1_ffn_w1, L1_ffn_b1, L1_ffn_w2, L1_ffn_b2, L2_xattn_W_Q, L2_xattn_W_K, L2_xattn_W_V, L2_xattn_W_O, L2_ffn_W_r, L2_ffn_W_k, L2_ffn_W_v, L2_ffn_mu_r, L2_ffn_mu_k, L3_xattn_Wq, L3_xattn_bq, L3_xattn_Wk, L3_xattn_bk, L3_xattn_Wv, L3_xattn_bv, L3_xattn_Wo, L3_xattn_bo, L3_ffn_g1, L3_ffn_w_qkv, L3_ffn_w_o, L3_ffn_g2, L3_ffn_w_router, L3_ffn_w1, L3_ffn_w2):
    import jax
    import jax.numpy as jnp

    def _L0_xattn_ref(k, v, q, mask, Wk, bk, Wv, bv, Wq, bq, Woff, boff, Wo, bo):
        import jax, jax.numpy as jnp
        import numpy as np
        import math
        B, M, D, H, NK = (4, 512, 256, 16, 5)
        HD = D // H

        def _gather_pad0(x, idx):
            Bx, Hx, W, hd = x.shape
            valid = (idx >= 0) & (idx < W)
            idxc = jnp.clip(idx, 0, W - 1).reshape(Bx, Hx, -1)
            g = jnp.take_along_axis(x, idxc[..., None], axis=2)
            g = g.reshape(idx.shape + (hd,))
            return g * valid[..., None].astype(x.dtype)
        Bq, Q, _ = q.shape
        key_len = k.shape[1]
        K = jnp.einsum('bmd,ed->bme', k, Wk) + bk
        V = jnp.einsum('bmd,ed->bme', v, Wv) + bv
        Qp = jnp.einsum('bqd,ed->bqe', q, Wq) + bq
        off = jnp.einsum('bqd,ed->bqe', Qp, Woff) + boff
        off = off.reshape(Bq, Q, H, NK).transpose(0, 2, 1, 3)
        Kh = K.reshape(Bq, key_len, H, HD).transpose(0, 2, 1, 3)
        Vh = V.reshape(Bq, key_len, H, HD).transpose(0, 2, 1, 3)
        Qh = Qp.reshape(Bq, Q, H, HD).transpose(0, 2, 1, 3)
        loc = jnp.arange(Q, dtype=jnp.float32)[:, None]
        left = -NK // 2
        ref = jnp.arange(left, NK + left, dtype=jnp.float32)
        sign_lens = (1 - mask).sum(-1).astype(jnp.float32) - 1.0
        loc_x = jnp.mod(ref + off + loc, sign_lens[:, None, None, None])
        xg = loc_x / (key_len - 1) * 2.0 - 1.0
        ix = ((xg + 1.0) * key_len - 1.0) / 2.0
        x0 = jnp.floor(ix)
        dx = ix - x0
        i0 = x0.astype(jnp.int32)
        i1 = i0 + 1
        w0 = (1.0 - dx)[..., None]
        w1 = dx[..., None]
        sk = 0.5 * (w0 * _gather_pad0(Kh, i0) + w1 * _gather_pad0(Kh, i1))
        sv = 0.5 * (w0 * _gather_pad0(Vh, i0) + w1 * _gather_pad0(Vh, i1))
        scores = jnp.einsum('bhqd,bhqkd->bhqk', Qh / math.sqrt(HD), sk)
        attn = jax.nn.softmax(scores, axis=-1)
        ctx = jnp.einsum('bhqk,bhqkd->bhqd', attn, sv)
        ctx = ctx.transpose(0, 2, 1, 3).reshape(Bq, Q, H * HD)
        return jnp.einsum('bqd,ed->bqe', ctx, Wo) + bo

    def _L0_ffn_ref(h, router_w, w1, b1, w2, b2):
        import jax, jax.numpy as jnp
        import numpy as np
        B, S, D, E, F = (2, 512, 256, 14, 512)
        Bb, Ss, Dd = h.shape
        x = h.reshape(-1, Dd)
        logits = x @ router_w
        assignments = jnp.argmax(logits, axis=-1)
        probs = jax.nn.softmax(logits, axis=-1)
        weights = jnp.take_along_axis(probs, assignments[:, None], axis=1)[:, 0]
        hid = jnp.einsum('nd,edf->nef', x, w1) + b1
        hid = jax.nn.gelu(hid, approximate=False)
        all_out = jnp.einsum('nef,efd->ned', hid, w2) + b2
        sel = jnp.take_along_axis(all_out, assignments[:, None, None], axis=1)[:, 0, :]
        moe_out = (sel * weights[:, None]).reshape(Bb, Ss, Dd)
        return moe_out

    def _L1_xattn_ref(q_in, k_in, v_in, Wq, bq, Wk, bk, Wv, bv, Wo, bo):
        import jax, jax.numpy as jnp
        import numpy as np
        H = 16
        B, S, D = q_in.shape
        hd = D // H
        q = q_in @ Wq.T + bq
        k = k_in @ Wk.T + bk
        v = v_in @ Wv.T + bv
        q = q.reshape(B, S, H, hd).transpose(0, 2, 1, 3)
        k = k.reshape(B, S, H, hd).transpose(0, 2, 1, 3)
        v = v.reshape(B, S, H, hd).transpose(0, 2, 1, 3)
        scores = jnp.einsum('bhqd,bhkd->bhqk', q, k) / jnp.sqrt(jnp.float32(hd))
        probs = jax.nn.softmax(scores, axis=-1)
        attn = jnp.einsum('bhqk,bhkd->bhqd', probs, v)
        concat = attn.transpose(0, 2, 1, 3).reshape(B, S, D)
        return concat @ Wo.T + bo

    def _L1_ffn_ref(x, w1, b1, w2, b2):
        import jax, jax.numpy as jnp
        import numpy as np
        EPS = 1e-08

        def _ste(x, q):
            return x + jax.lax.stop_gradient(q - x)

        def quant_act_uint8(x):
            s = jax.lax.stop_gradient(jnp.maximum(jnp.max(x), EPS)) / 255.0
            q = jnp.clip(jnp.round(x / s), 0.0, 255.0) * s
            return (_ste(x, q), s)

        def quant_weight_int8_perchannel(w):
            s = jax.lax.stop_gradient(jnp.maximum(jnp.max(jnp.abs(w), axis=1, keepdims=True), EPS)) / 127.0
            q = jnp.clip(jnp.round(w / s), -128.0, 127.0) * s
            return (_ste(w, q), s[:, 0])

        def quant_bias_int32(b, s_in, s_w):
            s = jax.lax.stop_gradient(s_in * s_w)
            q = jnp.round(b / s) * s
            return _ste(b, q)

        def quant_linear(x, w, b):
            xq, s_in = quant_act_uint8(x)
            wq, s_w = quant_weight_int8_perchannel(w)
            bq = quant_bias_int32(b, s_in, s_w)
            return jnp.einsum('btd,fd->btf', xq, wq) + bq
        h = jax.nn.relu(quant_linear(x, w1, b1))
        return quant_linear(h, w2, b2)

    def _L2_xattn_ref(input_Q, input_K, input_V, W_Q, W_K, W_V, W_O):
        import jax, jax.numpy as jnp
        import numpy as np
        D_MODEL = 256
        D_K = 64
        HEADS = 16
        b, s, _ = input_Q.shape

        def split_heads(x):
            return x.reshape(b, -1, HEADS, D_K).transpose(0, 2, 1, 3)
        Q = split_heads(input_Q @ W_Q)
        K = split_heads(input_K @ W_K)
        V = split_heads(input_V @ W_V)
        scores = jnp.einsum('bhsd,bhtd->bhst', Q, K) / np.sqrt(D_K)
        attn = jax.nn.softmax(scores, axis=-1)
        value = jnp.einsum('bhst,bhtd->bhsd', attn, V)
        value = value.transpose(0, 2, 1, 3).reshape(b, s, HEADS * D_K)
        return value @ W_O

    def _L2_ffn_ref(x, W_r, W_k, W_v, mu_r, mu_k):
        import jax, jax.numpy as jnp
        import numpy as np
        DIM = 256

        def _reference_tuple_inner(x, W_r, W_k, W_v, mu_r, mu_k):
            B, T, C = x.shape
            x_prev = jnp.concatenate([jnp.zeros((B, 1, C), x.dtype), x[:, :-1, :]], axis=1)
            xr = mu_r * x + (1.0 - mu_r) * x_prev
            xk = mu_k * x + (1.0 - mu_k) * x_prev
            r = jax.nn.sigmoid(jnp.einsum('btc,dc->btd', xr, W_r))
            k = jnp.einsum('btc,dc->btd', xk, W_k)
            k_act = jnp.square(jax.nn.relu(k))
            out = r * jnp.einsum('btc,dc->btd', k_act, W_v)
            new_state = x[:, -1, :]
            return (out, new_state)
        return _reference_tuple_inner(x, W_r, W_k, W_v, mu_r, mu_k)[0]

    def _L3_xattn_ref(query, key, value, mask, Wq, bq, Wk, bk, Wv, bv, Wo, bo):
        import jax, jax.numpy as jnp
        import numpy as np
        D_MODEL = 256
        NUM_HEADS = 16
        D_K = D_MODEL // NUM_HEADS
        B, S = (4, 512)
        q = query @ Wq.T + bq
        k = key @ Wk.T + bk
        v = value @ Wv.T + bv

        def split(x):
            b, s, _ = x.shape
            return x.reshape(b, s, NUM_HEADS, D_K).transpose(0, 2, 1, 3)
        q, k, v = (split(q), split(k), split(v))
        scores = jnp.einsum('bhqd,bhkd->bhqk', q, k) / jnp.sqrt(jnp.float32(D_K))
        scores = jnp.where(mask, scores, jnp.float32(-jnp.inf))
        probs = jax.nn.softmax(scores, axis=-1)
        ctx = jnp.einsum('bhqk,bhkd->bhqd', probs, v)
        b = ctx.shape[0]
        ctx = ctx.transpose(0, 2, 1, 3).reshape(b, -1, D_MODEL)
        return ctx @ Wo.T + bo

    def _L3_ffn_ref(x, g1, w_qkv, w_o, g2, w_router, w1, w2):
        import jax, jax.numpy as jnp
        import numpy as np
        import math
        B, S, D = (2, 512, 256)
        H = 16
        HD = D // H
        FFN = 512
        E = 8
        TOP_K = 2
        CAP_FACTOR = 1.25
        EPS = 1e-06
        BASE = 10000.0
        CAP = max(math.ceil(B * S * TOP_K * CAP_FACTOR / E), 1)

        def _rmsnorm(x, w):
            rms = jax.lax.rsqrt(jnp.mean(x * x, axis=-1, keepdims=True) + EPS)
            return w * x * rms

        def _rope(x, cos, sin):
            xr = x[..., 0::2]
            xi = x[..., 1::2]
            c = cos[None, None]
            s_ = sin[None, None]
            out_r = xr * c - xi * s_
            out_i = xr * s_ + xi * c
            return jnp.stack([out_r, out_i], axis=-1).reshape(x.shape)

        def _mha(x, w_qkv, w_o):
            b, s, d = x.shape
            qkv = x @ w_qkv
            q, k, v = jnp.split(qkv, 3, axis=-1)
            to_heads = lambda z: z.reshape(b, s, H, HD).transpose(0, 2, 1, 3)
            q, k, v = (to_heads(q), to_heads(k), to_heads(v))
            theta = BASE ** (-2.0 * (jnp.arange(HD // 2, dtype=jnp.float32) / HD))
            freqs = jnp.arange(s, dtype=jnp.float32)[:, None] * theta[None, :]
            cos, sin = (jnp.cos(freqs), jnp.sin(freqs))
            q = _rope(q, cos, sin)
            k = _rope(k, cos, sin)
            scores = jnp.einsum('bhqd,bhkd->bhqk', q, k) / jnp.sqrt(jnp.float32(HD))
            causal = jnp.tril(jnp.ones((s, s), dtype=bool))
            scores = jnp.where(causal, scores, -jnp.inf)
            attn = jax.nn.softmax(scores, axis=-1)
            y = jnp.einsum('bhqk,bhkd->bhqd', attn, v)
            y = y.transpose(0, 2, 1, 3).reshape(b, s, d)
            return y @ w_o

        def _moe(x, w_router, w1, w2):
            b, s, d = x.shape
            t = b * s
            xf = x.reshape(t, d)
            logits = xf.astype(jnp.float32) @ w_router.astype(jnp.float32)
            probs = jax.nn.softmax(logits, axis=-1)
            g, eidx = jax.lax.top_k(probs, TOP_K)
            fg = g.reshape(t * TOP_K)
            fe = eidx.reshape(t * TOP_K)
            tok_of = jnp.arange(t * TOP_K) // TOP_K
            masked = jnp.where(fe[None, :] == jnp.arange(E)[:, None], fg[None, :], -jnp.inf)
            vals, idx = jax.lax.top_k(masked, CAP)
            valid = jnp.isfinite(vals)
            gates = jnp.where(valid, vals, 0.0)
            tok = tok_of[idx]
            xe = xf[tok]
            h = jax.nn.relu(jnp.einsum('ecd,edf->ecf', xe, w1))
            ye = jnp.einsum('ecf,efd->ecd', h, w2) * gates[..., None]
            y = jnp.zeros_like(xf).at[tok.reshape(-1)].add(ye.reshape(-1, d))
            return y.reshape(b, s, d)
        x = x + _mha(_rmsnorm(x, g1), w_qkv, w_o)
        x = x + _moe(_rmsnorm(x, g2), w_router, w1, w2)
        return x
    x = x + _L0_xattn_ref(ctx_1024, ctx_1024, _layernorm(x, axis=-1), mask_BxS2_if0, L0_xattn_Wk, L0_xattn_bk, L0_xattn_Wv, L0_xattn_bv, L0_xattn_Wq, L0_xattn_bq, L0_xattn_Woff, L0_xattn_boff, L0_xattn_Wo, L0_xattn_bo)
    x = x + _L0_ffn_ref(_layernorm(x, axis=-1), L0_ffn_router_w, L0_ffn_w1, L0_ffn_b1, L0_ffn_w2, L0_ffn_b2)
    x = x + _L1_xattn_ref(_layernorm(x, axis=-1), ctx_1024, ctx_1024, L1_xattn_Wq, L1_xattn_bq, L1_xattn_Wk, L1_xattn_bk, L1_xattn_Wv, L1_xattn_bv, L1_xattn_Wo, L1_xattn_bo)
    x = x + _L1_ffn_ref(_layernorm(x, axis=-1), L1_ffn_w1, L1_ffn_b1, L1_ffn_w2, L1_ffn_b2)
    x = x + _L2_xattn_ref(_layernorm(x, axis=-1), ctx_1024, ctx_1024, L2_xattn_W_Q, L2_xattn_W_K, L2_xattn_W_V, L2_xattn_W_O)
    x = x + _L2_ffn_ref(_layernorm(x, axis=-1), L2_ffn_W_r, L2_ffn_W_k, L2_ffn_W_v, L2_ffn_mu_r, L2_ffn_mu_k)
    x = x + _L3_xattn_ref(_layernorm(x, axis=-1), ctx_1024, ctx_1024, mask_Bx1x1xS2_bf1, L3_xattn_Wq, L3_xattn_bq, L3_xattn_Wk, L3_xattn_bk, L3_xattn_Wv, L3_xattn_bv, L3_xattn_Wo, L3_xattn_bo)
    x = x + _L3_ffn_ref(_layernorm(x, axis=-1), L3_ffn_g1, L3_ffn_w_qkv, L3_ffn_w_o, L3_ffn_g2, L3_ffn_w_router, L3_ffn_w1, L3_ffn_w2)
    return x

_drawn_inputs = setup_inputs


def setup_inputs(seed=0):
    import zlib

    import numpy as np

    out = dict(_drawn_inputs(seed))
    spreads = {'L0_xattn_bk': (0.0, 0.8),
     'L0_xattn_bv': (0.0, 0.326),
     'L0_xattn_bq': (0.0, 0.8),
     'L0_xattn_boff': (0.0, 0.8),
     'L0_xattn_bo': (0.0, 0.1),
     'L0_ffn_b1': (0.0, 0.703),
     'L0_ffn_b2': (0.0, 0.698),
     'L3_xattn_bq': (0.0, 0.673),
     'L3_xattn_bk': (0.0, 0.8),
     'L3_xattn_bv': (0.0, 0.1),
     'L3_xattn_bo': (0.0, 0.1),
     'L3_ffn_g1': (1.0, 0.6),
     'L3_ffn_g2': (1.0, 0.6)}
    factors = {'L0_xattn_Wk': 8.0,
     'L0_xattn_Wq': 6.009,
     'L0_xattn_Woff': 6.207,
     'L1_xattn_Wq': 8.0,
     'L1_xattn_bq': 8.0,
     'L1_xattn_Wk': 8.0,
     'L1_xattn_bk': 8.0,
     'L1_xattn_bv': 8.0,
     'L1_xattn_bo': 3.574,
     'L1_ffn_b1': 8.0,
     'L1_ffn_b2': 8.0,
     'L2_ffn_W_r': 3.92,
     'L2_ffn_mu_r': 8.0,
     'L3_ffn_w_router': 8.0,
     'L3_ffn_w1': 8.0,
     'L3_ffn_w2': 8.0}
    for name, (base, spread) in spreads.items():
        noise = np.random.default_rng([zlib.crc32(name.encode()), seed]).standard_normal(out[name].shape)
        drawn = base * np.exp(spread * noise) if base else spread * noise
        out[name] = jnp.asarray(drawn.astype(out[name].dtype))
    for name, factor in factors.items():
        out[name] = (out[name] * factor).astype(out[name].dtype)
    return out
```

```python
from contextlib import ExitStack

import concourse.bass as bass
from concourse import mybir

F32 = mybir.dt.float32
BF16 = mybir.dt.bfloat16
I32 = mybir.dt.int32
U32 = mybir.dt.uint32
ACT = mybir.ActivationFunctionType
ALU = mybir.AluOpType
AX_X = mybir.AxisListType.X

P = 128
B, S, D = 8, 512, 256
QT = S // P
TILES = B * QT
DK = D // P
H = 16
SLOT = 32
LN_EPS = 1e-5
RMS_EPS = 1e-6
NEG = -1e30
ROUND = 1.5 * 2.0 ** 23
NK = 5
E0, E3, FFN = 14, 8, 512
CAP = 320


class Core:

    def __init__(self, nc, ctx, dram):
        self.nc, self.ctx, self.dram = nc, ctx, dram
        self.n = 0

        def sb(name, shape, dt=F32):
            return ctx.enter_context(nc.sbuf_tensor(name, shape, dt))

        self.x = sb("x_res", [P, TILES, D])
        self.nT = sb("normed_T", [P, DK, B * S])
        self.ctxT = sb("ctx_T", [P, DK, B * S])
        self.ident = sb("ident", [P, P])
        self.ones = sb("ones", [P, P])
        self.eps = sb("eps", [P, 2])

        self.stage_sems = []

    def sem(self, name):
        self.n += 1
        self.stage_sems.append(self.nc.alloc_semaphore(name=f"{name}_{self.n}"))
        return self.stage_sems[-1]

    def end_stage(self):
        self.nc.clear_and_free_semaphores(self.stage_sems)
        self.nc.all_engine_barrier()
        self.stage_sems = []


def batch_cols(b):
    return bass.ds(b * S, S)


def load_stage(nc, C):
    loaded, made, memset_done = C.sem("loaded"), C.sem("made"), C.sem("memset")
    with nc.Block() as block:
        @block.sync
        def _(sp):
            sp.dma_start(C.x[:], C.dram["x"].rearrange("b (t p) d -> p (b t) d", p=P)).then_inc(loaded, 16)
            sp.dma_start(C.ctxT[:], C.dram["ctx_T"].rearrange("(k p) t -> p k t", p=P)).then_inc(loaded, 16)
            sp.wait_ge(loaded, 32)

        @block.gpsimd
        def _(pool):
            nc.gpsimd.memset(C.ones[:], 1.0).then_inc(memset_done, 1)
            nc.gpsimd.memset(C.eps[:, 0:1], LN_EPS).then_inc(made, 1)
            nc.gpsimd.memset(C.eps[:, 1:2], RMS_EPS).then_inc(made, 1)
            pool.wait_ge(memset_done, 1)
            nc.gpsimd.affine_select(out=C.ident[:], in_=C.ones[:], compare_op=ALU.is_equal, fill=0.0, base=0,
                                    pattern=[[-1, P]], channel_multiplier=1).then_inc(made, 1)
    C.end_stage()


def norm_stage(nc, C, keep=None, gain=None, layer=True, src=None):
    src = C.x if src is None else src
    uid = C.n
    with ExitStack() as ctx:
        def sb(name, shape, dt=F32):
            return ctx.enter_context(nc.sbuf_tensor(f"{name}_{uid}", shape, dt))

        stats = sb("stats", [P, QT, 6])
        mv = sb("mean_var", [P, QT, 2])
        std = sb("std", [P, 2, QT])
        rstd = sb("rstd", [P, 2, QT])
        sq = sb("mean_square", [P, QT])
        normed = sb("normed", [P, 2, QT, D])
        gain_row = sb("gain_row", [P, D])
        turned = [ctx.enter_context(nc.psum_tensor(f"turned{i}_{uid}", [P, S], F32)) for i in range(2 * DK)]
        gain_loaded, var_ready, std_ready = C.sem("gain_loaded"), C.sem("var_ready"), C.sem("std_ready")
        normed_ready, turned_ready, copied = C.sem("normed_ready"), C.sem("turned_ready"), C.sem("copied")
        norms = int(layer) + int(gain is not None)

        with nc.Block() as block:
            if gain is not None:
                @block.sync
                def _(sp):
                    sp.dma_start(gain_row[:], gain.partition_broadcast(P)).then_inc(gain_loaded, 16)

            @block.vector
            def _(dve):
                if gain is not None:
                    dve.wait_ge(gain_loaded, 16)

                def moments(tiles):
                    for t in range(QT):
                        nc.vector.bn_stats(stats[:, t, :], tiles(t))
                    dve.drain()
                    for t in range(QT):
                        nc.vector.bn_aggr(mv[:, t, :], stats[:, t, :])
                    dve.drain()

                with dve.Fori(0, B // 2) as pair:
                    for u in range(2):
                        b = pair * 2 + u
                        tiles = lambda t: src[:, b * QT + t, :]
                        out = normed[:, u]
                        if layer:
                            moments(tiles)
                            nc.vector.tensor_copy(sq[:], mv[:, :, 1]).then_inc(var_ready, 1)
                            dve.wait_ge(std_ready, b * norms + 1)
                            nc.vector.reciprocal(rstd[:, 0], std[:, 0])
                            dve.drain()
                            if u == 0:
                                dve.wait_ge(turned_ready, pair * 2)
                            else:
                                dve.wait_ge(turned_ready, pair * 2)
                            for t in range(QT):
                                to = out[:, t, :] if keep is None else keep[:, b * QT + t, :]
                                ins = nc.vector.tensor_scalar(to, tiles(t), mv[:, t, 0:1], rstd[:, 0, t:t + 1],
                                                              ALU.subtract, ALU.mult)
                            if gain is None:
                                ins.then_inc(normed_ready, 1)
                            else:
                                dve.drain()
                                tiles = lambda t: keep[:, b * QT + t, :]
                        if gain is not None:
                            moments(tiles)
                            nc.vector.tensor_tensor(sq[:], mv[:, :, 0], mv[:, :, 0], ALU.mult)
                            dve.drain()
                            nc.vector.tensor_tensor(sq[:], sq[:], mv[:, :, 1], ALU.add).then_inc(var_ready, 1)
                            dve.wait_ge(std_ready, b * norms + norms)
                            nc.vector.reciprocal(rstd[:, 1], std[:, 1])
                            dve.drain()
                            dve.wait_ge(turned_ready, pair * 2)
                            for t in range(QT):
                                ins = nc.vector.scalar_tensor_tensor(out=out[:, t, :], in0=tiles(t),
                                                                     scalar=rstd[:, 1, t:t + 1], in1=gain_row[:],
                                                                     op0=ALU.mult, op1=ALU.mult)
                            ins.then_inc(normed_ready, 1)

            @block.tensor
            def _(pe):
                with pe.Fori(0, B // 2) as pair:
                    for u in range(2):
                        b = pair * 2 + u
                        pe.wait_ge(normed_ready, b + 1)
                        pe.wait_ge(copied, pair * 2)
                        for k in range(DK):
                            for t in range(QT):
                                ins = nc.tensor.transpose(turned[2 * u + k][:, t * P:(t + 1) * P],
                                                          normed[:, u, t, k * P:(k + 1) * P], C.ident[:])
                        ins.then_inc(turned_ready, 1)

            @block.scalar
            def _(act):
                with act.Fori(0, B // 2) as pair:
                    for u in range(2):
                        b = pair * 2 + u
                        for n in range(norms):
                            rms = gain is not None and n == norms - 1
                            act.wait_ge(var_ready, b * norms + n + 1)
                            nc.scalar.activation(std[:, int(rms)], sq[:], ACT.Sqrt,
                                                 bias=C.eps[:, int(rms):int(rms) + 1]).then_inc(std_ready, 1)
                        act.wait_ge(turned_ready, b + 1)
                        for k in range(DK):
                            ins = nc.scalar.activation(C.nT[:, k, batch_cols(b)], turned[2 * u + k][:], ACT.Copy)
                        ins.then_inc(copied, 1)
    C.end_stage()


def store_stage(nc, C):
    stored = C.sem("stored")
    with nc.Block() as block:
        @block.sync
        def _(sp):
            sp.dma_start(C.dram["out"].rearrange("b (t p) d -> p (b t) d", p=P), C.x[:]).then_inc(stored, 16)
            sp.wait_ge(stored, 16)


def attention_stage(nc, C, w, hd, cross=True, causal=False, rope=False, biased=False, masked=False, res=None):
    res = C.x if res is None else res
    uid = C.n
    slot = max(hd, SLOT)
    HG = P // slot
    G = H // HG
    U = HG * QT
    VC = HG * hd
    KO = H * hd // P
    scale = float(hd) ** -0.5
    kvT = C.ctxT if cross else C.nT

    with ExitStack() as ctx:
        def sb(name, shape, dt=F32):
            return ctx.enter_context(nc.sbuf_tensor(f"{name}_{uid}", shape, dt))

        def psum(name, n):
            return [ctx.enter_context(nc.psum_tensor(f"{name}{i}_{uid}", [P, 512], F32)) for i in range(n)]

        names = ["q", "k"] + (["q_swap", "k_swap"] if rope else [])
        w_all = {m: sb(f"w_{m}_all", [P, DK, G * P]) for m in names}
        w_g = {m: [sb(f"w_{m}_group{u}", [P, DK, P]) for u in range(2)] for m in names}
        wv = sb("w_v", [P, DK, H * hd])
        wo = sb("w_o", [P, KO, D])
        q = [sb(f"q{u}", [P, S]) for u in range(2)]
        k = [sb(f"k{u}", [P, S]) for u in range(2)]
        v = [sb(f"v{u}", [P, QT, VC]) for u in range(2)]
        kv_chunk = sb("kv_chunk", [P, DK, S])
        probs = [sb(f"probs{i}", [P, S]) for i in range(3)]
        probsT = [sb(f"probsT{i}", [P, S]) for i in range(2)]
        neg_max = sb("neg_max", [P, 4])
        sums = [sb(f"sums{u}", [P, U]) for u in range(2)]
        recip = sb("recip", [P, U])
        heads = sb("heads_out", [P, QT, H * hd])
        headsT = sb("heads_out_T", [P, KO, S])
        added = sb("added", [P, D])
        if rope:
            cos, sin = sb("cos", [P, S]), sb("sin", [P, S])
            turn_a, turn_b = sb("turn_a", [P, S]), sb("turn_b", [P, S])
        if biased:
            bq, bk = sb("b_q", [P, G]), sb("b_k", [P, G])
            bv, bo = sb("b_v", [P, H * hd]), sb("b_o", [P, D])
        if masked:
            mask_in = sb("mask_in", [1, B * S], mybir.dt.uint8)
            mask = sb("mask_bias", [1, B * S])
            mask_slot = sb("mask_slot", [1, P])
        if causal:
            future = sb("future", [P, P])
        ps_proj, ps_s, ps_t, ps_o = psum("ps_proj", 2), psum("ps_scores", 2), psum("ps_turned", 2), psum("ps_out", 2)

        weights, prepared = C.sem("weights"), C.sem("prepared")
        kv_staged, w_staged, projected = C.sem("kv_staged"), C.sem("w_staged"), C.sem("projected")
        q_ready, v_ready = C.sem("q_ready"), C.sem("v_ready")
        scored, maxed, exp_done = C.sem("scored"), C.sem("maxed"), C.sem("exp_done")
        turned, copied, summed = C.sem("turned"), C.sem("copied"), C.sem("summed")
        normalised, headsT_turned, headsT_copied = C.sem("normalised"), C.sem("headsT_turned"), C.sem("headsT_copied")
        out_ready, out_taken = C.sem("out_ready"), C.sem("out_taken")

        loads = [(w_all[m], w[m].rearrange("(c p) n -> p c n", p=P)) for m in names]
        loads += [(wv, w["v"].rearrange("(c p) n -> p c n", p=P)), (wo, w["o"].rearrange("(c p) n -> p c n", p=P))]
        if rope:
            loads += [(cos, w["cos"]), (sin, w["sin"])]
        if biased:
            loads += [(bq, w["bq"]), (bk, w["bk"]),
                      (bv, w["bv"].partition_broadcast(P)), (bo, w["bo"].partition_broadcast(P))]
        if masked:
            loads += [(mask_in, w["mask"]), (mask_slot, w["mask_slot"])]
        if causal:
            loads += [(future, w["future"])]

        def keys(t):
            return (t + 1) * P if causal else S

        def unit(s):
            return s // QT, s % QT

        with nc.Block() as block:
            @block.sync
            def _(sp):
                for to, of in loads:
                    sp.dma_start(to[:], of).then_inc(weights, 16)

            @block.gpsimd
            def _(pool):
                pool.wait_ge(weights, 16 * len(loads))
                with pool.Fori(0, B) as b:
                    pool.wait_ge(projected, b * G)
                    nc.gpsimd.tensor_copy(kv_chunk[:], kvT[:, :, batch_cols(b)]).then_inc(kv_staged, 1)
                    with pool.Fori(0, G // 2) as pair:
                        for u in range(2):
                            g = pair * 2 + u
                            pool.wait_ge(projected, b * G + pair * 2)
                            for m in names:
                                nc.gpsimd.tensor_copy(w_g[m][u][:], w_all[m][:, :, bass.ds(g * P, P)]) \
                                    .then_inc(w_staged, 1)

            @block.tensor
            def _(pe):
                pe.wait_ge(weights, 16 * len(loads))
                pe.wait_ge(prepared, 1)
                with pe.Fori(0, B) as b:
                    with pe.Fori(0, G // 2) as pair:
                        for u in range(2):
                            g = pair * 2 + u
                            n = b * G + g
                            pe.wait_ge(w_staged, (n + 1) * len(names))
                            pe.wait_ge(kv_staged, b + 1)
                            pe.wait_ge(out_taken, b * QT)
                            pe.wait_ge(exp_done, n * U)
                            pe.wait_ge(copied, n * U)
                            for m, bank in zip(names, ps_proj + ps_s):
                                src = kv_chunk[:] if m[0] == "k" and cross else None
                                last = not (masked and m == "k")
                                for c in range(DK):
                                    rhs = C.nT[:, c, batch_cols(b)] if m[0] == "q" or not cross else kv_chunk[:, c, :]
                                    nc.tensor.matmul(bank[:], w_g[m][u][:, c, :], rhs, start=(c == 0),
                                                     stop=(c == DK - 1 and last))
                                if not last:
                                    nc.tensor.matmul(bank[:], mask_slot[:], mask[:, batch_cols(b)],
                                                     start=False, stop=True)
                            for t in range(QT):
                                for c in range(DK):
                                    ins = nc.tensor.matmul(ps_t[0][:, t * VC:(t + 1) * VC],
                                                           kv_chunk[:, c, t * P:(t + 1) * P],
                                                           wv[:, c, bass.ds(g * VC, VC)], start=(c == 0),
                                                           stop=(c == DK - 1))
                            ins.then_inc(projected, 1)
                            pe.wait_ge(q_ready, n + 1)
                            pe.wait_ge(v_ready, n + 1)
                            for s in range(U + 2):
                                if s < U:
                                    h, t = unit(s)
                                    part = slice(h * slot, (h + 1) * slot)
                                    if s >= 2:
                                        pe.wait_ge(exp_done, n * U + s - 1)
                                    ins = nc.tensor.matmul(ps_s[s % 2][:, :keys(t)], q[u][part, t * P:(t + 1) * P],
                                                           k[u][part, :keys(t)], start=True, stop=not causal)
                                    if causal:
                                        ins = nc.tensor.matmul(ps_s[s % 2][:, t * P:keys(t)], C.ident[:], future[:],
                                                               start=False, stop=True)
                                    ins.then_inc(scored, 1)
                                if 1 <= s <= U:
                                    i = s - 1
                                    pe.wait_ge(exp_done, n * U + i + 1)
                                    if i >= 2:
                                        pe.wait_ge(copied, n * U + i - 1)
                                    for c in range(keys(unit(i)[1]) // P):
                                        ins = nc.tensor.transpose(ps_t[i % 2][:, c * P:(c + 1) * P],
                                                                  probs[i % 3][:, c * P:(c + 1) * P], C.ident[:])
                                    ins.then_inc(turned, 1)
                                if s >= 2:
                                    i = s - 2
                                    h, t = unit(i)
                                    pe.wait_ge(copied, n * U + i + 1)
                                    if i == 0:
                                        pe.wait_ge(normalised, n + 1)
                                    nk = keys(t) // P
                                    for c in range(nk):
                                        ins = nc.tensor.matmul(ps_o[u][:, i * hd:(i + 1) * hd],
                                                               probsT[i % 2][:, c * P:(c + 1) * P],
                                                               v[u][:, c, h * hd:(h + 1) * hd],
                                                               start=(c == 0), stop=(c == nk - 1))
                                    ins.then_inc(summed, 1)
                    pe.wait_ge(normalised, (b + 1) * G + 2)
                    for c in range(KO):
                        if c >= 2:
                            pe.wait_ge(headsT_copied, b * KO + c - 1)
                        for t in range(QT):
                            ins = nc.tensor.transpose(ps_t[c % 2][:, t * P:(t + 1) * P],
                                                      heads[:, t, c * P:(c + 1) * P], C.ident[:])
                        ins.then_inc(headsT_turned, 1)
                    pe.wait_ge(headsT_copied, (b + 1) * KO)
                    for t in range(QT):
                        if t >= 2:
                            pe.wait_ge(out_taken, b * QT + t - 1)
                        for c in range(KO):
                            ins = nc.tensor.matmul(ps_proj[t % 2][:, :D], headsT[:, c, t * P:(t + 1) * P], wo[:, c, :],
                                                   start=(c == 0), stop=(c == KO - 1))
                        ins.then_inc(out_ready, 1)

            @block.scalar
            def _(act):
                act.wait_ge(prepared, 1)
                with act.Fori(0, B) as b:
                    with act.Fori(0, G // 2) as pair:
                        for u in range(2):
                            g = pair * 2 + u
                            n = b * G + g
                            if not rope:
                                act.wait_ge(projected, n + 1)
                                nc.scalar.activation(q[u][:], ps_proj[0][:], ACT.Identity, scale=scale,
                                                     bias=bq[:, bass.ds(g, 1)] if biased else 0.0)
                                nc.scalar.activation(k[u][:], ps_proj[1][:], ACT.Identity,
                                                     bias=bk[:, bass.ds(g, 1)] if biased else 0.0).then_inc(q_ready, 1)
                            for s in range(U):
                                act.wait_ge(maxed, n * U + s + 1)
                                if s >= 3:
                                    act.wait_ge(turned, n * U + s - 2)
                                cols = keys(unit(s)[1])
                                nc.scalar.activation(probs[s % 3][:, :cols], ps_s[s % 2][:, :cols], ACT.Exp,
                                                     bias=neg_max[:, s % 4:s % 4 + 1],
                                                     accum_out=sums[u][:, s:s + 1]).then_inc(exp_done, 1)

            @block.vector
            def _(dve):
                dve.wait_ge(weights, 16 * len(loads))
                if masked:
                    nc.vector.tensor_scalar(mask[:], mask_in[:], 1.0, -NEG, ALU.subtract, ALU.mult)
                if biased:
                    nc.vector.tensor_scalar(bq[:], bq[:], scale, None, ALU.mult)
                dve.drain().then_inc(prepared, 1)
                dve.sem_inc(normalised, 2)
                with dve.Fori(0, B) as b:
                    with dve.Fori(0, G // 2) as pair:
                        for u in range(2):
                            g = pair * 2 + u
                            n = b * G + g
                            dve.wait_ge(projected, n + 1)
                            if rope:
                                for to, a, swap, by in ((q[u], ps_proj[0], ps_s[0], scale), (k[u], ps_proj[1], ps_s[1], 1.0)):
                                    nc.vector.scalar_tensor_tensor(out=turn_a[:], in0=a[:], scalar=by, in1=cos[:],
                                                                   op0=ALU.mult, op1=ALU.mult)
                                    nc.vector.scalar_tensor_tensor(out=turn_b[:], in0=swap[:], scalar=by, in1=sin[:],
                                                                   op0=ALU.mult, op1=ALU.mult)
                                    dve.drain()
                                    ins = nc.vector.tensor_tensor(to[:], turn_a[:], turn_b[:], ALU.add)
                                    dve.drain()
                                dve.sem_inc(q_ready, 1)
                            values = ps_t[0][:, :QT * VC].rearrange("p (t c) -> p t c", t=QT)
                            if biased:
                                nc.vector.tensor_tensor(v[u][:], values, bv[:, bass.ds(g * VC, VC)].unsqueeze(1)
                                                        .broadcast_to([P, QT, VC]), ALU.add).then_inc(v_ready, 1)
                            else:
                                nc.vector.tensor_copy(v[u][:], values).then_inc(v_ready, 1)
                            for s in range(U + 1):
                                if s < U:
                                    dve.wait_ge(scored, n * U + s + 1)
                                    nc.vector.tensor_reduce(neg_max[:, s % 4:s % 4 + 1],
                                                            ps_s[s % 2][:, :keys(unit(s)[1])], AX_X, ALU.max,
                                                            negate=True).then_inc(maxed, 1)
                                if s >= 1:
                                    i = s - 1
                                    cols = keys(unit(i)[1])
                                    dve.wait_ge(turned, n * U + i + 1)
                                    if i >= 2:
                                        dve.wait_ge(summed, n * U + i - 1)
                                    nc.vector.tensor_copy(probsT[i % 2][:, :cols], ps_t[i % 2][:, :cols]) \
                                        .then_inc(copied, 1)
                            dve.wait_ge(exp_done, (n + 1) * U)
                            nc.vector.reciprocal(recip[:], sums[u][:])
                            dve.drain()
                            dve.wait_ge(summed, (n + 1) * U)
                            to = heads[:, :, bass.ds(g * VC, VC)].rearrange("p t (h d) -> p t h d", h=HG)
                            of = ps_o[u][:, :U * hd].rearrange("p (h t d) -> p t h d", h=HG, t=QT)
                            by = recip[:].rearrange("p (h t) -> p t h", h=HG).unsqueeze(3).broadcast_to([P, QT, HG, hd])
                            nc.vector.tensor_tensor(to, of, by, ALU.mult).then_inc(normalised, 1)
                    for c in range(KO):
                        dve.wait_ge(headsT_turned, b * KO + c + 1)
                        nc.vector.tensor_copy(headsT[:, c, :], ps_t[c % 2][:]).then_inc(headsT_copied, 1)
                    for t in range(QT):
                        dve.wait_ge(out_ready, b * QT + t + 1)
                        x_tile = res[:, b * QT + t, :]
                        if biased:
                            nc.vector.tensor_tensor(added[:], ps_proj[t % 2][:, :D], bo[:], ALU.add).then_inc(out_taken, 1)
                            dve.drain()
                            nc.vector.tensor_tensor(x_tile, x_tile, added[:], ALU.add)
                            dve.drain()
                        else:
                            nc.vector.tensor_tensor(x_tile, x_tile, ps_proj[t % 2][:, :D], ALU.add).then_inc(out_taken, 1)
    C.end_stage()




def stage_tensors(nc, ctx, uid):
    def sb(name, shape, dt=F32):
        return ctx.enter_context(nc.sbuf_tensor(f"{name}_{uid}", shape, dt))

    def psum(name, n, dt=F32):
        return [ctx.enter_context(nc.psum_tensor(f"{name}{i}_{uid}", [P, 2048 // mybir.dt.size(dt)], dt)) for i in range(n)]

    return sb, psum


def channel_mix_stage(nc, C, w):
    with ExitStack() as ctx:
        sb, psum = stage_tensors(nc, ctx, C.n)
        wr, wk, wv = (sb(n, [P, DK, D]) for n in ("w_r", "w_k", "w_v"))
        mu, rest = sb("mu", [P, 2, DK]), sb("one_less_mu", [P, 2, DK])
        earlier = sb("earlier", [P, S])
        mixed = [sb(f"mixed{u}", [P, 2, DK, S]) for u in range(2)]
        k_act = [sb(f"k_act{u}", [P, DK, S]) for u in range(2)]
        gate, gated = sb("gate", [P, 2, D]), sb("gated", [P, D])
        ps_k, ps_o = psum("ps_k", 2 * DK), psum("ps_rv", QT)
        weights, mixed_ready, k_ready = C.sem("weights"), C.sem("mixed_ready"), C.sem("k_ready")
        k_acted, out_ready, gate_ready, out_taken = C.sem("k_acted"), C.sem("out_ready"), C.sem("gate_ready"), C.sem("out_taken")

        with nc.Block() as block:
            @block.sync
            def _(sp):
                for to, of in ((wr, w["r"]), (wk, w["k"]), (wv, w["v"])):
                    sp.dma_start(to[:], of.rearrange("(c p) n -> p c n", p=P)).then_inc(weights, 16)
                sp.dma_start(mu[:], w["mu"]).then_inc(weights, 16)

            @block.vector
            def _(dve):
                dve.wait_ge(weights, 64)
                nc.vector.tensor_scalar(rest[:], mu[:], -1.0, 1.0, ALU.mult, ALU.add)
                nc.vector.memset(earlier[:, 0:1], 0.0)
                dve.drain()
                with dve.Fori(0, B // 2) as pair:
                    for u in range(2):
                        b = pair * 2 + u
                        dve.wait_ge(out_ready, pair * 2 * QT)
                        for i in range(2):
                            for c in range(DK):
                                nc.vector.tensor_scalar(earlier[:, 1:], C.nT[:, c, bass.ds(b * S, S - 1)],
                                                        rest[:, i, c:c + 1], None, ALU.mult)
                                dve.drain()
                                nc.vector.scalar_tensor_tensor(out=mixed[u][:, i, c, :], in0=C.nT[:, c, batch_cols(b)],
                                                               scalar=mu[:, i, c:c + 1], in1=earlier[:],
                                                               op0=ALU.mult, op1=ALU.add)
                                dve.drain()
                        dve.sem_inc(mixed_ready, 1)
                        for c in range(DK):
                            dve.wait_ge(k_ready, b * DK + c + 1)
                            bank = ps_k[u * DK + c]
                            ins = nc.vector.tensor_scalar(k_act[u][:, c, :], bank[:], 0.0, None, ALU.max)
                            dve.drain()
                            ins = nc.vector.tensor_tensor(k_act[u][:, c, :], k_act[u][:, c, :], k_act[u][:, c, :], ALU.mult)
                            ins.then_inc(k_acted, 1)
                        for t in range(QT):
                            dve.wait_ge(gate_ready, b * QT + t + 1)
                            nc.vector.tensor_tensor(gated[:], gate[:, t % 2, :], ps_o[t][:, D:], ALU.mult).then_inc(out_taken, 1)
                            dve.drain()
                            x_tile = C.x[:, b * QT + t, :]
                            nc.vector.tensor_tensor(x_tile, x_tile, gated[:], ALU.add)
                            dve.drain()

            @block.tensor
            def _(pe):
                pe.wait_ge(weights, 64)
                with pe.Fori(0, B // 2) as pair:
                    for u in range(2):
                        b = pair * 2 + u
                        pe.wait_ge(mixed_ready, b + 1)
                        pe.wait_ge(k_acted, pair * 2 * DK)
                        for m in range(DK):
                            for c in range(DK):
                                ins = nc.tensor.matmul(ps_k[u * DK + m][:], wk[:, c, m * P:(m + 1) * P],
                                                       mixed[u][:, 1, c, :], start=(c == 0), stop=(c == DK - 1))
                            ins.then_inc(k_ready, 1)
                        for t in range(QT):
                            pe.wait_ge(out_taken, b * QT)
                            for c in range(DK):
                                nc.tensor.matmul(ps_o[t][:, :D], mixed[u][:, 0, c, t * P:(t + 1) * P], wr[:, c, :],
                                                 start=(c == 0), stop=(c == DK - 1))
                            pe.wait_ge(k_acted, (b + 1) * DK)
                            for c in range(DK):
                                ins = nc.tensor.matmul(ps_o[t][:, D:], k_act[u][:, c, t * P:(t + 1) * P], wv[:, c, :],
                                                       start=(c == 0), stop=(c == DK - 1))
                            ins.then_inc(out_ready, 1)

            @block.scalar
            def _(act):
                with act.Fori(0, B // 2) as pair:
                    for u in range(2):
                        b = pair * 2 + u
                        for t in range(QT):
                            act.wait_ge(out_ready, b * QT + t + 1)
                            if t >= 2:
                                act.wait_ge(out_taken, b * QT + t - 1)
                            else:
                                act.wait_ge(out_taken, b * QT)
                            nc.scalar.activation(gate[:, t % 2, :], ps_o[t][:, :D], ACT.Sigmoid).then_inc(gate_ready, 1)
    C.end_stage()


def router_stage(nc, C, w, experts, share, capacity=None, add=None):
    E, N = experts, TILES * experts
    BITS = 30
    with ExitStack() as ctx:
        sb, psum = stage_tensors(nc, ctx, C.n)
        wr = sb("w_router", [P, DK, E])
        first = sb("first_rank", [P, E])
        logitsT = sb("logits_T", [P, 2, S])
        logits = sb("logits", [P, TILES, E])
        probs = sb("probs", [P, TILES, E])
        left, ranked, chosen = sb("left", [P, TILES, E]), sb("ranked", [P, TILES, E]), sb("chosen", [P, TILES, E])
        best = sb("best", [P, TILES])
        if capacity:
            bits, bit, trial = sb("threshold_bits", [P, E], I32), sb("bit", [P, E], I32), sb("trial_bits", [P, E], I32)
            enough = sb("enough", [P, E], I32)
            counts, room = sb("counts", [P, E]), sb("room", [P, E])
            over = sb("over", [P, TILES, E])
            equal = sb("equal", [P, E, TILES])
            before, zeros = sb("before", [P, E, TILES]), sb("zeros", [P, TILES])
            lower = sb("lower", [P, P])
        ps_l, ps_t, ps_c, ps_e = psum("ps_logits", 2), psum("ps_turned", 2), psum("ps_counts", 1), psum("ps_equal", 2)
        weights, logitsT_ready, logitsT_copied = C.sem("weights"), C.sem("logitsT_ready"), C.sem("logitsT_copied")
        turned, taken, less_max, exp_ready = C.sem("turned"), C.sem("taken"), C.sem("less_max"), C.sem("exp_ready")
        counts_ready, counted, zeroed = C.sem("counts_ready"), C.sem("counted"), C.sem("zeroed")
        loads = [(wr, w["router"].rearrange("(c p) e -> p c e", p=P)), (first, w["first"].partition_broadcast(P))]
        if capacity:
            loads.append((lower, w["lower"]))

        def each(row):
            return row[:].unsqueeze(2).broadcast_to([P, TILES, E])

        def per_expert(col):
            return col.unsqueeze(1).broadcast_to([P, TILES, E])

        with nc.Block() as block:
            @block.sync
            def _(sp):
                for to, of in loads:
                    sp.dma_start(to[:], of).then_inc(weights, 16)

            @block.gpsimd
            def _(pool):
                nc.gpsimd.memset(logitsT[:], 0.0).then_inc(zeroed, 1)

            @block.scalar
            def _(act):
                act.wait_ge(zeroed, 1)
                with act.Fori(0, B // 2) as pair:
                    for u in range(2):
                        b = pair * 2 + u
                        act.wait_ge(logitsT_ready, b + 1)
                        nc.scalar.activation(logitsT[:E, u, :], ps_l[u][:E, :], ACT.Copy).then_inc(logitsT_copied, 1)
                act.wait_ge(less_max, 1)
                nc.scalar.activation(probs[:], probs[:], ACT.Exp).then_inc(exp_ready, 1)

            @block.tensor
            def _(pe):
                pe.wait_ge(weights, 16 * len(loads))
                with pe.Fori(0, B // 2) as pair:
                    for u in range(2):
                        b = pair * 2 + u
                        pe.wait_ge(logitsT_copied, pair * 2)
                        for c in range(DK):
                            ins = nc.tensor.matmul(ps_l[u][:E, :], wr[:, c, :], C.nT[:, c, batch_cols(b)],
                                                   start=(c == 0), stop=(c == DK - 1))
                        ins.then_inc(logitsT_ready, 1)
                        pe.wait_ge(logitsT_copied, b + 1)
                        pe.wait_ge(taken, pair * 2)
                        for t in range(QT):
                            ins = nc.tensor.transpose(ps_t[u][:, t * P:(t + 1) * P], logitsT[:, u, t * P:(t + 1) * P],
                                                      C.ident[:])
                        ins.then_inc(turned, 1)
                if capacity:
                    with pe.Fori(0, BITS) as i:
                        pe.wait_ge(counts_ready, i + 1)
                        nc.tensor.matmul(ps_c[0][:, :E], C.ones[:], counts[:], start=True, stop=True).then_inc(counted, 1)
                    pe.wait_ge(counts_ready, BITS + 1)
                    nc.tensor.matmul(ps_c[0][:, :E], C.ones[:], counts[:], start=True, stop=True)
                    nc.tensor.matmul(ps_e[0][:, :N], lower[:], equal[:], start=True, stop=True)
                    nc.tensor.matmul(ps_e[1][:, :N], C.ones[:], equal[:], start=True, stop=True).then_inc(counted, 1)

            @block.vector
            def _(dve):
                dve.wait_ge(weights, 16 * len(loads))
                with dve.Fori(0, B // 2) as pair:
                    for u in range(2):
                        b = pair * 2 + u
                        dve.wait_ge(turned, b + 1)
                        nc.vector.tensor_copy(logits[:, bass.ds(b * QT, QT), :],
                                              ps_t[u][:].rearrange("p (t e) -> p t e", t=QT)[:, :, :E]).then_inc(taken, 1)
                dve.drain()
                nc.vector.tensor_reduce(best[:], logits[:], AX_X, ALU.max)
                dve.drain()
                nc.vector.tensor_tensor(probs[:], logits[:], each(best), ALU.subtract)
                dve.drain().then_inc(less_max, 1)

                def first_best(of, marks):
                    nc.vector.tensor_reduce(best[:], of[:], AX_X, ALU.max)
                    dve.drain()
                    nc.vector.tensor_tensor(ranked[:], of[:], each(best), ALU.is_equal)
                    dve.drain()
                    nc.vector.tensor_tensor(ranked[:], ranked[:], per_expert(first[:]), ALU.mult)
                    dve.drain()
                    nc.vector.tensor_reduce(best[:], ranked[:], AX_X, ALU.max)
                    dve.drain()
                    nc.vector.tensor_tensor(marks[:], ranked[:], each(best), ALU.is_equal)
                    dve.drain()

                if not capacity:
                    first_best(logits, chosen)
                dve.wait_ge(exp_ready, 1)
                nc.vector.tensor_reduce(best[:], probs[:], AX_X, ALU.add)
                dve.drain()
                nc.vector.reciprocal(best[:], best[:])
                dve.drain()
                nc.vector.tensor_tensor(probs[:], probs[:], each(best), ALU.mult)
                dve.drain()
                if capacity:
                    first_best(probs, chosen)
                    nc.vector.scalar_tensor_tensor(out=left[:], in0=chosen[:], scalar=-2.0, in1=probs[:],
                                                   op0=ALU.mult, op1=ALU.add)
                    dve.drain()
                    first_best(left, left)
                    nc.vector.tensor_tensor(chosen[:], chosen[:], left[:], ALU.add)
                    dve.drain()
                nc.vector.tensor_tensor(share[:], probs[:], chosen[:], ALU.mult)
                dve.drain()
                if capacity:
                    nc.vector.memset(bits[:], 0)
                    nc.vector.memset(trial[:], 1 << (BITS - 1))
                    nc.vector.memset(bit[:], 1 << (BITS - 1))
                    dve.drain()
                    with dve.Fori(0, BITS) as i:
                        nc.vector.tensor_tensor(over[:], share[:], per_expert(trial[:].bitcast(F32)), ALU.is_ge)
                        dve.drain()
                        nc.vector.tensor_reduce(counts[:], over[:].rearrange("p t e -> p e t"), AX_X, ALU.add)
                        dve.drain().then_inc(counts_ready, 1)
                        dve.wait_ge(counted, i + 1)
                        nc.vector.tensor_scalar(enough[:], ps_c[0][:, :E], float(capacity), -1.0, ALU.is_ge, ALU.mult)
                        dve.drain()
                        nc.vector.tensor_tensor(enough[:], enough[:], bit[:], ALU.bitwise_and)
                        dve.drain()
                        nc.vector.tensor_tensor(bits[:], bits[:], enough[:], ALU.bitwise_or)
                        nc.vector.tensor_scalar(bit[:], bit[:], 1, None, ALU.logical_shift_right)
                        dve.drain()
                        nc.vector.tensor_tensor(trial[:], bits[:], bit[:], ALU.bitwise_or)
                        dve.drain()
                    threshold = per_expert(bits[:].bitcast(F32))
                    nc.vector.tensor_tensor(over[:], share[:], threshold, ALU.is_gt)
                    nc.vector.tensor_tensor(equal[:].rearrange("p e t -> p t e"), share[:], threshold, ALU.is_equal)
                    nc.vector.memset(zeros[:], 0.0)
                    dve.drain()
                    nc.vector.tensor_reduce(counts[:], over[:].rearrange("p t e -> p e t"), AX_X, ALU.add)
                    dve.drain().then_inc(counts_ready, 1)
                    dve.wait_ge(counted, BITS + 1)
                    nc.vector.tensor_scalar(room[:], ps_c[0][:, :E], -1.0, float(capacity), ALU.mult, ALU.add)
                    totals = ps_e[1][:, :N].rearrange("p (e t) -> p e t", e=E)
                    nc.vector.memset(before[:, :, 0:1], 0.0)
                    for e in range(E):
                        nc.vector.tensor_tensor_scan(before[:, e, 1:], totals[:, e, :TILES - 1], zeros[:, :TILES - 1],
                                                     0.0, ALU.add, ALU.add)
                    dve.drain()
                    nc.vector.tensor_tensor(before[:], before[:], ps_e[0][:, :N].rearrange("p (e t) -> p e t", e=E), ALU.add)
                    dve.drain()
                    nc.vector.tensor_tensor(before[:], before[:], room[:].unsqueeze(2).broadcast_to([P, E, TILES]), ALU.is_lt)
                    dve.drain()
                    nc.vector.tensor_tensor(before[:], before[:], equal[:], ALU.mult)
                    dve.drain()
                    nc.vector.tensor_tensor(over[:], over[:], before[:].rearrange("p e t -> p t e"), ALU.add)
                    dve.drain()
                    nc.vector.tensor_tensor(share[:], share[:], over[:], ALU.mult)
                if add is not None:
                    nc.vector.tensor_tensor(C.x[:], C.x[:], add[:], ALU.add)
    C.end_stage()


def experts_stage(nc, C, w1, w2, experts, share, func, b1=None, b2=None):
    E, FK = experts, FFN // P
    with ExitStack() as ctx:
        sb, psum = stage_tensors(nc, ctx, C.n)
        w1_e = [sb(f"w1_{u}", [P, DK, FFN]) for u in range(2)]
        w2_e = [sb(f"w2_{u}", [P, FK, D]) for u in range(2)]
        hid = [sb(f"hidden{v}", [P, FK, S]) for v in range(2)]
        if b1 is not None:
            b1_e, b2_e = [sb(f"b1_{u}", [P, FK]) for u in range(2)], [sb(f"b2_{u}", [P, D]) for u in range(2)]
            biased = sb("biased", [P, 2, D])
        ps_h, ps_y = psum("ps_hidden", FK), psum("ps_out", QT)
        loaded = [C.sem(f"expert_loaded{u}") for u in range(2)]
        hid_ready, hid_acted, out_ready, out_taken = C.sem("hid_ready"), C.sem("hid_acted"), C.sem("out_ready"), C.sem("out_taken")
        per_expert = 16 * (4 if b1 is not None else 2)

        with nc.Block() as block:
            @block.sync
            def _(sp):
                with sp.Fori(0, E // 2) as pair:
                    for u in range(2):
                        e = pair * 2 + u
                        sp.wait_ge(out_taken, pair * (2 * B * QT))
                        sp.dma_start(w1_e[u][:], w1[e].rearrange("(c p) f -> p c f", p=P)).then_inc(loaded[u], 16)
                        sp.dma_start(w2_e[u][:], w2[e].rearrange("(c p) n -> p c n", p=P)).then_inc(loaded[u], 16)
                        if b1 is not None:
                            sp.dma_start(b1_e[u][:], b1[e]).then_inc(loaded[u], 16)
                            sp.dma_start(b2_e[u][:], b2[e].partition_broadcast(P)).then_inc(loaded[u], 16)

            @block.tensor
            def _(pe):
                with pe.Fori(0, E // 2) as epair:
                    for u in range(2):
                        e = epair * 2 + u
                        with pe.Fori(0, B // 2) as bpair:
                            for v in range(2):
                                m = e * B + bpair * 2 + v
                                for f in range(FK):
                                    pe.wait_ge(loaded[u], (epair + 1) * per_expert)
                                    pe.wait_ge(hid_acted, m * FK)
                                    for c in range(DK):
                                        ins = nc.tensor.matmul(ps_h[f][:], w1_e[u][:, c, f * P:(f + 1) * P],
                                                               C.nT[:, c, batch_cols(bpair * 2 + v)],
                                                               start=(c == 0), stop=(c == DK - 1))
                                    ins.then_inc(hid_ready, 1)
                            for v in range(2):
                                m = e * B + bpair * 2 + v
                                for t in range(QT):
                                    pe.wait_ge(hid_acted, (m + 1) * FK)
                                    pe.wait_ge(out_taken, m * QT + (t if v else 0))
                                    for f in range(FK):
                                        ins = nc.tensor.matmul(ps_y[t][:, :D], hid[v][:, f, t * P:(t + 1) * P],
                                                               w2_e[u][:, f, :], start=(f == 0), stop=(f == FK - 1))
                                    ins.then_inc(out_ready, 1)

            @block.scalar
            def _(act):
                with act.Fori(0, E // 2) as epair:
                    for u in range(2):
                        e = epair * 2 + u
                        with act.Fori(0, B // 2) as bpair:
                            for v in range(2):
                                m = e * B + bpair * 2 + v
                                for f in range(FK):
                                    act.wait_ge(hid_ready, m * FK + f + 1)
                                    act.wait_ge(out_ready, (e * B + bpair * 2) * QT)
                                    nc.scalar.activation(hid[v][:, f, :], ps_h[f][:], func,
                                                         bias=b1_e[u][:, f:f + 1] if b1 is not None else 0.0) \
                                        .then_inc(hid_acted, 1)

            @block.vector
            def _(dve):
                with dve.Fori(0, E // 2) as epair:
                    for u in range(2):
                        e = epair * 2 + u
                        with dve.Fori(0, B) as b:
                            for t in range(QT):
                                tile = b * QT + t
                                dve.wait_ge(out_ready, (e * B + b) * QT + t + 1)
                                x_tile = C.x[:, tile, :]
                                part = ps_y[t][:, :D]
                                if b1 is not None:
                                    part = biased[:, t % 2, :]
                                    nc.vector.tensor_tensor(part, ps_y[t][:, :D], b2_e[u][:], ALU.add)
                                    dve.drain()
                                nc.vector.scalar_tensor_tensor(out=x_tile, in0=part, scalar=share[:, tile, bass.ds(e, 1)],
                                                               in1=x_tile, op0=ALU.mult, op1=ALU.add)
                                dve.drain().then_inc(out_taken, 1)
    C.end_stage()


def quantised_stage(nc, C, w):
    F = 1024
    FK = F // P
    with ExitStack() as ctx:
        sb, psum = stage_tensors(nc, ctx, C.n)
        w1, w2 = sb("w1", [P, FK, D]), sb("w2", [P, DK, F])
        w1q, w2q = sb("w1_int", [P, FK, D], BF16), sb("w2_int", [P, DK, F], BF16)
        w1T, w2T = sb("w1_int_T", [P, DK, F], BF16), sb("w2_int_T", [P, FK, D], BF16)
        s1, r1 = sb("w1_scale", [P, FK]), sb("w1_inverse", [P, FK])
        s2, r2 = sb("w2_scale", [P, DK]), sb("w2_inverse", [P, DK])
        b1, b2 = sb("b1", [P, FK]), sb("b2", [P, DK])
        tmp1, tmp2 = sb("tmp1", [P, FK]), sb("tmp2", [P, DK])
        top = sb("top", [P, 1])
        top_all = sb("top_all", [P, 2])
        s_in, r_in = sb("in_scale", [P, 2]), sb("in_inverse", [P, 2])
        f_scale, f_inv = sb("f_scale", [P, FK]), sb("f_inverse", [P, FK])
        d_scale, d_inv = sb("d_scale", [P, DK]), sb("d_inverse", [P, DK])
        q_scale, q_bias = sb("q_scale", [P, FK]), sb("q_bias", [P, FK])
        diag = sb("diagonals", [P, 2, DK, P])
        rows = sb("scale_and_bias_rows", [P, 2, D])
        most = sb("most", [P, FK, B])
        ident16 = sb("ident16", [P, P], BF16)
        relu_n = sb("relu_n", [P, 2, S])
        nq = sb("n_int", [P, DK, B * S], BF16)
        relu_h = sb("relu_h", [P, 2, S])
        hq = [sb(f"hidden_int{u}", [P, FK, S], BF16) for u in range(2)]
        out = sb("out", [P, D])
        ps_w = psum("ps_weights", 1, BF16)
        ps_r = psum("ps_rows", 1)
        ps_h, ps_o = psum("ps_hidden", 4), psum("ps_out", 2)
        loaded, w_ready, w_turned, w_copied = C.sem("loaded"), C.sem("w_ready"), C.sem("w_turned"), C.sem("w_copied")
        top_ready, top_reduced, n_scaled = C.sem("top_ready"), C.sem("top_reduced"), C.sem("in_scale_ready")
        relu_ready, n_ready = C.sem("relu_ready"), C.sem("n_ready")
        hid_ready, hid_maxed, diag_ready, rows_ready = C.sem("hid_ready"), C.sem("hid_maxed"), C.sem("diag_ready"), C.sem("rows_ready")
        scales_ready, hid2_ready, relu2_ready = C.sem("scales_ready"), C.sem("hid2_ready"), C.sem("relu2_ready")
        hq_ready, out_ready, out_taken = C.sem("hq_ready"), C.sem("out_ready"), C.sem("out_taken")

        def largest_to_scale(dve, i):
            nc.vector.tensor_scalar(s_in[:, i:i + 1], top_all[:, i:i + 1], 1e-8, 1.0 / 255.0, ALU.max, ALU.mult)
            dve.drain()
            nc.vector.reciprocal(r_in[:, i:i + 1], s_in[:, i:i + 1])
            dve.drain()

        def bias(dve, b, scale, inv, tmp):
            nc.vector.reciprocal(inv[:], scale[:])
            dve.drain()
            nc.vector.tensor_tensor(tmp[:], b[:], inv[:], ALU.mult)
            dve.drain()
            nc.vector.tensor_scalar(tmp[:], tmp[:], ROUND, -ROUND, ALU.add, ALU.add)
            dve.drain()
            nc.vector.tensor_tensor(b[:], tmp[:], scale[:], ALU.mult)
            dve.drain()

        with nc.Block() as block:
            @block.sync
            def _(sp):
                sp.dma_start(w1[:], w["w1"].rearrange("(c p) d -> p c d", p=P)).then_inc(loaded, 16)
                sp.dma_start(w2[:], w["w2"].rearrange("(c p) f -> p c f", p=P)).then_inc(loaded, 16)
                sp.dma_start(b1[:], w["b1"]).then_inc(loaded, 16)
                sp.dma_start(b2[:], w["b2"]).then_inc(loaded, 16)

            @block.gpsimd
            def _(pool):
                for i in range(2):
                    pool.wait_ge(top_ready, i + 1)
                    nc.gpsimd.partition_all_reduce(top_all[:, i:i + 1], top[:], P, bass.bass_isa.ReduceOp.max) \
                        .then_inc(top_reduced, 1)

            @block.vector
            def _(dve):
                dve.wait_ge(loaded, 64)
                nc.vector.tensor_copy(ident16[:], C.ident[:])
                for wt, s, r, n in ((w1, s1, r1, FK), (w2, s2, r2, DK)):
                    nc.vector.tensor_reduce(s[:], wt[:], AX_X, ALU.max, apply_absolute_value=True)
                    dve.drain()
                    nc.vector.tensor_scalar(s[:], s[:], 1e-8, 1.0 / 127.0, ALU.max, ALU.mult)
                    dve.drain()
                    nc.vector.reciprocal(r[:], s[:])
                    dve.drain()
                for wt, wq, r, n in ((w1, w1q, r1, FK), (w2, w2q, r2, DK)):
                    for i in range(n):
                        nc.vector.tensor_scalar(wt[:, i, :], wt[:, i, :], r[:, i:i + 1], ROUND, ALU.mult, ALU.add)
                    dve.drain()
                    nc.vector.tensor_scalar(wt[:], wt[:], -ROUND, 127.0, ALU.add, ALU.min)
                    dve.drain()
                    nc.vector.tensor_scalar(wq[:], wt[:], -128.0, None, ALU.max)
                dve.drain().then_inc(w_ready, 1)
                nc.vector.tensor_reduce(top[:], C.nT[:].rearrange("p c t -> p (c t)"), AX_X, ALU.max).then_inc(top_ready, 1)
                dve.wait_ge(top_reduced, 1)
                largest_to_scale(dve, 0)
                dve.sem_inc(n_scaled, 1)
                for c in range(DK):
                    with dve.Fori(0, B // 2) as pair:
                        for u in range(2):
                            b = pair * 2 + u
                            dve.wait_ge(relu_ready, b + (c * B + 1))
                            nc.vector.tensor_scalar(nq[:, c, batch_cols(b)], relu_n[:, u, :], ROUND, -ROUND,
                                                    ALU.add, ALU.add).then_inc(n_ready, 1)
                nc.vector.tensor_scalar(f_scale[:], s1[:], s_in[:, 0:1], None, ALU.mult)
                dve.drain()
                bias(dve, b1, f_scale, f_inv, tmp1)
                with dve.Fori(0, B) as b:
                    for f in range(FK):
                        dve.wait_ge(hid_ready, b * FK + f + 1)
                        nc.vector.tensor_reduce(most[:, f, bass.ds(b, 1)], ps_h[f % 4][:], AX_X, ALU.max).then_inc(hid_maxed, 1)
                dve.drain()
                nc.vector.tensor_reduce(tmp1[:], most[:], AX_X, ALU.max)
                dve.drain()
                nc.vector.tensor_tensor(tmp1[:], tmp1[:], f_scale[:], ALU.mult)
                dve.drain()
                nc.vector.tensor_tensor(tmp1[:], tmp1[:], b1[:], ALU.add)
                dve.drain()
                nc.vector.tensor_reduce(top[:], tmp1[:], AX_X, ALU.max)
                dve.drain()
                nc.vector.tensor_scalar(top[:], top[:], 0.0, None, ALU.max).then_inc(top_ready, 1)
                dve.wait_ge(top_reduced, 2)
                largest_to_scale(dve, 1)
                nc.vector.tensor_scalar(q_scale[:], f_scale[:], r_in[:, 1:2], None, ALU.mult)
                nc.vector.tensor_scalar(q_bias[:], b1[:], r_in[:, 1:2], None, ALU.mult)
                nc.vector.tensor_scalar(d_scale[:], s2[:], s_in[:, 1:2], None, ALU.mult)
                dve.drain().then_inc(scales_ready, 1)
                bias(dve, b2, d_scale, d_inv, tmp2)
                for c in range(DK):
                    nc.vector.tensor_scalar(diag[:, 0, c, :], C.ident[:], d_scale[:, c:c + 1], None, ALU.mult)
                    nc.vector.tensor_scalar(diag[:, 1, c, :], C.ident[:], b2[:, c:c + 1], None, ALU.mult)
                dve.drain().then_inc(diag_ready, 1)
                dve.wait_ge(rows_ready, 1)
                nc.vector.tensor_copy(rows[:].rearrange("p a d -> p (a d)"), ps_r[0][:])
                dve.drain()
                with dve.Fori(0, B // 2) as pair:
                    for u in range(2):
                        b = pair * 2 + u
                        for f in range(FK):
                            dve.wait_ge(relu2_ready, b * FK + f + 1)
                            dve.wait_ge(out_ready, pair * 2 * QT)
                            nc.vector.tensor_scalar(hq[u][:, f, :], relu_h[:, f % 2, :], ROUND, -ROUND,
                                                    ALU.add, ALU.add).then_inc(hq_ready, 1)
                        for t in range(QT):
                            dve.wait_ge(out_ready, b * QT + t + 1)
                            nc.vector.tensor_tensor(out[:], ps_o[t % 2][:, :D], rows[:, 0, :], ALU.mult).then_inc(out_taken, 1)
                            dve.drain()
                            nc.vector.tensor_tensor(out[:], out[:], rows[:, 1, :], ALU.add)
                            dve.drain()
                            x_tile = C.x[:, b * QT + t, :]
                            nc.vector.tensor_tensor(x_tile, x_tile, out[:], ALU.add)
                            dve.drain()

            @block.scalar
            def _(act):
                act.wait_ge(w_turned, 1)
                nc.scalar.activation(w1T[:, 0, :], ps_w[0][:], ACT.Copy).then_inc(w_copied, 1)
                act.wait_ge(w_turned, 2)
                nc.scalar.activation(w1T[:, 1, :], ps_w[0][:], ACT.Copy).then_inc(w_copied, 1)
                for i in range(2):
                    act.wait_ge(w_turned, 3 + i)
                    nc.scalar.activation(w2T[:, 4 * i:4 * i + 4, :].rearrange("p c d -> p (c d)"), ps_w[0][:],
                                         ACT.Copy).then_inc(w_copied, 1)
                act.wait_ge(n_scaled, 1)
                for c in range(DK):
                    with act.Fori(0, B // 2) as pair:
                        for u in range(2):
                            b = pair * 2 + u
                            act.wait_ge(n_ready, pair * 2 + c * B)
                            nc.scalar.activation(relu_n[:, u, :], C.nT[:, c, batch_cols(b)], ACT.Relu,
                                                 scale=r_in[:, 0:1]).then_inc(relu_ready, 1)
                act.wait_ge(scales_ready, 1)
                with act.Fori(0, B) as b:
                    for f in range(FK):
                        act.wait_ge(hid2_ready, b * FK + f + 1)
                        if f >= 2:
                            act.wait_ge(hq_ready, b * FK + f - 1)
                        else:
                            act.wait_ge(hq_ready, b * FK)
                        nc.scalar.activation(relu_h[:, f % 2, :], ps_h[f % 4][:], ACT.Relu, scale=q_scale[:, f:f + 1],
                                             bias=q_bias[:, f:f + 1]).then_inc(relu2_ready, 1)

            @block.tensor
            def _(pe):
                pe.wait_ge(w_ready, 1)
                for c in range(DK):
                    if c:
                        pe.wait_ge(w_copied, c)
                    for f in range(FK):
                        ins = nc.tensor.transpose(ps_w[0][:, f * P:(f + 1) * P], w1q[:, f, c * P:(c + 1) * P], ident16[:])
                    ins.then_inc(w_turned, 1)
                for i in range(2):
                    pe.wait_ge(w_copied, 2 + i)
                    for f in range(4):
                        for c in range(DK):
                            ins = nc.tensor.transpose(ps_w[0][:, f * D + c * P:f * D + (c + 1) * P],
                                                      w2q[:, c, (4 * i + f) * P:(4 * i + f + 1) * P], ident16[:])
                    ins.then_inc(w_turned, 1)
                pe.wait_ge(w_copied, 4)
                pe.wait_ge(n_ready, DK * B)

                def hidden(b, f, ready):
                    for c in range(DK):
                        ins = nc.tensor.matmul(ps_h[f % 4][:], w1T[:, c, f * P:(f + 1) * P], nq[:, c, batch_cols(b)],
                                               start=(c == 0), stop=(c == DK - 1))
                    ins.then_inc(ready, 1)

                with pe.Fori(0, B) as b:
                    for f in range(FK):
                        if f >= 4:
                            pe.wait_ge(hid_maxed, b * FK + f - 3)
                        else:
                            pe.wait_ge(hid_maxed, b * FK)
                        hidden(b, f, hid_ready)
                pe.wait_ge(diag_ready, 1)
                for a in range(2):
                    for c in range(DK):
                        ins = nc.tensor.matmul(ps_r[0][:, a * D + c * P:a * D + (c + 1) * P], C.ones[:], diag[:, a, c, :],
                                               start=True, stop=True)
                ins.then_inc(rows_ready, 1)
                with pe.Fori(0, B // 2) as pair:
                    for u in range(2):
                        b = pair * 2 + u
                        for f in range(FK):
                            if f >= 4:
                                pe.wait_ge(relu2_ready, b * FK + f - 3)
                            else:
                                pe.wait_ge(relu2_ready, b * FK)
                                pe.wait_ge(hid_maxed, B * FK)
                            hidden(b, f, hid2_ready)
                        for t in range(QT):
                            pe.wait_ge(hq_ready, (b + 1) * FK)
                            pe.wait_ge(out_taken, b * QT + max(t - 1, 0))
                            for f in range(FK):
                                ins = nc.tensor.matmul(ps_o[t % 2][:, :D], hq[u][:, f, t * P:(t + 1) * P], w2T[:, f, :],
                                                       start=(f == 0), stop=(f == FK - 1))
                            ins.then_inc(out_ready, 1)
    C.end_stage()




def deformable_stage(nc, C, w):
    HD, ROWS = D // H, S + 1
    N = H * NK
    HALF = H // 2
    NH = HALF * NK
    PAIR = 4 * HD
    with ExitStack() as ctx:
        sb, psum = stage_tensors(nc, ctx, C.n)
        table = [nc.dram_tensor(f"kv_table{u}", [H * ROWS, PAIR], F32, kind="Internal").ap() for u in range(2)]
        wkv, wq, wo = sb("w_kv", [P, DK, 2 * D]), sb("w_q", [P, DK, D]), sb("w_o", [P, DK, D])
        woff = sb("w_off", [P, DK, N])
        bkv, bq, bo = sb("b_kv", [P, 2 * D]), sb("b_q", [P, D]), sb("b_o", [P, D])
        bq_col, boff = sb("b_q_col", [P, DK]), sb("b_off", [P, N])
        shift, row = sb("shift", [P, N]), sb("row", [P, N])
        mask_in, unmasked = sb("mask_in", [P, B, QT], I32), sb("unmasked", [P, B, QT])
        places = sb("places", [P, QT])
        length, inv_length, neg_length = sb("length", [P, B]), sb("inv_length", [P, B]), sb("neg_length", [P, B])
        n_chunk, kv_chunk = sb("n_chunk", [P, DK, S]), sb("kv_chunk", [P, DK, S])
        qT = sb("q_T", [P, DK, S])
        kv = [sb(f"kv{u}", [P, QT, 2 * D]) for u in range(2)]
        q = [sb(f"q{u}", [P, QT, D]) for u in range(2)]
        pos, whole, over = sb("pos", [P, QT, N]), sb("whole", [P, QT, N]), sb("over", [P, QT, N])
        w_hi = [sb(f"w_hi{u}", [P, QT, N]) for u in range(2)]
        w_lo = [sb(f"w_lo{u}", [P, QT, N]) for u in range(2)]
        index = sb("index", [P, QT, N], U32)
        index_tile = [sb(f"index_tile{i}", [P, N], U32) for i in range(2)]
        got = [sb(f"gathered{i}", [P, NH, PAIR]) for i in range(2)]
        lo, hi = sb("lo", [P, NH, 2 * HD]), sb("hi", [P, NH, 2 * HD])
        prod = sb("prod", [P, NH, HD])
        score, top = sb("score", [P, HALF, NK]), sb("top", [P, HALF])
        zeros = sb("zeros", [H, PAIR])
        heads, headsT = sb("heads_out", [P, QT, D]), sb("heads_out_T", [P, DK, S])
        added = sb("added", [P, D])
        ps_kv, ps_q, ps_qT = psum("ps_kv", 2), psum("ps_q", 2), psum("ps_qT", 2)
        ps_off, ps_o = psum("ps_off", 1), psum("ps_out", 1)
        loaded, zeroed, staged = C.sem("loaded"), C.sem("zeroed"), C.sem("staged")
        gathers_begun = C.sem("gathers_begun")
        parts_ready, length_ready = C.sem("parts_ready"), C.sem("length_ready")
        places_ready, borders = C.sem("places_ready"), C.sem("borders")
        kv_ready, kv_taken, q_ready, q_taken = C.sem("kv_ready"), C.sem("kv_taken"), C.sem("q_ready"), C.sem("q_taken")
        qT_ready, qT_taken, off_ready, off_taken = C.sem("qT_ready"), C.sem("qT_taken"), C.sem("off_ready"), C.sem("off_taken")
        table_written = [C.sem(f"table_written{u}") for u in range(2)]
        index_ready, index_used = C.sem("index_ready"), C.sem("index_used")
        gathered = [C.sem(f"gathered{i}") for i in range(2)]
        got_used = [C.sem(f"got_used{i}") for i in range(2)]
        shifted, exp_ready, sampled = C.sem("shifted"), C.sem("exp_ready"), C.sem("sampled")
        headsT_turned, headsT_copied = C.sem("headsT_turned"), C.sem("headsT_copied")
        out_ready, out_taken = C.sem("out_ready"), C.sem("out_taken")
        loads = [(wkv, w["wkv"].rearrange("(c p) n -> p c n", p=P)), (wq, w["wq"].rearrange("(c p) n -> p c n", p=P)),
                 (wo, w["wo"].rearrange("(c p) n -> p c n", p=P)), (woff, w["woff"].rearrange("(c p) n -> p c n", p=P)),
                 (bq_col, w["bq_col"]), (mask_in, w["mask"])]
        loads += [(to, w[n].partition_broadcast(P)) for to, n in (
            (bkv, "bkv"), (bq, "bq"), (bo, "bo"), (boff, "boff"), (shift, "shift"), (row, "row"))]

        def table_of(u, ahead):
            rows = table[u].rearrange("(h r) c -> r h c", h=H)
            return rows[1:, :, :2 * HD] if ahead == 0 else rows[:S, :, 2 * HD:]

        with nc.Block() as block:
            @block.sync
            def _(sp):
                for to, of in loads:
                    sp.dma_start(to[:], of).then_inc(loaded, 16)
                sp.wait_ge(zeroed, 1)
                for u in range(2):
                    rows = table[u].rearrange("(h r) c -> h r c", h=H)
                    sp.dma_start(rows[:, 0, :2 * HD], zeros[:, :2 * HD]).then_inc(borders, 16)
                    sp.dma_start(rows[:, S, 2 * HD:], zeros[:, 2 * HD:]).then_inc(borders, 16)
                with sp.Fori(0, B // 2) as pair:
                    for u in range(2):
                        b = pair * 2 + u
                        sp.wait_ge(kv_taken, (b + 1) * QT)
                        for t in range(QT):
                            for ahead in range(2):
                                sp.dma_start(table_of(u, ahead)[t * P:(t + 1) * P],
                                             kv[u][:, t, :].rearrange("p (h c) -> p h c", h=H)).then_inc(table_written[u], 16)
                sp.wait_ge(table_written[0], B // 2 * 32 * QT)
                sp.wait_ge(table_written[1], B // 2 * 32 * QT)

            @block.gpsimd
            def _(pool):
                nc.gpsimd.memset(zeros[:], 0.0).then_inc(zeroed, 1)
                nc.gpsimd.iota(places[:], [[P, QT]], base=0, channel_multiplier=1,
                               allow_small_or_imprecise_dtypes=True).then_inc(places_ready, 1)
                with pool.Fori(0, B // 2) as pair:
                    for u in range(2):
                        with pool.Fori(0, QT // 2) as tpair:
                            for v in range(2):
                                tile = (pair * 2 + u) * QT + tpair * 2 + v
                                pool.wait_ge(table_written[u], (pair + 1) * (32 * QT))
                                pool.wait_ge(index_ready, tile + 1)
                                for half in range(2):
                                    pool.wait_ge(got_used[half], tile)
                                    pool.wait_ge(borders, 64)
                                    pool.sem_inc(gathers_begun, 1)
                                    for c in range(NH):
                                        n = half * NH + c
                                        nc.gpsimd.indirect_dma_start(
                                            got[half][:, c, :], None, table[u],
                                            bass.IndirectOffsetOnAxis(ap=index_tile[v][:, n:n + 1], axis=0)) \
                                            .then_inc(gathered[half], 16)

            @block.scalar
            def _(act):
                act.wait_ge(loaded, 16 * len(loads))
                with act.Fori(0, B) as b:
                    act.wait_ge(q_ready, b * QT)
                    act.wait_ge(kv_ready, b * QT)
                    nc.scalar.activation(kv_chunk[:], C.ctxT[:, :, batch_cols(b)], ACT.Copy)
                    nc.scalar.activation(n_chunk[:], C.nT[:, :, batch_cols(b)], ACT.Copy)
                    act.drain().then_inc(staged, 1)
                    for c in range(DK):
                        act.wait_ge(qT_ready, b * DK + c + 1)
                        nc.scalar.activation(qT[:, c, :], ps_qT[c][:], ACT.Identity, bias=bq_col[:, c:c + 1]) \
                            .then_inc(qT_taken, 1)
                    for half in range(2 * QT):
                        act.wait_ge(shifted, b * (2 * QT) + half + 1)
                        nc.scalar.activation(score[:], score[:], ACT.Exp).then_inc(exp_ready, 1)

            @block.tensor
            def _(pe):
                pe.wait_ge(loaded, 16 * len(loads))
                pe.wait_ge(parts_ready, 1)
                nc.tensor.matmul(ps_off[0][:, :B], C.ones[:], length[:], start=True, stop=True).then_inc(length_ready, 1)
                pe.wait_ge(parts_ready, 2)
                with pe.Fori(0, B) as b:
                    for c in range(DK):
                        pe.wait_ge(staged, b + 1)
                        pe.wait_ge(qT_taken, b * DK)
                        for i in range(DK):
                            ins = nc.tensor.matmul(ps_qT[c][:], wq[:, i, c * P:(c + 1) * P], n_chunk[:, i, :],
                                                   start=(i == 0), stop=(i == DK - 1))
                        ins.then_inc(qT_ready, 1)
                    for t in range(QT):
                        if t >= 2:
                            pe.wait_ge(kv_taken, b * QT + t - 1)
                            pe.wait_ge(q_taken, b * QT + t - 1)
                        else:
                            pe.wait_ge(kv_taken, b * QT)
                            pe.wait_ge(q_taken, b * QT)
                        for i in range(DK):
                            ins = nc.tensor.matmul(ps_kv[t % 2][:], kv_chunk[:, i, t * P:(t + 1) * P], wkv[:, i, :],
                                                   start=(i == 0), stop=(i == DK - 1))
                        ins.then_inc(kv_ready, 1)
                        for i in range(DK):
                            ins = nc.tensor.matmul(ps_q[t % 2][:, :D], n_chunk[:, i, t * P:(t + 1) * P], wq[:, i, :],
                                                   start=(i == 0), stop=(i == DK - 1))
                        ins.then_inc(q_ready, 1)
                    pe.wait_ge(qT_taken, (b + 1) * DK)
                    for t in range(QT):
                        for i in range(DK):
                            ins = nc.tensor.matmul(ps_off[0][:, t * N:(t + 1) * N], qT[:, i, t * P:(t + 1) * P],
                                                   woff[:, i, :], start=(i == 0), stop=(i == DK - 1))
                    ins.then_inc(off_ready, 1)
                    for c in range(DK):
                        pe.wait_ge(sampled, b + 1)
                        for t in range(QT):
                            ins = nc.tensor.transpose(ps_qT[c][:, t * P:(t + 1) * P], heads[:, t, c * P:(c + 1) * P],
                                                      C.ident[:])
                        ins.then_inc(headsT_turned, 1)
                    for t in range(QT):
                        pe.wait_ge(headsT_copied, (b + 1) * DK)
                        pe.wait_ge(out_taken, b * QT + t)
                        for c in range(DK):
                            ins = nc.tensor.matmul(ps_o[0][:, :D], headsT[:, c, t * P:(t + 1) * P], wo[:, c, :],
                                                   start=(c == 0), stop=(c == DK - 1))
                        ins.then_inc(out_ready, 1)

            @block.vector
            def _(dve):
                dve.wait_ge(loaded, 16 * len(loads))
                dve.wait_ge(places_ready, 1)
                nc.vector.tensor_scalar(unmasked[:], mask_in[:], -1.0, 1.0, ALU.mult, ALU.add)
                dve.drain()
                nc.vector.tensor_reduce(length[:], unmasked[:], AX_X, ALU.add)
                dve.drain().then_inc(parts_ready, 1)
                dve.wait_ge(length_ready, 1)
                nc.vector.tensor_scalar(length[:], ps_off[0][:, :B], -1.0, None, ALU.add)
                dve.drain()
                nc.vector.reciprocal(inv_length[:], length[:])
                nc.vector.tensor_scalar(neg_length[:], length[:], -1.0, None, ALU.mult)
                dve.drain().then_inc(parts_ready, 1)
                with dve.Fori(0, B // 2) as pair:
                    for u in range(2):
                        b = pair * 2 + u
                        now = bass.ds(b, 1)
                        dve.wait_ge(table_written[u], pair * (32 * QT))
                        for t in range(QT):
                            dve.wait_ge(kv_ready, b * QT + t + 1)
                            nc.vector.tensor_tensor(kv[u][:, t, :], ps_kv[t % 2][:], bkv[:], ALU.add).then_inc(kv_taken, 1)
                            dve.wait_ge(q_ready, b * QT + t + 1)
                            nc.vector.tensor_tensor(q[u][:, t, :], ps_q[t % 2][:, :D], bq[:], ALU.add).then_inc(q_taken, 1)
                        dve.drain()
                        nc.vector.tensor_scalar(q[u][:], q[u][:], float(HD) ** -0.5, None, ALU.mult)
                        dve.wait_ge(off_ready, b + 1)
                        by_tile = lambda r: r[:].unsqueeze(1).broadcast_to([P, QT, N])
                        nc.vector.tensor_tensor(pos[:], ps_off[0][:, :QT * N].rearrange("p (t n) -> p t n", t=QT),
                                                by_tile(boff), ALU.add).then_inc(off_taken, 1)
                        dve.drain()
                        nc.vector.tensor_tensor(pos[:], pos[:], by_tile(shift), ALU.add)
                        dve.drain()
                        nc.vector.tensor_tensor(pos[:], pos[:], places[:].unsqueeze(2).broadcast_to([P, QT, N]), ALU.add)
                        dve.drain()
                        nc.vector.tensor_scalar(whole[:], pos[:], inv_length[:, now], ROUND, ALU.mult, ALU.add)
                        dve.drain()
                        nc.vector.tensor_scalar(whole[:], whole[:], -ROUND, neg_length[:, now], ALU.add, ALU.mult)
                        dve.drain()
                        nc.vector.tensor_tensor(pos[:], pos[:], whole[:], ALU.add)
                        dve.drain()
                        nc.vector.tensor_scalar(over[:], pos[:], 0.0, length[:, now], ALU.is_lt, ALU.mult)
                        dve.drain()
                        nc.vector.tensor_tensor(pos[:], pos[:], over[:], ALU.add)
                        dve.drain()
                        nc.vector.tensor_scalar(pos[:], pos[:], S / (S - 1.0), -0.5, ALU.mult, ALU.add)
                        dve.drain()
                        nc.vector.tensor_scalar(whole[:], pos[:], ROUND, -ROUND, ALU.add, ALU.add)
                        dve.drain()
                        nc.vector.tensor_tensor(over[:], whole[:], pos[:], ALU.is_gt)
                        dve.drain()
                        nc.vector.tensor_tensor(whole[:], whole[:], over[:], ALU.subtract)
                        dve.drain()
                        nc.vector.tensor_tensor(pos[:], pos[:], whole[:], ALU.subtract)
                        nc.vector.tensor_scalar(whole[:], whole[:], -1.0, S - 1.0, ALU.max, ALU.min)
                        dve.drain()
                        nc.vector.tensor_scalar(w_hi[u][:], pos[:], 0.5, None, ALU.mult)
                        nc.vector.tensor_scalar(w_lo[u][:], pos[:], -0.5, 0.5, ALU.mult, ALU.add)
                        nc.vector.tensor_tensor(index[:], whole[:], by_tile(row), ALU.add)
                        dve.drain()
                        for t in range(2):
                            nc.vector.tensor_copy(index_tile[t][:], index[:, t, :]).then_inc(index_ready, 1)
                        for t in range(QT):
                            tile = b * QT + t
                            for half in range(2):
                                own = slice(half * NH, (half + 1) * NH)
                                dve.wait_ge(gathered[half], (tile + 1) * (16 * NH))
                                pairs = got[half][:]
                                by = lambda m: m[u][:, t, own].unsqueeze(2).broadcast_to([P, NH, 2 * HD])
                                nc.vector.tensor_tensor(lo[:], pairs[:, :, :2 * HD], by(w_lo), ALU.mult)
                                nc.vector.tensor_tensor(hi[:], pairs[:, :, 2 * HD:], by(w_hi), ALU.mult)
                                dve.drain().then_inc(got_used[half], 1)
                                nc.vector.tensor_tensor(lo[:], lo[:], hi[:], ALU.add)
                                dve.drain()
                                by_head = lo[:].rearrange("p (h k) c -> p h k c", h=HALF)
                                prods = prod[:].rearrange("p (h k) c -> p h k c", h=HALF)
                                query = q[u][:, t, half * (D // 2):(half + 1) * (D // 2)] \
                                    .rearrange("p (h c) -> p h c", h=HALF).unsqueeze(2).broadcast_to([P, HALF, NK, HD])
                                nc.vector.tensor_tensor(prods, by_head[:, :, :, :HD], query, ALU.mult)
                                dve.drain()
                                nc.vector.tensor_reduce(score[:], prods, AX_X, ALU.add)
                                dve.drain()
                                per_head = top[:].unsqueeze(2).broadcast_to([P, HALF, NK])
                                nc.vector.tensor_reduce(top[:], score[:], AX_X, ALU.max)
                                dve.drain()
                                nc.vector.tensor_tensor(score[:], score[:], per_head, ALU.subtract)
                                dve.drain().then_inc(shifted, 1)
                                dve.wait_ge(exp_ready, tile * 2 + half + 1)
                                nc.vector.tensor_reduce(top[:], score[:], AX_X, ALU.add)
                                dve.drain()
                                nc.vector.reciprocal(top[:], top[:])
                                dve.drain()
                                nc.vector.tensor_tensor(score[:], score[:], per_head, ALU.mult)
                                dve.drain()
                                nc.vector.tensor_tensor(prods, by_head[:, :, :, HD:],
                                                        score[:].unsqueeze(3).broadcast_to([P, HALF, NK, HD]), ALU.mult)
                                dve.drain()
                                nc.vector.tensor_reduce(
                                    heads[:, t, half * (D // 2):(half + 1) * (D // 2)].rearrange("p (h c) -> p h c", h=HALF),
                                    prod[:].rearrange("p (h k) c -> p h c k", h=HALF), AX_X, ALU.add)
                                dve.drain()
                            if t + 2 < QT:
                                nc.vector.tensor_copy(index_tile[t % 2][:], index[:, t + 2, :]).then_inc(index_ready, 1)
                        dve.sem_inc(sampled, 1)
                        for c in range(DK):
                            dve.wait_ge(headsT_turned, b * DK + c + 1)
                            nc.vector.tensor_copy(headsT[:, c, :], ps_qT[c][:]).then_inc(headsT_copied, 1)
                        for t in range(QT):
                            dve.wait_ge(out_ready, b * QT + t + 1)
                            nc.vector.tensor_tensor(added[:], ps_o[0][:, :D], bo[:], ALU.add).then_inc(out_taken, 1)
                            dve.drain()
                            x_tile = C.x[:, b * QT + t, :]
                            nc.vector.tensor_tensor(x_tile, x_tile, added[:], ALU.add)
                            dve.drain()
    C.end_stage()




def build(nc, d, stages=None):
    with ExitStack() as ctx:
        C = Core(nc, ctx, d)
        share = ctx.enter_context(nc.sbuf_tensor("share", [P, TILES, E0], F32))
        share0, share3 = share, share[:, :, :E3]
        y = C.ctxT[:].rearrange("p c (t d) -> p (c t) d", d=D)

        def cross(l, hd, **more):
            norm_stage(nc, C)
            w = {n: d[f"{l}_w{n}"] for n in "qkvo"}
            if more.get("biased"):
                w.update({n: d[f"{l}_{n}"] for n in ("bq", "bk", "bv", "bo")})
            if more.get("masked"):
                w.update(mask=d["mask"], mask_slot=d["mask_slot"])
            attention_stage(nc, C, w, hd, **more)

        def ffn0():
            norm_stage(nc, C)
            router_stage(nc, C, dict(router=d["L0_router"], first=d["first0"]), E0, share0)
            experts_stage(nc, C, d["L0_w1"], d["L0_w2"], E0, share0, ACT.Gelu, d["L0_b1"], d["L0_b2"])

        def ffn1():
            norm_stage(nc, C)
            quantised_stage(nc, C, dict(w1=d["L1_w1"], w2=d["L1_w2"], b1=d["L1_b1"], b2=d["L1_b2"]))

        def ffn2():
            norm_stage(nc, C)
            channel_mix_stage(nc, C, dict(r=d["L2_wr"], k=d["L2_wk2"], v=d["L2_wv2"], mu=d["L2_mu"]))

        def ffn3():
            norm_stage(nc, C, keep=y, gain=d["L3_g1"])
            attention_stage(nc, C, {n: d[f"L3f_{n}"] for n in ("q", "k", "q_swap", "k_swap", "v", "o", "cos", "sin", "future")},
                            16, cross=False, causal=True, rope=True, res=y)
            norm_stage(nc, C, gain=d["L3_g2"], layer=False, src=y)
            router_stage(nc, C, dict(router=d["L3_router"], first=d["first3"], lower=d["lower"]), E3, share3,
                         capacity=CAP, add=y)
            experts_stage(nc, C, d["L3_w1"], d["L3_w2"], E3, share3, ACT.Relu)

        load_stage(nc, C)
        steps = {
            "L0x": lambda: (norm_stage(nc, C), deformable_stage(nc, C, {n: d[f"L0_{n}"] for n in (
                "wkv", "bkv", "wq", "bq", "bq_col", "woff", "boff", "shift", "wo", "bo", "mask", "row")})),
            "L0f": ffn0,
            "L1x": lambda: cross("L1", 16, biased=True),
            "L1f": ffn1,
            "L2x": lambda: cross("L2", 64),
            "L2f": ffn2,
            "L3x": lambda: cross("L3", 16, biased=True, masked=True),
            "L3f": ffn3,
        }
        for name in stages or steps:
            steps[name]()
        store_stage(nc, C)


def slots(w):
    import numpy as np
    out = np.zeros((w.shape[0], H, SLOT), w.dtype)
    out[:, :, :16] = w.reshape(w.shape[0], H, 16)
    return out.reshape(w.shape[0], H * SLOT)


def slot_bias(b):
    return slots(b[None])[0].reshape(4, P).T


def lay_out(a):
    import numpy as np
    o = {"x": a["x"], "ctx_T": a["ctx_1024"].reshape(B * S, D).T}
    for l in ("L1", "L3"):
        o[f"{l}_wq"] = slots(a[f"{l}_xattn_Wq"].T)
        o[f"{l}_wk"] = slots(a[f"{l}_xattn_Wk"].T)
        o[f"{l}_wv"] = a[f"{l}_xattn_Wv"].T
        o[f"{l}_wo"] = a[f"{l}_xattn_Wo"].T
        o[f"{l}_bq"] = slot_bias(a[f"{l}_xattn_bq"])
        bk = slots(a[f"{l}_xattn_bk"][None])[0].reshape(4, P).T
        o[f"{l}_bk"] = bk
        o[f"{l}_bv"], o[f"{l}_bo"] = a[f"{l}_xattn_bv"], a[f"{l}_xattn_bo"]
    for n in "qkvo":
        o[f"L2_w{n}"] = a[f"L2_xattn_W_{n.upper()}"]
    o["mask"] = a["mask_Bx1x1xS2_bf1"].reshape(1, B * S).view(np.uint8)
    o["mask_slot"] = np.tile(np.eye(1, SLOT, 16, dtype=np.float32), (1, 4))
    o["L0_wkv"] = np.concatenate([a[f"L0_xattn_W{n}"].T.reshape(D, H, 16) for n in "kv"], axis=2).reshape(D, 2 * D)
    o["L0_bkv"] = np.concatenate([a[f"L0_xattn_b{n}"].reshape(H, 16) for n in "kv"], axis=1).reshape(2 * D)
    o["L0_wq"], o["L0_bq"] = a["L0_xattn_Wq"].T, a["L0_xattn_bq"]
    o["L0_bq_col"] = a["L0_xattn_bq"].reshape(DK, P).T
    o["L0_woff"], o["L0_boff"] = a["L0_xattn_Woff"].T, a["L0_xattn_boff"]
    o["L0_wo"], o["L0_bo"] = a["L0_xattn_Wo"].T, a["L0_xattn_bo"]
    o["L0_mask"] = a["mask_BxS2_if0"].reshape(B, QT, P).transpose(2, 0, 1)
    o["L0_shift"] = np.tile(np.arange(-NK // 2, NK + -NK // 2, dtype=np.float32), H)
    o["L0_row"] = (np.repeat(np.arange(H), NK) * (S + 1) + 1).astype(np.float32)
    o["L0_router"], o["L3_router"] = a["L0_ffn_router_w"], a["L3_ffn_w_router"]
    o["L0_w1"], o["L0_w2"], o["L0_b2"] = a["L0_ffn_w1"], a["L0_ffn_w2"], a["L0_ffn_b2"]
    o["L0_b1"] = a["L0_ffn_b1"].reshape(E0, FFN // P, P).transpose(0, 2, 1)
    o["L1_w1"], o["L1_w2"] = a["L1_ffn_w1"], a["L1_ffn_w2"]
    o["L1_b1"], o["L1_b2"] = a["L1_ffn_b1"].reshape(-1, P).T, a["L1_ffn_b2"].reshape(-1, P).T
    o["L2_wr"], o["L2_wk2"], o["L2_wv2"] = (a[f"L2_ffn_W_{n}"].T for n in "rkv")
    o["L2_mu"] = np.stack([a[f"L2_ffn_mu_{n}"].reshape(DK, P).T for n in "rk"], axis=1)
    o["L3_g1"], o["L3_g2"] = a["L3_ffn_g1"], a["L3_ffn_g2"]
    q, k, v = np.split(a["L3_ffn_w_qkv"], 3, axis=1)
    swap = np.arange(D) ^ 1
    o["L3f_q"], o["L3f_k"], o["L3f_q_swap"], o["L3f_k_swap"] = slots(q), slots(k), slots(q[:, swap]), slots(k[:, swap])
    o["L3f_v"], o["L3f_o"] = v, a["L3_ffn_w_o"]
    o["L3_w1"], o["L3_w2"] = a["L3_ffn_w1"], a["L3_ffn_w2"]
    theta = np.float32(10000.0) ** (np.float32(-2.0) * (np.arange(8, dtype=np.float32) / np.float32(16)))
    angle = (np.arange(S, dtype=np.float32)[:, None] * theta[None, :]).astype(np.float32)
    feature = np.arange(P) % SLOT
    inside = (feature < 16)[:, None]
    pair = np.minimum(feature, 15) // 2
    sign = np.where(feature % 2 == 0, -1.0, 1.0)[:, None]
    o["L3f_cos"] = (np.cos(angle).T[pair] * inside).astype(np.float32)
    o["L3f_sin"] = (np.sin(angle).T[pair] * sign * inside).astype(np.float32)
    o["L3f_future"] = (np.triu(np.ones((P, P)), 1) * NEG).astype(np.float32)
    o["lower"] = np.triu(np.ones((P, P), np.float32), 1)
    o["first0"], o["first3"] = np.arange(E0, 0, -1, dtype=np.float32), np.arange(E3, 0, -1, dtype=np.float32)
    return {k: np.ascontiguousarray(v) for k, v in o.items()}


def kernel(**inputs):
    import numpy as np
    import concourse.bacc as bacc
    from concourse.bass_utils import run_bass_kernel_spmd

    nc = bacc.Bacc("TRN2", target_bir_lowering=False, num_devices=1)
    arrays = {f"in_{k}": v for k, v in lay_out({k: np.asarray(v) for k, v in inputs.items()}).items()}
    d = {k[3:]: nc.dram_tensor(k, v.shape, mybir.dt.from_np(v.dtype), kind="ExternalInput").ap() for k, v in arrays.items()}
    d["out"] = nc.dram_tensor("out", (B, S, D), F32, kind="ExternalOutput").ap()
    build(nc, d)
    return run_bass_kernel_spmd(nc, [arrays], core_ids=[0]).results[0]["out"]
```

```python
from contextlib import ExitStack

import concourse.bass as bass
from concourse import mybir

F32 = mybir.dt.float32
BF16 = mybir.dt.bfloat16
I32 = mybir.dt.int32
U32 = mybir.dt.uint32
ACT = mybir.ActivationFunctionType
ALU = mybir.AluOpType
AX_X = mybir.AxisListType.X

P = 128
B, S, D = 8, 512, 256
QT = S // P
TILES = B * QT
DK = D // P
H = 16
SLOT = 32
LN_EPS = 1e-5
RMS_EPS = 1e-6
NEG = -1e30
ROUND = 1.5 * 2.0 ** 23
NK = 5
E0, E3, FFN = 14, 8, 512
CAP = 320


class Core:

    def __init__(self, nc, ctx, dram):
        self.nc, self.ctx, self.dram = nc, ctx, dram
        self.n = 0

        def sb(name, shape, dt=F32):
            return ctx.enter_context(nc.sbuf_tensor(name, shape, dt))

        self.x = sb("x_res", [P, TILES, D])
        self.nT = sb("normed_T", [P, DK, B * S])
        self.ctxT = sb("ctx_T", [P, DK, B * S])
        self.ident = sb("ident", [P, P])
        self.ones = sb("ones", [P, P])
        self.eps = sb("eps", [P, 2])

        self.stage_sems = []

    def sem(self, name):
        self.n += 1
        self.stage_sems.append(self.nc.alloc_semaphore(name=f"{name}_{self.n}"))
        return self.stage_sems[-1]

    def end_stage(self):
        self.nc.clear_and_free_semaphores(self.stage_sems)
        self.nc.all_engine_barrier()
        self.stage_sems = []


def batch_cols(b):
    return bass.ds(b * S, S)


def load_stage(nc, C):
    loaded, made, memset_done = C.sem("loaded"), C.sem("made"), C.sem("memset")
    with nc.Block() as block:
        @block.sync
        def _(sp):
            sp.dma_start(C.x[:], C.dram["x"].rearrange("b (t p) d -> p (b t) d", p=P)).then_inc(loaded, 16)
            sp.dma_start(C.ctxT[:], C.dram["ctx_T"].rearrange("(k p) t -> p k t", p=P)).then_inc(loaded, 16)
            sp.wait_ge(loaded, 32)

        @block.gpsimd
        def _(pool):
            nc.gpsimd.memset(C.ones[:], 1.0).then_inc(memset_done, 1)
            nc.gpsimd.memset(C.eps[:, 0:1], LN_EPS).then_inc(made, 1)
            nc.gpsimd.memset(C.eps[:, 1:2], RMS_EPS).then_inc(made, 1)
            pool.wait_ge(memset_done, 1)
            nc.gpsimd.affine_select(out=C.ident[:], in_=C.ones[:], compare_op=ALU.is_equal, fill=0.0, base=0,
                                    pattern=[[-1, P]], channel_multiplier=1).then_inc(made, 1)
    C.end_stage()


def norm_stage(nc, C, keep=None, gain=None, layer=True, src=None):
    src = C.x if src is None else src
    uid = C.n
    with ExitStack() as ctx:
        def sb(name, shape, dt=F32):
            return ctx.enter_context(nc.sbuf_tensor(f"{name}_{uid}", shape, dt))

        stats = sb("stats", [P, QT, 6])
        mv = sb("mean_var", [P, QT, 2])
        std = sb("std", [P, 2, QT])
        rstd = sb("rstd", [P, 2, QT])
        sq = sb("mean_square", [P, QT])
        normed = sb("normed", [P, 2, QT, D])
        gain_row = sb("gain_row", [P, D])
        turned = [ctx.enter_context(nc.psum_tensor(f"turned{i}_{uid}", [P, S], F32)) for i in range(2 * DK)]
        gain_loaded, var_ready, std_ready = C.sem("gain_loaded"), C.sem("var_ready"), C.sem("std_ready")
        normed_ready, turned_ready, copied = C.sem("normed_ready"), C.sem("turned_ready"), C.sem("copied")
        norms = int(layer) + int(gain is not None)

        with nc.Block() as block:
            if gain is not None:
                @block.sync
                def _(sp):
                    sp.dma_start(gain_row[:], gain.partition_broadcast(P)).then_inc(gain_loaded, 16)

            @block.vector
            def _(dve):
                if gain is not None:
                    dve.wait_ge(gain_loaded, 16)

                def moments(tiles):
                    for t in range(QT):
                        nc.vector.bn_stats(stats[:, t, :], tiles(t))
                    dve.drain()
                    for t in range(QT):
                        nc.vector.bn_aggr(mv[:, t, :], stats[:, t, :])
                    dve.drain()

                with dve.Fori(0, B // 2) as pair:
                    for u in range(2):
                        b = pair * 2 + u
                        tiles = lambda t: src[:, b * QT + t, :]
                        out = normed[:, u]
                        if layer:
                            moments(tiles)
                            nc.vector.tensor_copy(sq[:], mv[:, :, 1]).then_inc(var_ready, 1)
                            dve.wait_ge(std_ready, b * norms + 1)
                            nc.vector.reciprocal(rstd[:, 0], std[:, 0])
                            dve.drain()
                            if u == 0:
                                dve.wait_ge(turned_ready, pair * 2)
                            else:
                                dve.wait_ge(turned_ready, pair * 2)
                            for t in range(QT):
                                to = out[:, t, :] if keep is None else keep[:, b * QT + t, :]
                                ins = nc.vector.tensor_scalar(to, tiles(t), mv[:, t, 0:1], rstd[:, 0, t:t + 1],
                                                              ALU.subtract, ALU.mult)
                            if gain is None:
                                ins.then_inc(normed_ready, 1)
                            else:
                                dve.drain()
                                tiles = lambda t: keep[:, b * QT + t, :]
                        if gain is not None:
                            moments(tiles)
                            nc.vector.tensor_tensor(sq[:], mv[:, :, 0], mv[:, :, 0], ALU.mult)
                            dve.drain()
                            nc.vector.tensor_tensor(sq[:], sq[:], mv[:, :, 1], ALU.add).then_inc(var_ready, 1)
                            dve.wait_ge(std_ready, b * norms + norms)
                            nc.vector.reciprocal(rstd[:, 1], std[:, 1])
                            dve.drain()
                            dve.wait_ge(turned_ready, pair * 2)
                            for t in range(QT):
                                ins = nc.vector.scalar_tensor_tensor(out=out[:, t, :], in0=tiles(t),
                                                                     scalar=rstd[:, 1, t:t + 1], in1=gain_row[:],
                                                                     op0=ALU.mult, op1=ALU.mult)
                            ins.then_inc(normed_ready, 1)

            @block.tensor
            def _(pe):
                with pe.Fori(0, B // 2) as pair:
                    for u in range(2):
                        b = pair * 2 + u
                        pe.wait_ge(normed_ready, b + 1)
                        pe.wait_ge(copied, pair * 2)
                        for k in range(DK):
                            for t in range(QT):
                                ins = nc.tensor.transpose(turned[2 * u + k][:, t * P:(t + 1) * P],
                                                          normed[:, u, t, k * P:(k + 1) * P], C.ident[:])
                        ins.then_inc(turned_ready, 1)

            @block.scalar
            def _(act):
                with act.Fori(0, B // 2) as pair:
                    for u in range(2):
                        b = pair * 2 + u
                        for n in range(norms):
                            rms = gain is not None and n == norms - 1
                            act.wait_ge(var_ready, b * norms + n + 1)
                            nc.scalar.activation(std[:, int(rms)], sq[:], ACT.Sqrt,
                                                 bias=C.eps[:, int(rms):int(rms) + 1]).then_inc(std_ready, 1)
                        act.wait_ge(turned_ready, b + 1)
                        for k in range(DK):
                            ins = nc.scalar.activation(C.nT[:, k, batch_cols(b)], turned[2 * u + k][:], ACT.Copy)
                        ins.then_inc(copied, 1)
    C.end_stage()


def store_stage(nc, C):
    stored = C.sem("stored")
    with nc.Block() as block:
        @block.sync
        def _(sp):
            sp.dma_start(C.dram["out"].rearrange("b (t p) d -> p (b t) d", p=P), C.x[:]).then_inc(stored, 16)
            sp.wait_ge(stored, 16)


def attention_stage(nc, C, w, hd, cross=True, causal=False, rope=False, biased=False, masked=False, res=None):
    res = C.x if res is None else res
    uid = C.n
    slot = max(hd, SLOT)
    HG = P // slot
    G = H // HG
    U = HG * QT
    VC = HG * hd
    KO = H * hd // P
    scale = float(hd) ** -0.5
    kvT = C.ctxT if cross else C.nT

    with ExitStack() as ctx:
        def sb(name, shape, dt=F32):
            return ctx.enter_context(nc.sbuf_tensor(f"{name}_{uid}", shape, dt))

        def psum(name, n):
            return [ctx.enter_context(nc.psum_tensor(f"{name}{i}_{uid}", [P, 512], F32)) for i in range(n)]

        names = ["q", "k"] + (["q_swap", "k_swap"] if rope else [])
        w_all = {m: sb(f"w_{m}_all", [P, DK, G * P]) for m in names}
        w_g = {m: [sb(f"w_{m}_group{u}", [P, DK, P]) for u in range(2)] for m in names}
        wv = sb("w_v", [P, DK, H * hd])
        wo = sb("w_o", [P, KO, D])
        q = [sb(f"q{u}", [P, S]) for u in range(2)]
        k = [sb(f"k{u}", [P, S]) for u in range(2)]
        v = [sb(f"v{u}", [P, QT, VC]) for u in range(2)]
        kv_chunk = sb("kv_chunk", [P, DK, S])
        probs = [sb(f"probs{i}", [P, S]) for i in range(3)]
        probsT = [sb(f"probsT{i}", [P, S]) for i in range(2)]
        neg_max = sb("neg_max", [P, 4])
        sums = [sb(f"sums{u}", [P, U]) for u in range(2)]
        recip = sb("recip", [P, U])
        heads = sb("heads_out", [P, QT, H * hd])
        headsT = sb("heads_out_T", [P, KO, S])
        added = sb("added", [P, D])
        if rope:
            cos, sin = sb("cos", [P, S]), sb("sin", [P, S])
            turn_a, turn_b = sb("turn_a", [P, S]), sb("turn_b", [P, S])
        if biased:
            bq, bk = sb("b_q", [P, G]), sb("b_k", [P, G])
            bv, bo = sb("b_v", [P, H * hd]), sb("b_o", [P, D])
        if masked:
            mask_in = sb("mask_in", [1, B * S], mybir.dt.uint8)
            mask = sb("mask_bias", [1, B * S])
            mask_slot = sb("mask_slot", [1, P])
        if causal:
            future = sb("future", [P, P])
        ps_proj, ps_s, ps_t, ps_o = psum("ps_proj", 2), psum("ps_scores", 2), psum("ps_turned", 2), psum("ps_out", 2)

        weights, prepared = C.sem("weights"), C.sem("prepared")
        kv_staged, w_staged, projected = C.sem("kv_staged"), C.sem("w_staged"), C.sem("projected")
        q_ready, v_ready = C.sem("q_ready"), C.sem("v_ready")
        scored, maxed, exp_done = C.sem("scored"), C.sem("maxed"), C.sem("exp_done")
        turned, copied, summed = C.sem("turned"), C.sem("copied"), C.sem("summed")
        normalised, headsT_turned, headsT_copied = C.sem("normalised"), C.sem("headsT_turned"), C.sem("headsT_copied")
        out_ready, out_taken = C.sem("out_ready"), C.sem("out_taken")

        loads = [(w_all[m], w[m].rearrange("(c p) n -> p c n", p=P)) for m in names]
        loads += [(wv, w["v"].rearrange("(c p) n -> p c n", p=P)), (wo, w["o"].rearrange("(c p) n -> p c n", p=P))]
        if rope:
            loads += [(cos, w["cos"]), (sin, w["sin"])]
        if biased:
            loads += [(bq, w["bq"]), (bk, w["bk"]),
                      (bv, w["bv"].partition_broadcast(P)), (bo, w["bo"].partition_broadcast(P))]
        if masked:
            loads += [(mask_in, w["mask"]), (mask_slot, w["mask_slot"])]
        if causal:
            loads += [(future, w["future"])]

        def keys(t):
            return (t + 1) * P if causal else S

        def unit(s):
            return s // QT, s % QT

        with nc.Block() as block:
            @block.sync
            def _(sp):
                for to, of in loads:
                    sp.dma_start(to[:], of).then_inc(weights, 16)

            @block.gpsimd
            def _(pool):
                pool.wait_ge(weights, 16 * len(loads))
                with pool.Fori(0, B) as b:
                    pool.wait_ge(projected, b * G)
                    nc.gpsimd.tensor_copy(kv_chunk[:], kvT[:, :, batch_cols(b)]).then_inc(kv_staged, 1)
                    with pool.Fori(0, G // 2) as pair:
                        for u in range(2):
                            g = pair * 2 + u
                            pool.wait_ge(projected, b * G + pair * 2)
                            for m in names:
                                nc.gpsimd.tensor_copy(w_g[m][u][:], w_all[m][:, :, bass.ds(g * P, P)]) \
                                    .then_inc(w_staged, 1)

            @block.tensor
            def _(pe):
                pe.wait_ge(weights, 16 * len(loads))
                pe.wait_ge(prepared, 1)
                with pe.Fori(0, B) as b:
                    with pe.Fori(0, G // 2) as pair:
                        for u in range(2):
                            g = pair * 2 + u
                            n = b * G + g
                            pe.wait_ge(w_staged, (n + 1) * len(names))
                            pe.wait_ge(kv_staged, b + 1)
                            pe.wait_ge(out_taken, b * QT)
                            pe.wait_ge(exp_done, n * U)
                            pe.wait_ge(copied, n * U)
                            for m, bank in zip(names, ps_proj + ps_s):
                                src = kv_chunk[:] if m[0] == "k" and cross else None
                                last = not (masked and m == "k")
                                for c in range(DK):
                                    rhs = C.nT[:, c, batch_cols(b)] if m[0] == "q" or not cross else kv_chunk[:, c, :]
                                    nc.tensor.matmul(bank[:], w_g[m][u][:, c, :], rhs, start=(c == 0),
                                                     stop=(c == DK - 1 and last))
                                if not last:
                                    nc.tensor.matmul(bank[:], mask_slot[:], mask[:, batch_cols(b)],
                                                     start=False, stop=True)
                            for t in range(QT):
                                for c in range(DK):
                                    ins = nc.tensor.matmul(ps_t[0][:, t * VC:(t + 1) * VC],
                                                           kv_chunk[:, c, t * P:(t + 1) * P],
                                                           wv[:, c, bass.ds(g * VC, VC)], start=(c == 0),
                                                           stop=(c == DK - 1))
                            ins.then_inc(projected, 1)
                            pe.wait_ge(q_ready, n + 1)
                            pe.wait_ge(v_ready, n + 1)
                            for s in range(U + 2):
                                if s < U:
                                    h, t = unit(s)
                                    part = slice(h * slot, (h + 1) * slot)
                                    if s >= 2:
                                        pe.wait_ge(exp_done, n * U + s - 1)
                                    ins = nc.tensor.matmul(ps_s[s % 2][:, :keys(t)], q[u][part, t * P:(t + 1) * P],
                                                           k[u][part, :keys(t)], start=True, stop=not causal)
                                    if causal:
                                        ins = nc.tensor.matmul(ps_s[s % 2][:, t * P:keys(t)], C.ident[:], future[:],
                                                               start=False, stop=True)
                                    ins.then_inc(scored, 1)
                                if 1 <= s <= U:
                                    i = s - 1
                                    pe.wait_ge(exp_done, n * U + i + 1)
                                    if i >= 2:
                                        pe.wait_ge(copied, n * U + i - 1)
                                    for c in range(keys(unit(i)[1]) // P):
                                        ins = nc.tensor.transpose(ps_t[i % 2][:, c * P:(c + 1) * P],
                                                                  probs[i % 3][:, c * P:(c + 1) * P], C.ident[:])
                                    ins.then_inc(turned, 1)
                                if s >= 2:
                                    i = s - 2
                                    h, t = unit(i)
                                    pe.wait_ge(copied, n * U + i + 1)
                                    if i == 0:
                                        pe.wait_ge(normalised, n + 1)
                                    nk = keys(t) // P
                                    for c in range(nk):
                                        ins = nc.tensor.matmul(ps_o[u][:, i * hd:(i + 1) * hd],
                                                               probsT[i % 2][:, c * P:(c + 1) * P],
                                                               v[u][:, c, h * hd:(h + 1) * hd],
                                                               start=(c == 0), stop=(c == nk - 1))
                                    ins.then_inc(summed, 1)
                    pe.wait_ge(normalised, (b + 1) * G + 2)
                    for c in range(KO):
                        if c >= 2:
                            pe.wait_ge(headsT_copied, b * KO + c - 1)
                        for t in range(QT):
                            ins = nc.tensor.transpose(ps_t[c % 2][:, t * P:(t + 1) * P],
                                                      heads[:, t, c * P:(c + 1) * P], C.ident[:])
                        ins.then_inc(headsT_turned, 1)
                    pe.wait_ge(headsT_copied, (b + 1) * KO)
                    for t in range(QT):
                        if t >= 2:
                            pe.wait_ge(out_taken, b * QT + t - 1)
                        for c in range(KO):
                            ins = nc.tensor.matmul(ps_proj[t % 2][:, :D], headsT[:, c, t * P:(t + 1) * P], wo[:, c, :],
                                                   start=(c == 0), stop=(c == KO - 1))
                        ins.then_inc(out_ready, 1)

            @block.scalar
            def _(act):
                act.wait_ge(prepared, 1)
                with act.Fori(0, B) as b:
                    with act.Fori(0, G // 2) as pair:
                        for u in range(2):
                            g = pair * 2 + u
                            n = b * G + g
                            if not rope:
                                act.wait_ge(projected, n + 1)
                                nc.scalar.activation(q[u][:], ps_proj[0][:], ACT.Identity, scale=scale,
                                                     bias=bq[:, bass.ds(g, 1)] if biased else 0.0)
                                nc.scalar.activation(k[u][:], ps_proj[1][:], ACT.Identity,
                                                     bias=bk[:, bass.ds(g, 1)] if biased else 0.0).then_inc(q_ready, 1)
                            for s in range(U):
                                act.wait_ge(maxed, n * U + s + 1)
                                if s >= 3:
                                    act.wait_ge(turned, n * U + s - 2)
                                cols = keys(unit(s)[1])
                                nc.scalar.activation(probs[s % 3][:, :cols], ps_s[s % 2][:, :cols], ACT.Exp,
                                                     bias=neg_max[:, s % 4:s % 4 + 1],
                                                     accum_out=sums[u][:, s:s + 1]).then_inc(exp_done, 1)

            @block.vector
            def _(dve):
                dve.wait_ge(weights, 16 * len(loads))
                if masked:
                    nc.vector.tensor_scalar(mask[:], mask_in[:], 1.0, -NEG, ALU.subtract, ALU.mult)
                if biased:
                    nc.vector.tensor_scalar(bq[:], bq[:], scale, None, ALU.mult)
                dve.drain().then_inc(prepared, 1)
                dve.sem_inc(normalised, 2)
                with dve.Fori(0, B) as b:
                    with dve.Fori(0, G // 2) as pair:
                        for u in range(2):
                            g = pair * 2 + u
                            n = b * G + g
                            dve.wait_ge(projected, n + 1)
                            if rope:
                                for to, a, swap, by in ((q[u], ps_proj[0], ps_s[0], scale), (k[u], ps_proj[1], ps_s[1], 1.0)):
                                    nc.vector.scalar_tensor_tensor(out=turn_a[:], in0=a[:], scalar=by, in1=cos[:],
                                                                   op0=ALU.mult, op1=ALU.mult)
                                    nc.vector.scalar_tensor_tensor(out=turn_b[:], in0=swap[:], scalar=by, in1=sin[:],
                                                                   op0=ALU.mult, op1=ALU.mult)
                                    dve.drain()
                                    ins = nc.vector.tensor_tensor(to[:], turn_a[:], turn_b[:], ALU.add)
                                    dve.drain()
                                dve.sem_inc(q_ready, 1)
                            values = ps_t[0][:, :QT * VC].rearrange("p (t c) -> p t c", t=QT)
                            if biased:
                                nc.vector.tensor_tensor(v[u][:], values, bv[:, bass.ds(g * VC, VC)].unsqueeze(1)
                                                        .broadcast_to([P, QT, VC]), ALU.add).then_inc(v_ready, 1)
                            else:
                                nc.vector.tensor_copy(v[u][:], values).then_inc(v_ready, 1)
                            for s in range(U + 1):
                                if s < U:
                                    dve.wait_ge(scored, n * U + s + 1)
                                    nc.vector.tensor_reduce(neg_max[:, s % 4:s % 4 + 1],
                                                            ps_s[s % 2][:, :keys(unit(s)[1])], AX_X, ALU.max,
                                                            negate=True).then_inc(maxed, 1)
                                if s >= 1:
                                    i = s - 1
                                    cols = keys(unit(i)[1])
                                    dve.wait_ge(turned, n * U + i + 1)
                                    if i >= 2:
                                        dve.wait_ge(summed, n * U + i - 1)
                                    nc.vector.tensor_copy(probsT[i % 2][:, :cols], ps_t[i % 2][:, :cols]) \
                                        .then_inc(copied, 1)
                            dve.wait_ge(exp_done, (n + 1) * U)
                            nc.vector.reciprocal(recip[:], sums[u][:])
                            dve.drain()
                            dve.wait_ge(summed, (n + 1) * U)
                            to = heads[:, :, bass.ds(g * VC, VC)].rearrange("p t (h d) -> p t h d", h=HG)
                            of = ps_o[u][:, :U * hd].rearrange("p (h t d) -> p t h d", h=HG, t=QT)
                            by = recip[:].rearrange("p (h t) -> p t h", h=HG).unsqueeze(3).broadcast_to([P, QT, HG, hd])
                            nc.vector.tensor_tensor(to, of, by, ALU.mult).then_inc(normalised, 1)
                    for c in range(KO):
                        dve.wait_ge(headsT_turned, b * KO + c + 1)
                        nc.vector.tensor_copy(headsT[:, c, :], ps_t[c % 2][:]).then_inc(headsT_copied, 1)
                    for t in range(QT):
                        dve.wait_ge(out_ready, b * QT + t + 1)
                        x_tile = res[:, b * QT + t, :]
                        if biased:
                            nc.vector.tensor_tensor(added[:], ps_proj[t % 2][:, :D], bo[:], ALU.add).then_inc(out_taken, 1)
                            dve.drain()
                            nc.vector.tensor_tensor(x_tile, x_tile, added[:], ALU.add)
                            dve.drain()
                        else:
                            nc.vector.tensor_tensor(x_tile, x_tile, ps_proj[t % 2][:, :D], ALU.add).then_inc(out_taken, 1)
    C.end_stage()




def stage_tensors(nc, ctx, uid):
    def sb(name, shape, dt=F32):
        return ctx.enter_context(nc.sbuf_tensor(f"{name}_{uid}", shape, dt))

    def psum(name, n, dt=F32):
        return [ctx.enter_context(nc.psum_tensor(f"{name}{i}_{uid}", [P, 2048 // mybir.dt.size(dt)], dt)) for i in range(n)]

    return sb, psum


def channel_mix_stage(nc, C, w):
    with ExitStack() as ctx:
        sb, psum = stage_tensors(nc, ctx, C.n)
        wr, wk, wv = (sb(n, [P, DK, D]) for n in ("w_r", "w_k", "w_v"))
        mu, rest = sb("mu", [P, 2, DK]), sb("one_less_mu", [P, 2, DK])
        earlier = sb("earlier", [P, S])
        mixed = [sb(f"mixed{u}", [P, 2, DK, S]) for u in range(2)]
        k_act = [sb(f"k_act{u}", [P, DK, S]) for u in range(2)]
        gate, gated = sb("gate", [P, 2, D]), sb("gated", [P, D])
        ps_k, ps_o = psum("ps_k", 2 * DK), psum("ps_rv", QT)
        weights, mixed_ready, k_ready = C.sem("weights"), C.sem("mixed_ready"), C.sem("k_ready")
        k_acted, out_ready, gate_ready, out_taken = C.sem("k_acted"), C.sem("out_ready"), C.sem("gate_ready"), C.sem("out_taken")

        with nc.Block() as block:
            @block.sync
            def _(sp):
                for to, of in ((wr, w["r"]), (wk, w["k"]), (wv, w["v"])):
                    sp.dma_start(to[:], of.rearrange("(c p) n -> p c n", p=P)).then_inc(weights, 16)
                sp.dma_start(mu[:], w["mu"]).then_inc(weights, 16)

            @block.vector
            def _(dve):
                dve.wait_ge(weights, 64)
                nc.vector.tensor_scalar(rest[:], mu[:], -1.0, 1.0, ALU.mult, ALU.add)
                nc.vector.memset(earlier[:, 0:1], 0.0)
                dve.drain()
                with dve.Fori(0, B // 2) as pair:
                    for u in range(2):
                        b = pair * 2 + u
                        dve.wait_ge(out_ready, pair * 2 * QT)
                        for i in range(2):
                            for c in range(DK):
                                nc.vector.tensor_scalar(earlier[:, 1:], C.nT[:, c, bass.ds(b * S, S - 1)],
                                                        rest[:, i, c:c + 1], None, ALU.mult)
                                dve.drain()
                                nc.vector.scalar_tensor_tensor(out=mixed[u][:, i, c, :], in0=C.nT[:, c, batch_cols(b)],
                                                               scalar=mu[:, i, c:c + 1], in1=earlier[:],
                                                               op0=ALU.mult, op1=ALU.add)
                                dve.drain()
                        dve.sem_inc(mixed_ready, 1)
                        for c in range(DK):
                            dve.wait_ge(k_ready, b * DK + c + 1)
                            bank = ps_k[u * DK + c]
                            ins = nc.vector.tensor_scalar(k_act[u][:, c, :], bank[:], 0.0, None, ALU.max)
                            dve.drain()
                            ins = nc.vector.tensor_tensor(k_act[u][:, c, :], k_act[u][:, c, :], k_act[u][:, c, :], ALU.mult)
                            ins.then_inc(k_acted, 1)
                        for t in range(QT):
                            dve.wait_ge(gate_ready, b * QT + t + 1)
                            nc.vector.tensor_tensor(gated[:], gate[:, t % 2, :], ps_o[t][:, D:], ALU.mult).then_inc(out_taken, 1)
                            dve.drain()
                            x_tile = C.x[:, b * QT + t, :]
                            nc.vector.tensor_tensor(x_tile, x_tile, gated[:], ALU.add)
                            dve.drain()

            @block.tensor
            def _(pe):
                pe.wait_ge(weights, 64)
                with pe.Fori(0, B // 2) as pair:
                    for u in range(2):
                        b = pair * 2 + u
                        pe.wait_ge(mixed_ready, b + 1)
                        pe.wait_ge(k_acted, pair * 2 * DK)
                        for m in range(DK):
                            for c in range(DK):
                                ins = nc.tensor.matmul(ps_k[u * DK + m][:], wk[:, c, m * P:(m + 1) * P],
                                                       mixed[u][:, 1, c, :], start=(c == 0), stop=(c == DK - 1))
                            ins.then_inc(k_ready, 1)
                        for t in range(QT):
                            pe.wait_ge(out_taken, b * QT)
                            for c in range(DK):
                                nc.tensor.matmul(ps_o[t][:, :D], mixed[u][:, 0, c, t * P:(t + 1) * P], wr[:, c, :],
                                                 start=(c == 0), stop=(c == DK - 1))
                            pe.wait_ge(k_acted, (b + 1) * DK)
                            for c in range(DK):
                                ins = nc.tensor.matmul(ps_o[t][:, D:], k_act[u][:, c, t * P:(t + 1) * P], wv[:, c, :],
                                                       start=(c == 0), stop=(c == DK - 1))
                            ins.then_inc(out_ready, 1)

            @block.scalar
            def _(act):
                with act.Fori(0, B // 2) as pair:
                    for u in range(2):
                        b = pair * 2 + u
                        for t in range(QT):
                            act.wait_ge(out_ready, b * QT + t + 1)
                            if t >= 2:
                                act.wait_ge(out_taken, b * QT + t - 1)
                            else:
                                act.wait_ge(out_taken, b * QT)
                            nc.scalar.activation(gate[:, t % 2, :], ps_o[t][:, :D], ACT.Sigmoid).then_inc(gate_ready, 1)
    C.end_stage()


def router_stage(nc, C, w, experts, share, capacity=None, add=None):
    E, N = experts, TILES * experts
    BITS = 30
    with ExitStack() as ctx:
        sb, psum = stage_tensors(nc, ctx, C.n)
        wr = sb("w_router", [P, DK, E])
        first = sb("first_rank", [P, E])
        logitsT = sb("logits_T", [P, 2, S])
        logits = sb("logits", [P, TILES, E])
        probs = sb("probs", [P, TILES, E])
        left, ranked, chosen = sb("left", [P, TILES, E]), sb("ranked", [P, TILES, E]), sb("chosen", [P, TILES, E])
        best = sb("best", [P, TILES])
        if capacity:
            bits, bit, trial = sb("threshold_bits", [P, E], I32), sb("bit", [P, E], I32), sb("trial_bits", [P, E], I32)
            enough = sb("enough", [P, E], I32)
            counts, room = sb("counts", [P, E]), sb("room", [P, E])
            over = sb("over", [P, TILES, E])
            equal = sb("equal", [P, E, TILES])
            before, zeros = sb("before", [P, E, TILES]), sb("zeros", [P, TILES])
            lower = sb("lower", [P, P])
        ps_l, ps_t, ps_c, ps_e = psum("ps_logits", 2), psum("ps_turned", 2), psum("ps_counts", 1), psum("ps_equal", 2)
        weights, logitsT_ready, logitsT_copied = C.sem("weights"), C.sem("logitsT_ready"), C.sem("logitsT_copied")
        turned, taken, less_max, exp_ready = C.sem("turned"), C.sem("taken"), C.sem("less_max"), C.sem("exp_ready")
        counts_ready, counted, zeroed = C.sem("counts_ready"), C.sem("counted"), C.sem("zeroed")
        loads = [(wr, w["router"].rearrange("(c p) e -> p c e", p=P)), (first, w["first"].partition_broadcast(P))]
        if capacity:
            loads.append((lower, w["lower"]))

        def each(row):
            return row[:].unsqueeze(2).broadcast_to([P, TILES, E])

        def per_expert(col):
            return col.unsqueeze(1).broadcast_to([P, TILES, E])

        with nc.Block() as block:
            @block.sync
            def _(sp):
                for to, of in loads:
                    sp.dma_start(to[:], of).then_inc(weights, 16)

            @block.gpsimd
            def _(pool):
                nc.gpsimd.memset(logitsT[:], 0.0).then_inc(zeroed, 1)

            @block.scalar
            def _(act):
                act.wait_ge(zeroed, 1)
                with act.Fori(0, B // 2) as pair:
                    for u in range(2):
                        b = pair * 2 + u
                        act.wait_ge(logitsT_ready, b + 1)
                        nc.scalar.activation(logitsT[:E, u, :], ps_l[u][:E, :], ACT.Copy).then_inc(logitsT_copied, 1)
                act.wait_ge(less_max, 1)
                nc.scalar.activation(probs[:], probs[:], ACT.Exp).then_inc(exp_ready, 1)

            @block.tensor
            def _(pe):
                pe.wait_ge(weights, 16 * len(loads))
                with pe.Fori(0, B // 2) as pair:
                    for u in range(2):
                        b = pair * 2 + u
                        pe.wait_ge(logitsT_copied, pair * 2)
                        for c in range(DK):
                            ins = nc.tensor.matmul(ps_l[u][:E, :], wr[:, c, :], C.nT[:, c, batch_cols(b)],
                                                   start=(c == 0), stop=(c == DK - 1))
                        ins.then_inc(logitsT_ready, 1)
                        pe.wait_ge(logitsT_copied, b + 1)
                        pe.wait_ge(taken, pair * 2)
                        for t in range(QT):
                            ins = nc.tensor.transpose(ps_t[u][:, t * P:(t + 1) * P], logitsT[:, u, t * P:(t + 1) * P],
                                                      C.ident[:])
                        ins.then_inc(turned, 1)
                if capacity:
                    with pe.Fori(0, BITS) as i:
                        pe.wait_ge(counts_ready, i + 1)
                        nc.tensor.matmul(ps_c[0][:, :E], C.ones[:], counts[:], start=True, stop=True).then_inc(counted, 1)
                    pe.wait_ge(counts_ready, BITS + 1)
                    nc.tensor.matmul(ps_c[0][:, :E], C.ones[:], counts[:], start=True, stop=True)
                    nc.tensor.matmul(ps_e[0][:, :N], lower[:], equal[:], start=True, stop=True)
                    nc.tensor.matmul(ps_e[1][:, :N], C.ones[:], equal[:], start=True, stop=True).then_inc(counted, 1)

            @block.vector
            def _(dve):
                dve.wait_ge(weights, 16 * len(loads))
                with dve.Fori(0, B // 2) as pair:
                    for u in range(2):
                        b = pair * 2 + u
                        dve.wait_ge(turned, b + 1)
                        nc.vector.tensor_copy(logits[:, bass.ds(b * QT, QT), :],
                                              ps_t[u][:].rearrange("p (t e) -> p t e", t=QT)[:, :, :E]).then_inc(taken, 1)
                dve.drain()
                nc.vector.tensor_reduce(best[:], logits[:], AX_X, ALU.max)
                dve.drain()
                nc.vector.tensor_tensor(probs[:], logits[:], each(best), ALU.subtract)
                dve.drain().then_inc(less_max, 1)

                def first_best(of, marks):
                    nc.vector.tensor_reduce(best[:], of[:], AX_X, ALU.max)
                    dve.drain()
                    nc.vector.tensor_tensor(ranked[:], of[:], each(best), ALU.is_equal)
                    dve.drain()
                    nc.vector.tensor_tensor(ranked[:], ranked[:], per_expert(first[:]), ALU.mult)
                    dve.drain()
                    nc.vector.tensor_reduce(best[:], ranked[:], AX_X, ALU.max)
                    dve.drain()
                    nc.vector.tensor_tensor(marks[:], ranked[:], each(best), ALU.is_equal)
                    dve.drain()

                if not capacity:
                    first_best(logits, chosen)
                dve.wait_ge(exp_ready, 1)
                nc.vector.tensor_reduce(best[:], probs[:], AX_X, ALU.add)
                dve.drain()
                nc.vector.reciprocal(best[:], best[:])
                dve.drain()
                nc.vector.tensor_tensor(probs[:], probs[:], each(best), ALU.mult)
                dve.drain()
                if capacity:
                    first_best(probs, chosen)
                    nc.vector.scalar_tensor_tensor(out=left[:], in0=chosen[:], scalar=-2.0, in1=probs[:],
                                                   op0=ALU.mult, op1=ALU.add)
                    dve.drain()
                    first_best(left, left)
                    nc.vector.tensor_tensor(chosen[:], chosen[:], left[:], ALU.add)
                    dve.drain()
                nc.vector.tensor_tensor(share[:], probs[:], chosen[:], ALU.mult)
                dve.drain()
                if capacity:
                    nc.vector.memset(bits[:], 0)
                    nc.vector.memset(trial[:], 1 << (BITS - 1))
                    nc.vector.memset(bit[:], 1 << (BITS - 1))
                    dve.drain()
                    with dve.Fori(0, BITS) as i:
                        nc.vector.tensor_tensor(over[:], share[:], per_expert(trial[:].bitcast(F32)), ALU.is_ge)
                        dve.drain()
                        nc.vector.tensor_reduce(counts[:], over[:].rearrange("p t e -> p e t"), AX_X, ALU.add)
                        dve.drain().then_inc(counts_ready, 1)
                        dve.wait_ge(counted, i + 1)
                        nc.vector.tensor_scalar(enough[:], ps_c[0][:, :E], float(capacity), -1.0, ALU.is_ge, ALU.mult)
                        dve.drain()
                        nc.vector.tensor_tensor(enough[:], enough[:], bit[:], ALU.bitwise_and)
                        dve.drain()
                        nc.vector.tensor_tensor(bits[:], bits[:], enough[:], ALU.bitwise_or)
                        nc.vector.tensor_scalar(bit[:], bit[:], 1, None, ALU.logical_shift_right)
                        dve.drain()
                        nc.vector.tensor_tensor(trial[:], bits[:], bit[:], ALU.bitwise_or)
                        dve.drain()
                    threshold = per_expert(bits[:].bitcast(F32))
                    nc.vector.tensor_tensor(over[:], share[:], threshold, ALU.is_gt)
                    nc.vector.tensor_tensor(equal[:].rearrange("p e t -> p t e"), share[:], threshold, ALU.is_equal)
                    nc.vector.memset(zeros[:], 0.0)
                    dve.drain()
                    nc.vector.tensor_reduce(counts[:], over[:].rearrange("p t e -> p e t"), AX_X, ALU.add)
                    dve.drain().then_inc(counts_ready, 1)
                    dve.wait_ge(counted, BITS + 1)
                    nc.vector.tensor_scalar(room[:], ps_c[0][:, :E], -1.0, float(capacity), ALU.mult, ALU.add)
                    totals = ps_e[1][:, :N].rearrange("p (e t) -> p e t", e=E)
                    nc.vector.memset(before[:, :, 0:1], 0.0)
                    for e in range(E):
                        nc.vector.tensor_tensor_scan(before[:, e, 1:], totals[:, e, :TILES - 1], zeros[:, :TILES - 1],
                                                     0.0, ALU.add, ALU.add)
                    dve.drain()
                    nc.vector.tensor_tensor(before[:], before[:], ps_e[0][:, :N].rearrange("p (e t) -> p e t", e=E), ALU.add)
                    dve.drain()
                    nc.vector.tensor_tensor(before[:], before[:], room[:].unsqueeze(2).broadcast_to([P, E, TILES]), ALU.is_lt)
                    dve.drain()
                    nc.vector.tensor_tensor(before[:], before[:], equal[:], ALU.mult)
                    dve.drain()
                    nc.vector.tensor_tensor(over[:], over[:], before[:].rearrange("p e t -> p t e"), ALU.add)
                    dve.drain()
                    nc.vector.tensor_tensor(share[:], share[:], over[:], ALU.mult)
                if add is not None:
                    nc.vector.tensor_tensor(C.x[:], C.x[:], add[:], ALU.add)
    C.end_stage()


def experts_stage(nc, C, w1, w2, experts, share, func, b1=None, b2=None):
    E, FK = experts, FFN // P
    with ExitStack() as ctx:
        sb, psum = stage_tensors(nc, ctx, C.n)
        w1_e = [sb(f"w1_{u}", [P, DK, FFN]) for u in range(2)]
        w2_e = [sb(f"w2_{u}", [P, FK, D]) for u in range(2)]
        hid = [sb(f"hidden{v}", [P, FK, S]) for v in range(2)]
        if b1 is not None:
            b1_e, b2_e = [sb(f"b1_{u}", [P, FK]) for u in range(2)], [sb(f"b2_{u}", [P, D]) for u in range(2)]
            biased = sb("biased", [P, 2, D])
        ps_h, ps_y = psum("ps_hidden", FK), psum("ps_out", QT)
        loaded = [C.sem(f"expert_loaded{u}") for u in range(2)]
        hid_ready, hid_acted, out_ready, out_taken = C.sem("hid_ready"), C.sem("hid_acted"), C.sem("out_ready"), C.sem("out_taken")
        per_expert = 16 * (4 if b1 is not None else 2)

        with nc.Block() as block:
            @block.sync
            def _(sp):
                with sp.Fori(0, E // 2) as pair:
                    for u in range(2):
                        e = pair * 2 + u
                        sp.wait_ge(out_taken, pair * (2 * B * QT))
                        sp.dma_start(w1_e[u][:], w1[e].rearrange("(c p) f -> p c f", p=P)).then_inc(loaded[u], 16)
                        sp.dma_start(w2_e[u][:], w2[e].rearrange("(c p) n -> p c n", p=P)).then_inc(loaded[u], 16)
                        if b1 is not None:
                            sp.dma_start(b1_e[u][:], b1[e]).then_inc(loaded[u], 16)
                            sp.dma_start(b2_e[u][:], b2[e].partition_broadcast(P)).then_inc(loaded[u], 16)

            @block.tensor
            def _(pe):
                with pe.Fori(0, E // 2) as epair:
                    for u in range(2):
                        e = epair * 2 + u
                        with pe.Fori(0, B // 2) as bpair:
                            for v in range(2):
                                m = e * B + bpair * 2 + v
                                for f in range(FK):
                                    pe.wait_ge(loaded[u], (epair + 1) * per_expert)
                                    pe.wait_ge(hid_acted, m * FK)
                                    for c in range(DK):
                                        ins = nc.tensor.matmul(ps_h[f][:], w1_e[u][:, c, f * P:(f + 1) * P],
                                                               C.nT[:, c, batch_cols(bpair * 2 + v)],
                                                               start=(c == 0), stop=(c == DK - 1))
                                    ins.then_inc(hid_ready, 1)
                            for v in range(2):
                                m = e * B + bpair * 2 + v
                                for t in range(QT):
                                    pe.wait_ge(hid_acted, (m + 1) * FK)
                                    pe.wait_ge(out_taken, m * QT + (t if v else 0))
                                    for f in range(FK):
                                        ins = nc.tensor.matmul(ps_y[t][:, :D], hid[v][:, f, t * P:(t + 1) * P],
                                                               w2_e[u][:, f, :], start=(f == 0), stop=(f == FK - 1))
                                    ins.then_inc(out_ready, 1)

            @block.scalar
            def _(act):
                with act.Fori(0, E // 2) as epair:
                    for u in range(2):
                        e = epair * 2 + u
                        with act.Fori(0, B // 2) as bpair:
                            for v in range(2):
                                m = e * B + bpair * 2 + v
                                for f in range(FK):
                                    act.wait_ge(hid_ready, m * FK + f + 1)
                                    act.wait_ge(out_ready, (e * B + bpair * 2) * QT)
                                    nc.scalar.activation(hid[v][:, f, :], ps_h[f][:], func,
                                                         bias=b1_e[u][:, f:f + 1] if b1 is not None else 0.0) \
                                        .then_inc(hid_acted, 1)

            @block.vector
            def _(dve):
                with dve.Fori(0, E // 2) as epair:
                    for u in range(2):
                        e = epair * 2 + u
                        with dve.Fori(0, B) as b:
                            for t in range(QT):
                                tile = b * QT + t
                                dve.wait_ge(out_ready, (e * B + b) * QT + t + 1)
                                x_tile = C.x[:, tile, :]
                                part = ps_y[t][:, :D]
                                if b1 is not None:
                                    part = biased[:, t % 2, :]
                                    nc.vector.tensor_tensor(part, ps_y[t][:, :D], b2_e[u][:], ALU.add)
                                    dve.drain()
                                nc.vector.scalar_tensor_tensor(out=x_tile, in0=part, scalar=share[:, tile, bass.ds(e, 1)],
                                                               in1=x_tile, op0=ALU.mult, op1=ALU.add)
                                dve.drain().then_inc(out_taken, 1)
    C.end_stage()


def quantised_stage(nc, C, w):
    F = 1024
    FK = F // P
    with ExitStack() as ctx:
        sb, psum = stage_tensors(nc, ctx, C.n)
        w1, w2 = sb("w1", [P, FK, D]), sb("w2", [P, DK, F])
        w1q, w2q = sb("w1_int", [P, FK, D], BF16), sb("w2_int", [P, DK, F], BF16)
        w1T, w2T = sb("w1_int_T", [P, DK, F], BF16), sb("w2_int_T", [P, FK, D], BF16)
        s1, r1 = sb("w1_scale", [P, FK]), sb("w1_inverse", [P, FK])
        s2, r2 = sb("w2_scale", [P, DK]), sb("w2_inverse", [P, DK])
        b1, b2 = sb("b1", [P, FK]), sb("b2", [P, DK])
        tmp1, tmp2 = sb("tmp1", [P, FK]), sb("tmp2", [P, DK])
        top = sb("top", [P, 1])
        top_all = sb("top_all", [P, 2])
        s_in, r_in = sb("in_scale", [P, 2]), sb("in_inverse", [P, 2])
        f_scale, f_inv = sb("f_scale", [P, FK]), sb("f_inverse", [P, FK])
        d_scale, d_inv = sb("d_scale", [P, DK]), sb("d_inverse", [P, DK])
        q_scale, q_bias = sb("q_scale", [P, FK]), sb("q_bias", [P, FK])
        diag = sb("diagonals", [P, 2, DK, P])
        rows = sb("scale_and_bias_rows", [P, 2, D])
        most = sb("most", [P, FK, B])
        ident16 = sb("ident16", [P, P], BF16)
        relu_n = sb("relu_n", [P, 2, S])
        nq = sb("n_int", [P, DK, B * S], BF16)
        relu_h = sb("relu_h", [P, 2, S])
        hq = [sb(f"hidden_int{u}", [P, FK, S], BF16) for u in range(2)]
        out = sb("out", [P, D])
        ps_w = psum("ps_weights", 1, BF16)
        ps_r = psum("ps_rows", 1)
        ps_h, ps_o = psum("ps_hidden", 4), psum("ps_out", 2)
        loaded, w_ready, w_turned, w_copied = C.sem("loaded"), C.sem("w_ready"), C.sem("w_turned"), C.sem("w_copied")
        top_ready, top_reduced, n_scaled = C.sem("top_ready"), C.sem("top_reduced"), C.sem("in_scale_ready")
        relu_ready, n_ready = C.sem("relu_ready"), C.sem("n_ready")
        hid_ready, hid_maxed, diag_ready, rows_ready = C.sem("hid_ready"), C.sem("hid_maxed"), C.sem("diag_ready"), C.sem("rows_ready")
        scales_ready, hid2_ready, relu2_ready = C.sem("scales_ready"), C.sem("hid2_ready"), C.sem("relu2_ready")
        hq_ready, out_ready, out_taken = C.sem("hq_ready"), C.sem("out_ready"), C.sem("out_taken")

        def largest_to_scale(dve, i):
            nc.vector.tensor_scalar(s_in[:, i:i + 1], top_all[:, i:i + 1], 1e-8, 1.0 / 255.0, ALU.max, ALU.mult)
            dve.drain()
            nc.vector.reciprocal(r_in[:, i:i + 1], s_in[:, i:i + 1])
            dve.drain()

        def bias(dve, b, scale, inv, tmp):
            nc.vector.reciprocal(inv[:], scale[:])
            dve.drain()
            nc.vector.tensor_tensor(tmp[:], b[:], inv[:], ALU.mult)
            dve.drain()
            nc.vector.tensor_scalar(tmp[:], tmp[:], ROUND, -ROUND, ALU.add, ALU.add)
            dve.drain()
            nc.vector.tensor_tensor(b[:], tmp[:], scale[:], ALU.mult)
            dve.drain()

        with nc.Block() as block:
            @block.sync
            def _(sp):
                sp.dma_start(w1[:], w["w1"].rearrange("(c p) d -> p c d", p=P)).then_inc(loaded, 16)
                sp.dma_start(w2[:], w["w2"].rearrange("(c p) f -> p c f", p=P)).then_inc(loaded, 16)
                sp.dma_start(b1[:], w["b1"]).then_inc(loaded, 16)
                sp.dma_start(b2[:], w["b2"]).then_inc(loaded, 16)

            @block.gpsimd
            def _(pool):
                for i in range(2):
                    pool.wait_ge(top_ready, i + 1)
                    nc.gpsimd.partition_all_reduce(top_all[:, i:i + 1], top[:], P, bass.bass_isa.ReduceOp.max) \
                        .then_inc(top_reduced, 1)

            @block.vector
            def _(dve):
                dve.wait_ge(loaded, 64)
                nc.vector.tensor_copy(ident16[:], C.ident[:])
                for wt, s, r, n in ((w1, s1, r1, FK), (w2, s2, r2, DK)):
                    nc.vector.tensor_reduce(s[:], wt[:], AX_X, ALU.max, apply_absolute_value=True)
                    dve.drain()
                    nc.vector.tensor_scalar(s[:], s[:], 1e-8, 1.0 / 127.0, ALU.max, ALU.mult)
                    dve.drain()
                    nc.vector.reciprocal(r[:], s[:])
                    dve.drain()
                for wt, wq, r, n in ((w1, w1q, r1, FK), (w2, w2q, r2, DK)):
                    for i in range(n):
                        nc.vector.tensor_scalar(wt[:, i, :], wt[:, i, :], r[:, i:i + 1], ROUND, ALU.mult, ALU.add)
                    dve.drain()
                    nc.vector.tensor_scalar(wt[:], wt[:], -ROUND, 127.0, ALU.add, ALU.min)
                    dve.drain()
                    nc.vector.tensor_scalar(wq[:], wt[:], -128.0, None, ALU.max)
                dve.drain().then_inc(w_ready, 1)
                nc.vector.tensor_reduce(top[:], C.nT[:].rearrange("p c t -> p (c t)"), AX_X, ALU.max).then_inc(top_ready, 1)
                dve.wait_ge(top_reduced, 1)
                largest_to_scale(dve, 0)
                dve.sem_inc(n_scaled, 1)
                for c in range(DK):
                    with dve.Fori(0, B // 2) as pair:
                        for u in range(2):
                            b = pair * 2 + u
                            dve.wait_ge(relu_ready, b + (c * B + 1))
                            nc.vector.tensor_scalar(nq[:, c, batch_cols(b)], relu_n[:, u, :], ROUND, -ROUND,
                                                    ALU.add, ALU.add).then_inc(n_ready, 1)
                nc.vector.tensor_scalar(f_scale[:], s1[:], s_in[:, 0:1], None, ALU.mult)
                dve.drain()
                bias(dve, b1, f_scale, f_inv, tmp1)
                with dve.Fori(0, B) as b:
                    for f in range(FK):
                        dve.wait_ge(hid_ready, b * FK + f + 1)
                        nc.vector.tensor_reduce(most[:, f, bass.ds(b, 1)], ps_h[f % 4][:], AX_X, ALU.max).then_inc(hid_maxed, 1)
                dve.drain()
                nc.vector.tensor_reduce(tmp1[:], most[:], AX_X, ALU.max)
                dve.drain()
                nc.vector.tensor_tensor(tmp1[:], tmp1[:], f_scale[:], ALU.mult)
                dve.drain()
                nc.vector.tensor_tensor(tmp1[:], tmp1[:], b1[:], ALU.add)
                dve.drain()
                nc.vector.tensor_reduce(top[:], tmp1[:], AX_X, ALU.max)
                dve.drain()
                nc.vector.tensor_scalar(top[:], top[:], 0.0, None, ALU.max).then_inc(top_ready, 1)
                dve.wait_ge(top_reduced, 2)
                largest_to_scale(dve, 1)
                nc.vector.tensor_scalar(q_scale[:], f_scale[:], r_in[:, 1:2], None, ALU.mult)
                nc.vector.tensor_scalar(q_bias[:], b1[:], r_in[:, 1:2], None, ALU.mult)
                nc.vector.tensor_scalar(d_scale[:], s2[:], s_in[:, 1:2], None, ALU.mult)
                dve.drain().then_inc(scales_ready, 1)
                bias(dve, b2, d_scale, d_inv, tmp2)
                for c in range(DK):
                    nc.vector.tensor_scalar(diag[:, 0, c, :], C.ident[:], d_scale[:, c:c + 1], None, ALU.mult)
                    nc.vector.tensor_scalar(diag[:, 1, c, :], C.ident[:], b2[:, c:c + 1], None, ALU.mult)
                dve.drain().then_inc(diag_ready, 1)
                dve.wait_ge(rows_ready, 1)
                nc.vector.tensor_copy(rows[:].rearrange("p a d -> p (a d)"), ps_r[0][:])
                dve.drain()
                with dve.Fori(0, B // 2) as pair:
                    for u in range(2):
                        b = pair * 2 + u
                        for f in range(FK):
                            dve.wait_ge(relu2_ready, b * FK + f + 1)
                            dve.wait_ge(out_ready, pair * 2 * QT)
                            nc.vector.tensor_scalar(hq[u][:, f, :], relu_h[:, f % 2, :], ROUND, -ROUND,
                                                    ALU.add, ALU.add).then_inc(hq_ready, 1)
                        for t in range(QT):
                            dve.wait_ge(out_ready, b * QT + t + 1)
                            nc.vector.tensor_tensor(out[:], ps_o[t % 2][:, :D], rows[:, 0, :], ALU.mult).then_inc(out_taken, 1)
                            dve.drain()
                            nc.vector.tensor_tensor(out[:], out[:], rows[:, 1, :], ALU.add)
                            dve.drain()
                            x_tile = C.x[:, b * QT + t, :]
                            nc.vector.tensor_tensor(x_tile, x_tile, out[:], ALU.add)
                            dve.drain()

            @block.scalar
            def _(act):
                act.wait_ge(w_turned, 1)
                nc.scalar.activation(w1T[:, 0, :], ps_w[0][:], ACT.Copy).then_inc(w_copied, 1)
                act.wait_ge(w_turned, 2)
                nc.scalar.activation(w1T[:, 1, :], ps_w[0][:], ACT.Copy).then_inc(w_copied, 1)
                for i in range(2):
                    act.wait_ge(w_turned, 3 + i)
                    nc.scalar.activation(w2T[:, 4 * i:4 * i + 4, :].rearrange("p c d -> p (c d)"), ps_w[0][:],
                                         ACT.Copy).then_inc(w_copied, 1)
                act.wait_ge(n_scaled, 1)
                for c in range(DK):
                    with act.Fori(0, B // 2) as pair:
                        for u in range(2):
                            b = pair * 2 + u
                            act.wait_ge(n_ready, pair * 2 + c * B)
                            nc.scalar.activation(relu_n[:, u, :], C.nT[:, c, batch_cols(b)], ACT.Relu,
                                                 scale=r_in[:, 0:1]).then_inc(relu_ready, 1)
                act.wait_ge(scales_ready, 1)
                with act.Fori(0, B) as b:
                    for f in range(FK):
                        act.wait_ge(hid2_ready, b * FK + f + 1)
                        if f >= 2:
                            act.wait_ge(hq_ready, b * FK + f - 1)
                        else:
                            act.wait_ge(hq_ready, b * FK)
                        nc.scalar.activation(relu_h[:, f % 2, :], ps_h[f % 4][:], ACT.Relu, scale=q_scale[:, f:f + 1],
                                             bias=q_bias[:, f:f + 1]).then_inc(relu2_ready, 1)

            @block.tensor
            def _(pe):
                pe.wait_ge(w_ready, 1)
                for c in range(DK):
                    if c:
                        pe.wait_ge(w_copied, c)
                    for f in range(FK):
                        ins = nc.tensor.transpose(ps_w[0][:, f * P:(f + 1) * P], w1q[:, f, c * P:(c + 1) * P], ident16[:])
                    ins.then_inc(w_turned, 1)
                for i in range(2):
                    pe.wait_ge(w_copied, 2 + i)
                    for f in range(4):
                        for c in range(DK):
                            ins = nc.tensor.transpose(ps_w[0][:, f * D + c * P:f * D + (c + 1) * P],
                                                      w2q[:, c, (4 * i + f) * P:(4 * i + f + 1) * P], ident16[:])
                    ins.then_inc(w_turned, 1)
                pe.wait_ge(w_copied, 4)
                pe.wait_ge(n_ready, DK * B)

                def hidden(b, f, ready):
                    for c in range(DK):
                        ins = nc.tensor.matmul(ps_h[f % 4][:], w1T[:, c, f * P:(f + 1) * P], nq[:, c, batch_cols(b)],
                                               start=(c == 0), stop=(c == DK - 1))
                    ins.then_inc(ready, 1)

                with pe.Fori(0, B) as b:
                    for f in range(FK):
                        if f >= 4:
                            pe.wait_ge(hid_maxed, b * FK + f - 3)
                        else:
                            pe.wait_ge(hid_maxed, b * FK)
                        hidden(b, f, hid_ready)
                pe.wait_ge(diag_ready, 1)
                for a in range(2):
                    for c in range(DK):
                        ins = nc.tensor.matmul(ps_r[0][:, a * D + c * P:a * D + (c + 1) * P], C.ones[:], diag[:, a, c, :],
                                               start=True, stop=True)
                ins.then_inc(rows_ready, 1)
                with pe.Fori(0, B // 2) as pair:
                    for u in range(2):
                        b = pair * 2 + u
                        for f in range(FK):
                            if f >= 4:
                                pe.wait_ge(relu2_ready, b * FK + f - 3)
                            else:
                                pe.wait_ge(relu2_ready, b * FK)
                                pe.wait_ge(hid_maxed, B * FK)
                            hidden(b, f, hid2_ready)
                        for t in range(QT):
                            pe.wait_ge(hq_ready, (b + 1) * FK)
                            pe.wait_ge(out_taken, b * QT + max(t - 1, 0))
                            for f in range(FK):
                                ins = nc.tensor.matmul(ps_o[t % 2][:, :D], hq[u][:, f, t * P:(t + 1) * P], w2T[:, f, :],
                                                       start=(f == 0), stop=(f == FK - 1))
                            ins.then_inc(out_ready, 1)
    C.end_stage()




def deformable_stage(nc, C, w):
    HD, ROWS = D // H, S + 1
    N = H * NK
    HALF = H // 2
    NH = HALF * NK
    PAIR = 4 * HD
    with ExitStack() as ctx:
        sb, psum = stage_tensors(nc, ctx, C.n)
        table = [nc.dram_tensor(f"kv_table{u}", [H * ROWS, PAIR], F32, kind="Internal").ap() for u in range(2)]
        wkv, wq, wo = sb("w_kv", [P, DK, 2 * D]), sb("w_q", [P, DK, D]), sb("w_o", [P, DK, D])
        woff = sb("w_off", [P, DK, N])
        bkv, bq, bo = sb("b_kv", [P, 2 * D]), sb("b_q", [P, D]), sb("b_o", [P, D])
        bq_col, boff = sb("b_q_col", [P, DK]), sb("b_off", [P, N])
        shift, row = sb("shift", [P, N]), sb("row", [P, N])
        mask_in, unmasked = sb("mask_in", [P, B, QT], I32), sb("unmasked", [P, B, QT])
        places = sb("places", [P, QT])
        length, inv_length, neg_length = sb("length", [P, B]), sb("inv_length", [P, B]), sb("neg_length", [P, B])
        n_chunk, kv_chunk = sb("n_chunk", [P, DK, S]), sb("kv_chunk", [P, DK, S])
        qT = sb("q_T", [P, DK, S])
        kv = [sb(f"kv{u}", [P, QT, 2 * D]) for u in range(2)]
        q = [sb(f"q{u}", [P, QT, D]) for u in range(2)]
        pos, whole, over = sb("pos", [P, QT, N]), sb("whole", [P, QT, N]), sb("over", [P, QT, N])
        w_hi = [sb(f"w_hi{u}", [P, QT, N]) for u in range(2)]
        w_lo = [sb(f"w_lo{u}", [P, QT, N]) for u in range(2)]
        index = sb("index", [P, QT, N], U32)
        index_tile = [sb(f"index_tile{i}", [P, N], U32) for i in range(2)]
        got = [sb(f"gathered{i}", [P, NH, PAIR]) for i in range(2)]
        lo, hi = sb("lo", [P, NH, 2 * HD]), sb("hi", [P, NH, 2 * HD])
        prod = sb("prod", [P, NH, HD])
        score, top = sb("score", [P, HALF, NK]), sb("top", [P, HALF])
        zeros = sb("zeros", [H, PAIR])
        heads, headsT = sb("heads_out", [P, QT, D]), sb("heads_out_T", [P, DK, S])
        added = sb("added", [P, D])
        ps_kv, ps_q, ps_qT = psum("ps_kv", 2), psum("ps_q", 2), psum("ps_qT", 2)
        ps_off, ps_o = psum("ps_off", 1), psum("ps_out", 1)
        loaded, zeroed, staged = C.sem("loaded"), C.sem("zeroed"), C.sem("staged")
        gathers_begun = C.sem("gathers_begun")
        parts_ready, length_ready = C.sem("parts_ready"), C.sem("length_ready")
        places_ready, borders = C.sem("places_ready"), C.sem("borders")
        kv_ready, kv_taken, q_ready, q_taken = C.sem("kv_ready"), C.sem("kv_taken"), C.sem("q_ready"), C.sem("q_taken")
        qT_ready, qT_taken, off_ready, off_taken = C.sem("qT_ready"), C.sem("qT_taken"), C.sem("off_ready"), C.sem("off_taken")
        table_written = [C.sem(f"table_written{u}") for u in range(2)]
        index_ready, index_used = C.sem("index_ready"), C.sem("index_used")
        gathered = [C.sem(f"gathered{i}") for i in range(2)]
        got_used = [C.sem(f"got_used{i}") for i in range(2)]
        shifted, exp_ready, sampled = C.sem("shifted"), C.sem("exp_ready"), C.sem("sampled")
        headsT_turned, headsT_copied = C.sem("headsT_turned"), C.sem("headsT_copied")
        out_ready, out_taken = C.sem("out_ready"), C.sem("out_taken")
        loads = [(wkv, w["wkv"].rearrange("(c p) n -> p c n", p=P)), (wq, w["wq"].rearrange("(c p) n -> p c n", p=P)),
                 (wo, w["wo"].rearrange("(c p) n -> p c n", p=P)), (woff, w["woff"].rearrange("(c p) n -> p c n", p=P)),
                 (bq_col, w["bq_col"]), (mask_in, w["mask"])]
        loads += [(to, w[n].partition_broadcast(P)) for to, n in (
            (bkv, "bkv"), (bq, "bq"), (bo, "bo"), (boff, "boff"), (shift, "shift"), (row, "row"))]

        def table_of(u, ahead):
            rows = table[u].rearrange("(h r) c -> r h c", h=H)
            return rows[1:, :, :2 * HD] if ahead == 0 else rows[:S, :, 2 * HD:]

        with nc.Block() as block:
            @block.sync
            def _(sp):
                for to, of in loads:
                    sp.dma_start(to[:], of).then_inc(loaded, 16)
                sp.wait_ge(zeroed, 1)
                for u in range(2):
                    rows = table[u].rearrange("(h r) c -> h r c", h=H)
                    sp.dma_start(rows[:, 0, :2 * HD], zeros[:, :2 * HD]).then_inc(borders, 16)
                    sp.dma_start(rows[:, S, 2 * HD:], zeros[:, 2 * HD:]).then_inc(borders, 16)
                with sp.Fori(0, B // 2) as pair:
                    for u in range(2):
                        b = pair * 2 + u
                        sp.wait_ge(kv_taken, (b + 1) * QT)
                        for t in range(QT):
                            for ahead in range(2):
                                sp.dma_start(table_of(u, ahead)[t * P:(t + 1) * P],
                                             kv[u][:, t, :].rearrange("p (h c) -> p h c", h=H)).then_inc(table_written[u], 16)
                sp.wait_ge(table_written[0], B // 2 * 32 * QT)
                sp.wait_ge(table_written[1], B // 2 * 32 * QT)

            @block.gpsimd
            def _(pool):
                nc.gpsimd.memset(zeros[:], 0.0).then_inc(zeroed, 1)
                nc.gpsimd.iota(places[:], [[P, QT]], base=0, channel_multiplier=1,
                               allow_small_or_imprecise_dtypes=True).then_inc(places_ready, 1)
                with pool.Fori(0, B // 2) as pair:
                    for u in range(2):
                        with pool.Fori(0, QT // 2) as tpair:
                            for v in range(2):
                                tile = (pair * 2 + u) * QT + tpair * 2 + v
                                pool.wait_ge(table_written[u], (pair + 1) * (32 * QT))
                                pool.wait_ge(index_ready, tile + 1)
                                for half in range(2):
                                    pool.wait_ge(got_used[half], tile)
                                    pool.wait_ge(borders, 64)
                                    pool.sem_inc(gathers_begun, 1)
                                    for c in range(NH):
                                        n = half * NH + c
                                        nc.gpsimd.indirect_dma_start(
                                            got[half][:, c, :], None, table[u],
                                            bass.IndirectOffsetOnAxis(ap=index_tile[v][:, n:n + 1], axis=0)) \
                                            .then_inc(gathered[half], 16)

            @block.scalar
            def _(act):
                act.wait_ge(loaded, 16 * len(loads))
                with act.Fori(0, B) as b:
                    act.wait_ge(q_ready, b * QT)
                    act.wait_ge(kv_ready, b * QT)
                    nc.scalar.activation(kv_chunk[:], C.ctxT[:, :, batch_cols(b)], ACT.Copy)
                    nc.scalar.activation(n_chunk[:], C.nT[:, :, batch_cols(b)], ACT.Copy)
                    act.drain().then_inc(staged, 1)
                    for c in range(DK):
                        act.wait_ge(qT_ready, b * DK + c + 1)
                        nc.scalar.activation(qT[:, c, :], ps_qT[c][:], ACT.Identity, bias=bq_col[:, c:c + 1]) \
                            .then_inc(qT_taken, 1)
                    for half in range(2 * QT):
                        act.wait_ge(shifted, b * (2 * QT) + half + 1)
                        nc.scalar.activation(score[:], score[:], ACT.Exp).then_inc(exp_ready, 1)

            @block.tensor
            def _(pe):
                pe.wait_ge(loaded, 16 * len(loads))
                pe.wait_ge(parts_ready, 1)
                nc.tensor.matmul(ps_off[0][:, :B], C.ones[:], length[:], start=True, stop=True).then_inc(length_ready, 1)
                pe.wait_ge(parts_ready, 2)
                with pe.Fori(0, B) as b:
                    for c in range(DK):
                        pe.wait_ge(staged, b + 1)
                        pe.wait_ge(qT_taken, b * DK)
                        for i in range(DK):
                            ins = nc.tensor.matmul(ps_qT[c][:], wq[:, i, c * P:(c + 1) * P], n_chunk[:, i, :],
                                                   start=(i == 0), stop=(i == DK - 1))
                        ins.then_inc(qT_ready, 1)
                    for t in range(QT):
                        if t >= 2:
                            pe.wait_ge(kv_taken, b * QT + t - 1)
                            pe.wait_ge(q_taken, b * QT + t - 1)
                        else:
                            pe.wait_ge(kv_taken, b * QT)
                            pe.wait_ge(q_taken, b * QT)
                        for i in range(DK):
                            ins = nc.tensor.matmul(ps_kv[t % 2][:], kv_chunk[:, i, t * P:(t + 1) * P], wkv[:, i, :],
                                                   start=(i == 0), stop=(i == DK - 1))
                        ins.then_inc(kv_ready, 1)
                        for i in range(DK):
                            ins = nc.tensor.matmul(ps_q[t % 2][:, :D], n_chunk[:, i, t * P:(t + 1) * P], wq[:, i, :],
                                                   start=(i == 0), stop=(i == DK - 1))
                        ins.then_inc(q_ready, 1)
                    pe.wait_ge(qT_taken, (b + 1) * DK)
                    for t in range(QT):
                        for i in range(DK):
                            ins = nc.tensor.matmul(ps_off[0][:, t * N:(t + 1) * N], qT[:, i, t * P:(t + 1) * P],
                                                   woff[:, i, :], start=(i == 0), stop=(i == DK - 1))
                    ins.then_inc(off_ready, 1)
                    for c in range(DK):
                        pe.wait_ge(sampled, b + 1)
                        for t in range(QT):
                            ins = nc.tensor.transpose(ps_qT[c][:, t * P:(t + 1) * P], heads[:, t, c * P:(c + 1) * P],
                                                      C.ident[:])
                        ins.then_inc(headsT_turned, 1)
                    for t in range(QT):
                        pe.wait_ge(headsT_copied, (b + 1) * DK)
                        pe.wait_ge(out_taken, b * QT + t)
                        for c in range(DK):
                            ins = nc.tensor.matmul(ps_o[0][:, :D], headsT[:, c, t * P:(t + 1) * P], wo[:, c, :],
                                                   start=(c == 0), stop=(c == DK - 1))
                        ins.then_inc(out_ready, 1)

            @block.vector
            def _(dve):
                dve.wait_ge(loaded, 16 * len(loads))
                dve.wait_ge(places_ready, 1)
                nc.vector.tensor_scalar(unmasked[:], mask_in[:], -1.0, 1.0, ALU.mult, ALU.add)
                dve.drain()
                nc.vector.tensor_reduce(length[:], unmasked[:], AX_X, ALU.add)
                dve.drain().then_inc(parts_ready, 1)
                dve.wait_ge(length_ready, 1)
                nc.vector.tensor_scalar(length[:], ps_off[0][:, :B], -1.0, None, ALU.add)
                dve.drain()
                nc.vector.reciprocal(inv_length[:], length[:])
                nc.vector.tensor_scalar(neg_length[:], length[:], -1.0, None, ALU.mult)
                dve.drain().then_inc(parts_ready, 1)
                with dve.Fori(0, B // 2) as pair:
                    for u in range(2):
                        b = pair * 2 + u
                        now = bass.ds(b, 1)
                        dve.wait_ge(table_written[u], pair * (32 * QT))
                        for t in range(QT):
                            dve.wait_ge(kv_ready, b * QT + t + 1)
                            nc.vector.tensor_tensor(kv[u][:, t, :], ps_kv[t % 2][:], bkv[:], ALU.add).then_inc(kv_taken, 1)
                            dve.wait_ge(q_ready, b * QT + t + 1)
                            nc.vector.tensor_tensor(q[u][:, t, :], ps_q[t % 2][:, :D], bq[:], ALU.add).then_inc(q_taken, 1)
                        dve.drain()
                        nc.vector.tensor_scalar(q[u][:], q[u][:], float(HD) ** -0.5, None, ALU.mult)
                        dve.wait_ge(off_ready, b + 1)
                        by_tile = lambda r: r[:].unsqueeze(1).broadcast_to([P, QT, N])
                        nc.vector.tensor_tensor(pos[:], ps_off[0][:, :QT * N].rearrange("p (t n) -> p t n", t=QT),
                                                by_tile(boff), ALU.add).then_inc(off_taken, 1)
                        dve.drain()
                        nc.vector.tensor_tensor(pos[:], pos[:], by_tile(shift), ALU.add)
                        dve.drain()
                        nc.vector.tensor_tensor(pos[:], pos[:], places[:].unsqueeze(2).broadcast_to([P, QT, N]), ALU.add)
                        dve.drain()
                        nc.vector.tensor_scalar(whole[:], pos[:], inv_length[:, now], ROUND, ALU.mult, ALU.add)
                        dve.drain()
                        nc.vector.tensor_scalar(whole[:], whole[:], -ROUND, neg_length[:, now], ALU.add, ALU.mult)
                        dve.drain()
                        nc.vector.tensor_tensor(pos[:], pos[:], whole[:], ALU.add)
                        dve.drain()
                        nc.vector.tensor_scalar(over[:], pos[:], 0.0, length[:, now], ALU.is_lt, ALU.mult)
                        dve.drain()
                        nc.vector.tensor_tensor(pos[:], pos[:], over[:], ALU.add)
                        dve.drain()
                        nc.vector.tensor_scalar(pos[:], pos[:], S / (S - 1.0), -0.5, ALU.mult, ALU.add)
                        dve.drain()
                        nc.vector.tensor_scalar(whole[:], pos[:], ROUND, -ROUND, ALU.add, ALU.add)
                        dve.drain()
                        nc.vector.tensor_tensor(over[:], whole[:], pos[:], ALU.is_gt)
                        dve.drain()
                        nc.vector.tensor_tensor(whole[:], whole[:], over[:], ALU.subtract)
                        dve.drain()
                        nc.vector.tensor_tensor(pos[:], pos[:], whole[:], ALU.subtract)
                        nc.vector.tensor_scalar(whole[:], whole[:], -1.0, S - 1.0, ALU.max, ALU.min)
                        dve.drain()
                        nc.vector.tensor_scalar(w_hi[u][:], pos[:], 0.5, None, ALU.mult)
                        nc.vector.tensor_scalar(w_lo[u][:], pos[:], -0.5, 0.5, ALU.mult, ALU.add)
                        nc.vector.tensor_tensor(index[:], whole[:], by_tile(row), ALU.add)
                        dve.drain()
                        for t in range(2):
                            nc.vector.tensor_copy(index_tile[t][:], index[:, t, :]).then_inc(index_ready, 1)
                        for t in range(QT):
                            tile = b * QT + t
                            for half in range(2):
                                own = slice(half * NH, (half + 1) * NH)
                                dve.wait_ge(gathered[half], (tile + 1) * (16 * NH))
                                pairs = got[half][:]
                                by = lambda m: m[u][:, t, own].unsqueeze(2).broadcast_to([P, NH, 2 * HD])
                                nc.vector.tensor_tensor(lo[:], pairs[:, :, :2 * HD], by(w_lo), ALU.mult)
                                nc.vector.tensor_tensor(hi[:], pairs[:, :, 2 * HD:], by(w_hi), ALU.mult)
                                dve.drain().then_inc(got_used[half], 1)
                                nc.vector.tensor_tensor(lo[:], lo[:], hi[:], ALU.add)
                                dve.drain()
                                by_head = lo[:].rearrange("p (h k) c -> p h k c", h=HALF)
                                prods = prod[:].rearrange("p (h k) c -> p h k c", h=HALF)
                                query = q[u][:, t, half * (D // 2):(half + 1) * (D // 2)] \
                                    .rearrange("p (h c) -> p h c", h=HALF).unsqueeze(2).broadcast_to([P, HALF, NK, HD])
                                nc.vector.tensor_tensor(prods, by_head[:, :, :, :HD], query, ALU.mult)
                                dve.drain()
                                nc.vector.tensor_reduce(score[:], prods, AX_X, ALU.add)
                                dve.drain()
                                per_head = top[:].unsqueeze(2).broadcast_to([P, HALF, NK])
                                nc.vector.tensor_reduce(top[:], score[:], AX_X, ALU.max)
                                dve.drain()
                                nc.vector.tensor_tensor(score[:], score[:], per_head, ALU.subtract)
                                dve.drain().then_inc(shifted, 1)
                                dve.wait_ge(exp_ready, tile * 2 + half + 1)
                                nc.vector.tensor_reduce(top[:], score[:], AX_X, ALU.add)
                                dve.drain()
                                nc.vector.reciprocal(top[:], top[:])
                                dve.drain()
                                nc.vector.tensor_tensor(score[:], score[:], per_head, ALU.mult)
                                dve.drain()
                                nc.vector.tensor_tensor(prods, by_head[:, :, :, HD:],
                                                        score[:].unsqueeze(3).broadcast_to([P, HALF, NK, HD]), ALU.mult)
                                dve.drain()
                                nc.vector.tensor_reduce(
                                    heads[:, t, half * (D // 2):(half + 1) * (D // 2)].rearrange("p (h c) -> p h c", h=HALF),
                                    prod[:].rearrange("p (h k) c -> p h c k", h=HALF), AX_X, ALU.add)
                                dve.drain()
                            if t + 2 < QT:
                                nc.vector.tensor_copy(index_tile[t % 2][:], index[:, t + 2, :]).then_inc(index_ready, 1)
                        dve.sem_inc(sampled, 1)
                        for c in range(DK):
                            dve.wait_ge(headsT_turned, b * DK + c + 1)
                            nc.vector.tensor_copy(headsT[:, c, :], ps_qT[c][:]).then_inc(headsT_copied, 1)
                        for t in range(QT):
                            dve.wait_ge(out_ready, b * QT + t + 1)
                            nc.vector.tensor_tensor(added[:], ps_o[0][:, :D], bo[:], ALU.add).then_inc(out_taken, 1)
                            dve.drain()
                            x_tile = C.x[:, b * QT + t, :]
                            nc.vector.tensor_tensor(x_tile, x_tile, added[:], ALU.add)
                            dve.drain()
    C.end_stage()




def stacked_attention_stage(nc, C, w, cross=True, causal=False, rope=False, biased=False, masked=False, res=None):
    res = C.x if res is None else res
    uid = C.n
    HD = D // H
    HH, HQ = H // DK, H // DK // 2
    U = HQ * QT
    BLOCKS = {"q": ((0, 0, 3, True), (3, 1, 2, True), (5, 2, 1, True)),
              "k": ((0, 0, 3, False), (3, 0, 2, False), (5, 0, 1, False))}
    MAX_PARTS = 2
    MAX_ROW = 6 * HD + int(masked)
    ROWS = MAX_ROW + MAX_PARTS
    VW = SLOT
    scale = float(HD) ** -0.5
    kvT = C.ctxT if cross else C.nT
    USES0, USES1 = (3, 2) if rope else (2, 1)
    STACKS = 6 + int(masked)

    with ExitStack() as ctx:
        sb, psum = stage_tensors(nc, ctx, uid)
        names = ["q", "k", "v"] + (["q_swap", "k_swap"] if rope else [])
        W = {m: sb(f"w_{m}", [P, DK, D]) for m in names}
        wo = sb("w_o", [P, DK, D])
        kv_chunk = sb("kv_chunk", [P, DK, S])
        full = {m: sb(f"{m}_full", [P, S]) for m in "qk"}
        rest = sb("rest", [P, S])
        parts = {m: sb(f"{m}_parts", [P, 3, S], BF16) for m in "qk"}
        stack = {m: [sb(f"{m}_stack{c}", [P, HH, S], BF16) for c in range(DK)] for m in "qk"}
        v = [sb(f"v{c}", [P, QT, HH, VW]) for c in range(DK)]
        parts_dram = {m: [nc.dram_tensor(f"{m}_parts_dram{c}_{uid}", [3, HD, HH, S], BF16, kind="Internal").ap()
                          for c in range(DK)] for m in "qk"}
        neg_max = [sb(f"neg_max{x}", [P, P]) for x in range(2)]
        max_parts = [sb(f"max_parts{x}", [U, MAX_PARTS, P], BF16) for x in range(2)]
        exps = [sb(f"exps{i}", [P, HQ, S]) for i in range(2)]
        outs = sb("outputs", [P, S])
        recip = sb("recip", [P, QT, HQ])
        heads, headsT = sb("heads_out", [P, QT, D]), sb("heads_out_T", [P, DK, S])
        added = sb("added", [P, D])
        if rope:
            cos, sin = sb("cos", [P, S]), sb("sin", [P, S])
            turn = sb("turn", [P, S])
        if biased:
            bq, bk = sb("b_q", [P, DK]), sb("b_k", [P, DK])
            bv, bo = sb("b_v", [P, D]), sb("b_o", [P, D])
        if masked:
            mask_in = sb("mask_in", [1, B * S], mybir.dt.uint8)
            mask = sb("mask_bias", [1, B * S], BF16)
        if causal:
            future = sb("future", [P, 2, P])
            future16, ident16 = sb("future16", [P, 2, P], BF16), sb("ident16", [P, P], BF16)
        ps_p, ps_s, ps_t = psum("ps_proj", 2), psum("ps_scores", 2), psum("ps_scores_T", 2)
        ps_m, ps_o = psum("ps_max", 1)[0], psum("ps_out", 1)[0]

        weights, prepared, cleared = C.sem("weights"), C.sem("prepared"), C.sem("cleared")
        kv_staged = C.sem("kv_staged")
        q_projected, k_projected, v_projected = C.sem("q_projected"), C.sem("k_projected"), C.sem("v_projected")
        taken0, taken1, v_ready = C.sem("bank0_taken"), C.sem("bank1_taken"), C.sem("v_ready")
        full_ready, q_split, k_split = C.sem("full_ready"), C.sem("q_split"), C.sem("k_split")
        written = [C.sem(f"parts_written{c}") for c in range(DK)]
        stacked = [C.sem(f"stacked{g}") for g in range(4)]
        scored, maxed, max_turned, max_split = C.sem("scored"), C.sem("maxed"), C.sem("max_turned"), C.sem("max_split")
        max_stacked = [C.sem(f"max_stacked{x}") for x in range(2)]
        scored_T, exp_done, roped = C.sem("scored_T"), C.sem("exp_done"), C.sem("roped")
        summed, copied = C.sem("summed"), C.sem("copied")
        outs_turned, normalised = C.sem("outs_turned"), C.sem("normalised")
        turned, headsT_ready, out_ready = C.sem("turned"), C.sem("headsT_ready"), C.sem("out_ready")

        loads = [(W[m], w[m].rearrange("(c p) n -> p c n", p=P)) for m in names]
        loads += [(wo, w["o"].rearrange("(c p) n -> p c n", p=P))]
        if rope:
            loads += [(cos, w["cos"]), (sin, w["sin"])]
        if biased:
            loads += [(bq, w["bq"]), (bk, w["bk"]),
                      (bv, w["bv"].partition_broadcast(P)), (bo, w["bo"].partition_broadcast(P))]
        if masked:
            loads += [(mask_in, w["mask"])]
        if causal:
            loads += [(future, w["future"])]

        def keys(t):
            return (t + 1) * P if causal else S

        def first_query(t):
            return t * P if causal else 0

        def turns(b, g):
            return min(b * 4 + g + 3, B * 4) if isinstance(b, int) else b * 4 + g + 3

        def steps(eng, project, values, quad, output):
            for c in range(DK):
                project(0, c, USES0 * c, USES1 * c)
                values(0, c, USES0 * c)
            quad(None, (0, 0))
            quad(None, (0, 1))

            def batch(b, last):
                more = 0 if last else 1
                per0, per1 = DK * USES0 + 3, DK * USES1 + 3
                at0, at1 = DK * USES0 + b * per0, DK * USES1 + b * per1
                for c in range(DK):
                    if more:
                        project(b + 1, c, at0 + c * USES0, at1 + c * USES1)
                    for x in range(2):
                        g = 2 * c + x
                        ahead = (b, g + 2) if g < 2 else ((b + 1, g - 2) if more else None)
                        quad((b, g), ahead)
                    if more:
                        values(b + 1, c, at0 + c * USES0)
                output(b, at0 + more * DK * USES0, at1 + more * DK * USES1)

            with eng.Fori(0, B - 1) as b:
                batch(b, False)
            batch(B - 1, True)

        with nc.Block() as block:
            @block.sync
            def _(sp):
                for to, of in loads:
                    sp.dma_start(to[:], of).then_inc(weights, 16)
                sp.wait_ge(cleared, 10)
                if masked:
                    sp.wait_ge(prepared, 1)

                def project(b, c, at0, at1):
                    before = sp.to_reg(b * (16 * STACKS))
                    halves = sp.to_reg(b * DK + c + 1)
                    sp.wait_ge(q_split, halves)
                    if not (isinstance(b, int) and b == 0):
                        sp.wait_ge(stacked[2 * c], before)
                        sp.wait_ge(stacked[2 * c + 1], before)
                    for m in "qk":
                        if m == "k":
                            sp.wait_ge(k_split, halves)
                        for i in range(3):
                            sp.dma_start(parts_dram[m][c][i].rearrange("d h t -> h d t"), parts[m][:, i, :]) \
                                .then_inc(written[c], 16)

                def stack_quad(b, g, writes):
                    c, x = g // 2, g % 2
                    own = slice(x * HQ, (x + 1) * HQ)
                    sp.wait_ge(written[c], writes)
                    for m in "qk":
                        for row, part, n, over in BLOCKS[m]:
                            rows = stack[m][c][row * HD:(row + n) * HD, own, :]
                            of = parts_dram[m][c][part:part + n if not over else part + 1, :, own, :] \
                                .rearrange("i d h t -> i d (h t)")
                            if over:
                                of = of.broadcast_to([n, HD, HQ * S])
                            sp.dma_start(rows, of).then_inc(stacked[g], 16)
                    if masked:
                        sp.dma_start(stack["k"][c][6 * HD:6 * HD + 1, own, :],
                                     mask[:, batch_cols(b)].unsqueeze(1).broadcast_to([1, HQ, S])).then_inc(stacked[g], 16)

                def quad(now, ahead):
                    if now is not None:
                        done = sp.snap((now[0] * 4 + now[1] + 1) * U)
                        writes = sp.snap((now[0] + 2) * 96)
                    if ahead is not None:
                        quads = sp.snap(ahead[0] * 4 + ahead[1] + 1)
                    if now is None:
                        stack_quad(0, ahead[1], 96)
                        stack_quad(0, ahead[1] + 2, 96)
                    elif not (isinstance(now[0], int) and now[0] == B - 1):
                        sp.wait_ge(scored_T, done)
                        stack_quad(now[0] + 1, now[1], writes)
                    if ahead is not None:
                        c, x = ahead[1] // 2, ahead[1] % 2
                        sp.wait_ge(max_split, quads)
                        for i in range(MAX_PARTS):
                            sp.dma_start(stack["q"][c][MAX_ROW + i:MAX_ROW + i + 1, x * HQ:(x + 1) * HQ, :],
                                         max_parts[x][:, i, :]).then_inc(max_stacked[x], 16)

                none = lambda *a: None
                steps(sp, project, none, quad, none)

            @block.gpsimd
            def _(pool):
                pool.wait_ge(weights, 16 * len(loads))

                def project(b, c, at0, at1):
                    if c == 0:
                        pool.wait_ge(v_projected, b * DK)
                        nc.gpsimd.tensor_copy(kv_chunk[:], kvT[:, :, batch_cols(b)]).then_inc(kv_staged, 1)
                    n = b * DK + c
                    for m, split in (("q", q_split), ("k", k_split)):
                        pool.wait_ge(full_ready, 2 * n + (1 if m == "q" else 2))
                        nc.gpsimd.tensor_tensor(rest[:], full[m][:], parts[m][:, 0, :], ALU.subtract)
                        pool.drain()
                        nc.gpsimd.tensor_copy(parts[m][:, 1, :], rest[:])
                        pool.drain()
                        nc.gpsimd.tensor_tensor(parts[m][:, 2, :], rest[:], parts[m][:, 1, :], ALU.subtract)
                        pool.drain().then_inc(split, 1)

                none = lambda *a: None
                steps(pool, project, none, none, none)

            @block.tensor
            def _(pe):
                pe.wait_ge(weights, 16 * len(loads))
                pe.wait_ge(prepared, 1)
                pe.wait_ge(cleared, 10)
                pe.sem_inc(summed, 1)

                def matmuls(bank, m, c, rhs, done):
                    for i in range(DK):
                        ins = nc.tensor.matmul(bank[:], W[m][:, i, c * P:(c + 1) * P], rhs(i), start=(i == 0),
                                               stop=(i == DK - 1))
                    if done is not None:
                        ins.then_inc(done, 1)

                def project(b, c, at0, at1):
                    of_n = lambda i: C.nT[:, i, batch_cols(b)]
                    of_kv = lambda i: kvT[:, i, batch_cols(b)]
                    pe.wait_ge(taken0, at0)
                    if rope:
                        pe.wait_ge(taken1, at1)
                        matmuls(ps_p[0], "q", c, of_n, None)
                        matmuls(ps_p[1], "q_swap", c, of_n, q_projected)
                        pe.wait_ge(taken0, at0 + 1)
                        pe.wait_ge(taken1, at1 + 1)
                        matmuls(ps_p[0], "k", c, of_kv, None)
                        matmuls(ps_p[1], "k_swap", c, of_kv, k_projected)
                    else:
                        matmuls(ps_p[0], "q", c, of_n, q_projected)
                        pe.wait_ge(taken1, at1)
                        matmuls(ps_p[1], "k", c, of_kv, k_projected)

                def values(b, c, at0):
                    pe.wait_ge(taken0, at0 + USES0 - 1)
                    pe.wait_ge(kv_staged, b + 1)
                    for t in range(QT):
                        for i in range(DK):
                            ins = nc.tensor.matmul(ps_p[0][:, t * P:(t + 1) * P], kv_chunk[:, i, t * P:(t + 1) * P],
                                                   W["v"][:, i, c * P:(c + 1) * P], start=(i == 0), stop=(i == DK - 1))
                    ins.then_inc(v_projected, 1)

                def scores(b, g, u):
                    h, t = u // QT, u % QT
                    c, hh = g // 2, (g % 2) * HQ + h
                    pe.wait_ge(maxed, (b * 4 + g) * U + u)
                    if u == 0:
                        pe.wait_ge(stacked[g], (b + 1) * (16 * STACKS))
                    ins = nc.tensor.matmul(ps_s[u % 2][:, :keys(t)], stack["q"][c][:MAX_ROW, hh, t * P:(t + 1) * P],
                                           stack["k"][c][:MAX_ROW, hh, :keys(t)], start=True, stop=not causal)
                    if causal:
                        ins = nc.tensor.matmul(ps_s[u % 2][:, t * P:keys(t)], ident16[:], future16[:, 0, :],
                                               start=False, stop=True)
                    ins.then_inc(scored, 1)

                def scores_T(b, g, u):
                    i, h = u // HQ, u % HQ
                    c, x, hh = g // 2, g % 2, (g % 2) * HQ + h
                    pe.wait_ge(exp_done, (b * 4 + g) * U + u)
                    if u == 0:
                        pe.wait_ge(max_stacked[x], (b * DK + c + 1) * (16 * MAX_PARTS))
                    q0 = first_query(i)
                    ins = nc.tensor.matmul(ps_t[u % 2][:, q0:], stack["k"][c][:ROWS, hh, i * P:(i + 1) * P],
                                           stack["q"][c][:ROWS, hh, q0:], start=True, stop=not causal)
                    if causal:
                        ins = nc.tensor.matmul(ps_t[u % 2][:, q0:q0 + P], ident16[:], future16[:, 1, :],
                                               start=False, stop=True)
                    ins.then_inc(scored_T, 1)

                def sums(b, g, i):
                    c, m = g // 2, b * 4 + g
                    if i == 0:
                        pe.wait_ge(copied, m)
                        pe.wait_ge(v_ready, b * DK + c + 1)
                    pe.wait_ge(exp_done, m * U + (i + 1) * HQ + 1)
                    q0 = first_query(i)
                    for h in range(HQ):
                        ins = nc.tensor.matmul(ps_o[h * VW:(h + 1) * VW, q0:], v[c][:, i, (g % 2) * HQ + h, :],
                                               exps[i % 2][:, h, q0:], start=(i == 0), stop=(i == QT - 1))
                    ins.then_inc(summed, 1)

                def turn_outputs(b, g):
                    m = b * 4 + g
                    pe.wait_ge(copied, m + 1)
                    pe.wait_ge(max_split, turns(b, g))
                    pe.wait_ge(normalised, m)
                    for t in range(QT):
                        ins = nc.tensor.transpose(ps_m[:, t * P:(t + 1) * P], outs[:, t * P:(t + 1) * P], C.ident[:])
                    ins.then_inc(outs_turned, 1)

                def quad(now, ahead):
                    for u in range(U):
                        if now is not None:
                            scores_T(*now, u)
                        if ahead is not None:
                            scores(*ahead, u)
                        if now is not None and u == HQ - 1 and now[1]:
                            turn_outputs(now[0], now[1] - 1)
                        if now is not None and u % HQ == 1 and u > HQ:
                            sums(*now, u // HQ - 1)
                    if ahead is not None:
                        m = ahead[0] * 4 + ahead[1]
                        pe.wait_ge(maxed, (m + 1) * U + 1)
                        if now is not None:
                            pe.wait_ge(normalised, now[0] * 4 + now[1])
                        pe.wait_ge(max_split, m)
                        nc.tensor.transpose(ps_m[:, :P], neg_max[ahead[1] % 2][:], C.ident[:]).then_inc(max_turned, 1)
                    if now is not None:
                        sums(*now, QT - 1)

                def output(b, at0, at1):
                    taken = (taken0, taken1)
                    turn_outputs(b, 3)
                    for c in range(DK):
                        pe.wait_ge(taken[c], (at0, at1)[c])
                        pe.wait_ge(normalised, (b + 1) * 4)
                        for t in range(QT):
                            ins = nc.tensor.transpose(ps_p[c][:, t * P:(t + 1) * P], heads[:, t, c * P:(c + 1) * P],
                                                      C.ident[:])
                        ins.then_inc(turned, 1)
                    for t in range(QT):
                        pe.wait_ge(headsT_ready, b + 1)
                        pe.wait_ge(taken[t % 2], (at0, at1)[t % 2] + 1 + t // 2)
                        for c in range(DK):
                            ins = nc.tensor.matmul(ps_p[t % 2][:, :D], headsT[:, c, t * P:(t + 1) * P], wo[:, c, :],
                                                   start=(c == 0), stop=(c == DK - 1))
                        ins.then_inc(out_ready, 1)

                none = lambda *a: None
                steps(pe, project, values, quad, output)

            @block.scalar
            def _(act):
                act.wait_ge(prepared, 1)
                act.sem_inc(exp_done, 1)

                def project(b, c, at0, at1):
                    n = b * DK + c
                    for i, (m, ready, by, bank, taken) in enumerate((("q", q_projected, scale, 0, taken0),
                                                                     ("k", k_projected, 1.0, 1, taken1))):
                        split = q_split if m == "q" else k_split
                        act.wait_ge(split, n)
                        if c or not (isinstance(b, int) and b == 0):
                            act.wait_ge(written[1 - c], (b + c) * 96)
                        if rope:
                            act.wait_ge(roped, 2 * n + i + 1)
                            nc.scalar.activation(parts[m][:, 0, :], full[m][:], ACT.Copy).then_inc(full_ready, 1)
                        else:
                            act.wait_ge(ready, n + 1)
                            args = dict(scale=by, bias=(bq if m == "q" else bk)[:, c:c + 1] if biased else 0.0)
                            nc.scalar.activation(full[m][:], ps_p[bank][:], ACT.Identity, **args)
                            nc.scalar.activation(parts[m][:, 0, :], ps_p[bank][:], ACT.Identity, **args).then_inc(taken, 1)
                            act.drain().then_inc(full_ready, 1)

                def copy_outputs(b, g):
                    act.wait_ge(summed, (b * 4 + g + 1) * QT + 1)
                    act.wait_ge(outs_turned, b * 4 + g)
                    nc.scalar.activation(outs[:], ps_o[:], ACT.Copy).then_inc(copied, 1)

                def quad(now, ahead):
                    if now is None:
                        return
                    b, g = now
                    m = b * 4 + g
                    for u in range(U):
                        i, h = u // HQ, u % HQ
                        act.wait_ge(scored_T, m * U + u + 1)
                        if h == 0:
                            act.wait_ge(summed, m * QT + i)
                        q0 = first_query(i)
                        nc.scalar.activation(exps[i % 2][:, h, q0:], ps_t[u % 2][:, q0:], ACT.Exp).then_inc(exp_done, 1)
                        if u == HQ - 1 and g:
                            copy_outputs(b, g - 1)

                def output(b, at0, at1):
                    copy_outputs(b, 3)
                    for c in range(DK):
                        act.wait_ge(turned, b * DK + c + 1)
                        nc.scalar.activation(headsT[:, c, :], ps_p[c][:], ACT.Copy).then_inc((taken0, taken1)[c], 1)
                    act.drain().then_inc(headsT_ready, 1)

                none = lambda *a: None
                steps(act, project, none, quad, output)

            @block.vector
            def _(dve):
                dve.wait_ge(weights, 16 * len(loads))
                if masked:
                    nc.vector.tensor_scalar(mask[:], mask_in[:], 1.0, -NEG, ALU.subtract, ALU.mult)
                if biased:
                    nc.vector.tensor_scalar(bq[:], bq[:], scale, None, ALU.mult)
                if causal:
                    nc.vector.tensor_copy(future16[:], future[:])
                    nc.vector.tensor_copy(ident16[:], C.ident[:])
                dve.drain().then_inc(prepared, 2)
                for c in range(DK):
                    for m in "qk":
                        nc.vector.memset(stack[m][c][6 * HD:6 * HD + 4], 1.0).then_inc(cleared, 1)
                    nc.vector.memset(v[c][:, :, :, HD + 1:], 0.0).then_inc(cleared, 1)
                    nc.vector.memset(v[c][:, :, :, HD:HD + 1], 1.0).then_inc(cleared, 1)
                    nc.vector.memset(neg_max[c][:], 0.0).then_inc(cleared, 1)
                dve.drain()
                dve.sem_inc(maxed, 1)

                def project(b, c, at0, at1):
                    if rope:
                        n = b * DK + c
                        for i, (m, ready, by) in enumerate((("q", q_projected, scale), ("k", k_projected, 1.0))):
                            dve.wait_ge(ready, n + 1)
                            dve.wait_ge(q_split if m == "q" else k_split, n)
                            nc.vector.scalar_tensor_tensor(out=full[m][:], in0=ps_p[0][:], scalar=by, in1=cos[:],
                                                           op0=ALU.mult, op1=ALU.mult).then_inc(taken0, 1)
                            nc.vector.scalar_tensor_tensor(out=turn[:], in0=ps_p[1][:], scalar=by, in1=sin[:],
                                                           op0=ALU.mult, op1=ALU.mult).then_inc(taken1, 1)
                            dve.drain()
                            nc.vector.tensor_tensor(full[m][:], full[m][:], turn[:], ALU.add).then_inc(roped, 1)
                            dve.drain()

                def values(b, c, at0):
                    dve.wait_ge(v_projected, b * DK + c + 1)
                    of = ps_p[0][:].rearrange("p (t h d) -> p t h d", t=QT, h=HH)
                    if biased:
                        by = bv[:, c * P:(c + 1) * P].rearrange("p (h d) -> p h d", h=HH).unsqueeze(1) \
                            .broadcast_to([P, QT, HH, HD])
                        nc.vector.tensor_tensor(v[c][:, :, :, :HD], of, by, ALU.add).then_inc(v_ready, 1)
                    else:
                        nc.vector.tensor_copy(v[c][:, :, :, :HD], of).then_inc(v_ready, 1)
                    dve.drain().then_inc(taken0, 1)

                def normalise(b, g):
                    dve.wait_ge(outs_turned, b * 4 + g + 1)
                    of = ps_m[:].rearrange("p (t h w) -> p t h w", h=HQ, t=QT)
                    nc.vector.reciprocal(recip[:], of[:, :, :, HD])
                    dve.drain()
                    to = heads[:, :, g * HQ * HD:(g + 1) * HQ * HD].rearrange("p t (h d) -> p t h d", h=HQ)
                    nc.vector.tensor_tensor(to, of[:, :, :, :HD], recip[:].unsqueeze(3).broadcast_to([P, QT, HQ, HD]),
                                            ALU.mult).then_inc(normalised, 1)

                def quad(now, ahead):
                    if now is not None and now[1] and ahead is None:
                        normalise(now[0], now[1] - 1)
                    if ahead is not None:
                        b, g = ahead
                        m, x = b * 4 + g, g % 2
                        for h in range(HQ):
                            for t in range(QT):
                                dve.wait_ge(scored, m * U + h * QT + t + 1)
                                nc.vector.tensor_reduce(neg_max[x][:, h * QT + t:h * QT + t + 1],
                                                        ps_s[t % 2][:, :keys(t)], AX_X, ALU.max, negate=True).then_inc(maxed, 1)
                            if h == 1 and now is not None and now[1]:
                                normalise(now[0], now[1] - 1)
                        dve.wait_ge(max_turned, m + 1)
                        dve.wait_ge(max_stacked[x], (b * DK + g // 2) * (16 * MAX_PARTS))
                        nc.vector.tensor_copy(max_parts[x][:, 0, :], ps_m[:U, :P])
                        dve.drain()
                        nc.vector.tensor_tensor(max_parts[x][:, 1, :], ps_m[:U, :P], max_parts[x][:, 0, :], ALU.subtract)
                        dve.drain().then_inc(max_split, 1)

                def output(b, at0, at1):
                    normalise(b, 3)
                    for t in range(QT):
                        dve.wait_ge(out_ready, b * QT + t + 1)
                        x_tile = res[:, b * QT + t, :]
                        taken = (taken0, taken1)[t % 2]
                        if biased:
                            nc.vector.tensor_tensor(added[:], ps_p[t % 2][:, :D], bo[:], ALU.add).then_inc(taken, 1)
                            dve.drain()
                            nc.vector.tensor_tensor(x_tile, x_tile, added[:], ALU.add)
                            dve.drain()
                        else:
                            nc.vector.tensor_tensor(x_tile, x_tile, ps_p[t % 2][:, :D], ALU.add).then_inc(taken, 1)

                steps(dve, project, values, quad, output)
    C.end_stage()


def build(nc, d, stages=None):
    with ExitStack() as ctx:
        C = Core(nc, ctx, d)
        share = ctx.enter_context(nc.sbuf_tensor("share", [P, TILES, E0], F32))
        share0, share3 = share, share[:, :, :E3]
        y = C.ctxT[:].rearrange("p c (t d) -> p (c t) d", d=D)

        def cross(l, hd, **more):
            norm_stage(nc, C)
            w = {n: d[f"{l}_w{n}"] for n in "qkvo"}
            if more.get("biased"):
                w.update({n: d[f"{l}_{n}"] for n in ("bq", "bk", "bv", "bo")})
            if more.get("masked"):
                w["mask"] = d["mask"]
            if hd == 16:
                stacked_attention_stage(nc, C, w, **more)
            else:
                attention_stage(nc, C, w, hd, **more)

        def ffn0():
            norm_stage(nc, C)
            router_stage(nc, C, dict(router=d["L0_router"], first=d["first0"]), E0, share0)
            experts_stage(nc, C, d["L0_w1"], d["L0_w2"], E0, share0, ACT.Gelu, d["L0_b1"], d["L0_b2"])

        def ffn1():
            norm_stage(nc, C)
            quantised_stage(nc, C, dict(w1=d["L1_w1"], w2=d["L1_w2"], b1=d["L1_b1"], b2=d["L1_b2"]))

        def ffn2():
            norm_stage(nc, C)
            channel_mix_stage(nc, C, dict(r=d["L2_wr"], k=d["L2_wk2"], v=d["L2_wv2"], mu=d["L2_mu"]))

        def ffn3():
            norm_stage(nc, C, keep=y, gain=d["L3_g1"])
            stacked_attention_stage(nc, C, {n: d[f"L3f_{n}"] for n in ("q", "k", "q_swap", "k_swap", "v", "o", "cos", "sin", "future")},
                                    cross=False, causal=True, rope=True, res=y)
            norm_stage(nc, C, gain=d["L3_g2"], layer=False, src=y)
            router_stage(nc, C, dict(router=d["L3_router"], first=d["first3"], lower=d["lower"]), E3, share3,
                         capacity=CAP, add=y)
            experts_stage(nc, C, d["L3_w1"], d["L3_w2"], E3, share3, ACT.Relu)

        load_stage(nc, C)
        steps = {
            "L0x": lambda: (norm_stage(nc, C), deformable_stage(nc, C, {n: d[f"L0_{n}"] for n in (
                "wkv", "bkv", "wq", "bq", "bq_col", "woff", "boff", "shift", "wo", "bo", "mask", "row")})),
            "L0f": ffn0,
            "L1x": lambda: cross("L1", 16, biased=True),
            "L1f": ffn1,
            "L2x": lambda: cross("L2", 64),
            "L2f": ffn2,
            "L3x": lambda: cross("L3", 16, biased=True, masked=True),
            "L3f": ffn3,
        }
        for name in stages or steps:
            steps[name]()
        store_stage(nc, C)


def lay_out(a):
    import numpy as np
    o = {"x": a["x"], "ctx_T": a["ctx_1024"].reshape(B * S, D).T}
    for l in ("L1", "L3"):
        o[f"{l}_wq"] = a[f"{l}_xattn_Wq"].T
        o[f"{l}_wk"] = a[f"{l}_xattn_Wk"].T
        o[f"{l}_wv"] = a[f"{l}_xattn_Wv"].T
        o[f"{l}_wo"] = a[f"{l}_xattn_Wo"].T
        o[f"{l}_bq"], o[f"{l}_bk"] = (a[f"{l}_xattn_b{n}"].reshape(DK, P).T for n in "qk")
        o[f"{l}_bv"], o[f"{l}_bo"] = a[f"{l}_xattn_bv"], a[f"{l}_xattn_bo"]
    for n in "qkvo":
        o[f"L2_w{n}"] = a[f"L2_xattn_W_{n.upper()}"]
    o["mask"] = a["mask_Bx1x1xS2_bf1"].reshape(1, B * S).view(np.uint8)
    o["L0_wkv"] = np.concatenate([a[f"L0_xattn_W{n}"].T.reshape(D, H, 16) for n in "kv"], axis=2).reshape(D, 2 * D)
    o["L0_bkv"] = np.concatenate([a[f"L0_xattn_b{n}"].reshape(H, 16) for n in "kv"], axis=1).reshape(2 * D)
    o["L0_wq"], o["L0_bq"] = a["L0_xattn_Wq"].T, a["L0_xattn_bq"]
    o["L0_bq_col"] = a["L0_xattn_bq"].reshape(DK, P).T
    o["L0_woff"], o["L0_boff"] = a["L0_xattn_Woff"].T, a["L0_xattn_boff"]
    o["L0_wo"], o["L0_bo"] = a["L0_xattn_Wo"].T, a["L0_xattn_bo"]
    o["L0_mask"] = a["mask_BxS2_if0"].reshape(B, QT, P).transpose(2, 0, 1)
    o["L0_shift"] = np.tile(np.arange(-NK // 2, NK + -NK // 2, dtype=np.float32), H)
    o["L0_row"] = (np.repeat(np.arange(H), NK) * (S + 1) + 1).astype(np.float32)
    o["L0_router"], o["L3_router"] = a["L0_ffn_router_w"], a["L3_ffn_w_router"]
    o["L0_w1"], o["L0_w2"], o["L0_b2"] = a["L0_ffn_w1"], a["L0_ffn_w2"], a["L0_ffn_b2"]
    o["L0_b1"] = a["L0_ffn_b1"].reshape(E0, FFN // P, P).transpose(0, 2, 1)
    o["L1_w1"], o["L1_w2"] = a["L1_ffn_w1"], a["L1_ffn_w2"]
    o["L1_b1"], o["L1_b2"] = a["L1_ffn_b1"].reshape(-1, P).T, a["L1_ffn_b2"].reshape(-1, P).T
    o["L2_wr"], o["L2_wk2"], o["L2_wv2"] = (a[f"L2_ffn_W_{n}"].T for n in "rkv")
    o["L2_mu"] = np.stack([a[f"L2_ffn_mu_{n}"].reshape(DK, P).T for n in "rk"], axis=1)
    o["L3_g1"], o["L3_g2"] = a["L3_ffn_g1"], a["L3_ffn_g2"]
    q, k, v = np.split(a["L3_ffn_w_qkv"], 3, axis=1)
    swap = np.arange(D) ^ 1
    o["L3f_q"], o["L3f_k"], o["L3f_q_swap"], o["L3f_k_swap"] = q, k, q[:, swap], k[:, swap]
    o["L3f_v"], o["L3f_o"] = v, a["L3_ffn_w_o"]
    o["L3_w1"], o["L3_w2"] = a["L3_ffn_w1"], a["L3_ffn_w2"]
    theta = np.float32(10000.0) ** (np.float32(-2.0) * (np.arange(8, dtype=np.float32) / np.float32(16)))
    angle = (np.arange(S, dtype=np.float32)[:, None] * theta[None, :]).astype(np.float32)
    feature = np.arange(P) % 16
    pair = feature // 2
    sign = np.where(feature % 2 == 0, -1.0, 1.0)[:, None]
    o["L3f_cos"] = (np.cos(angle).T[pair]).astype(np.float32)
    o["L3f_sin"] = (np.sin(angle).T[pair] * sign).astype(np.float32)
    later = np.triu(np.ones((P, P)), 1)
    o["L3f_future"] = (np.stack([later, later.T], axis=1) * NEG).astype(np.float32)
    o["lower"] = np.triu(np.ones((P, P), np.float32), 1)
    o["first0"], o["first3"] = np.arange(E0, 0, -1, dtype=np.float32), np.arange(E3, 0, -1, dtype=np.float32)
    return {k: np.ascontiguousarray(v) for k, v in o.items()}


def kernel(**inputs):
    import numpy as np
    import concourse.bacc as bacc
    from concourse.bass_utils import run_bass_kernel_spmd

    nc = bacc.Bacc("TRN2", target_bir_lowering=False, num_devices=1)
    arrays = {f"in_{k}": v for k, v in lay_out({k: np.asarray(v) for k, v in inputs.items()}).items()}
    d = {k[3:]: nc.dram_tensor(k, v.shape, mybir.dt.from_np(v.dtype), kind="ExternalInput").ap() for k, v in arrays.items()}
    d["out"] = nc.dram_tensor("out", (B, S, D), F32, kind="ExternalOutput").ap()
    build(nc, d)
    return run_bass_kernel_spmd(nc, [arrays], core_ids=[0]).results[0]["out"]
```

```python
from contextlib import ExitStack

import concourse.bass as bass
from concourse import mybir

F32 = mybir.dt.float32
BF16 = mybir.dt.bfloat16
I32 = mybir.dt.int32
U32 = mybir.dt.uint32
ACT = mybir.ActivationFunctionType
ALU = mybir.AluOpType
AX_X = mybir.AxisListType.X

P = 128
B, S, D = 8, 512, 256
QT = S // P
TILES = B * QT
DK = D // P
H = 16
SLOT = 32
LN_EPS = 1e-5
RMS_EPS = 1e-6
NEG = -1e30
ROUND = 1.5 * 2.0 ** 23
NK = 5
E0, E3, FFN = 14, 8, 512
SLOTS0, SLOT_ROWS = 30, 30 * 2 * P
CAP = 320


class Core:

    def __init__(self, nc, ctx, dram):
        self.nc, self.ctx, self.dram = nc, ctx, dram
        self.n = 0

        def sb(name, shape, dt=F32):
            return ctx.enter_context(nc.sbuf_tensor(name, shape, dt))

        self.x = sb("x_res", [P, TILES, D])
        self.nT = sb("normed_T", [P, DK, B * S])
        self.ctxT = sb("ctx_T", [P, DK, B * S])
        self.ident = sb("ident", [P, P])
        self.ones = sb("ones", [P, P])
        self.zeros = sb("zeros", [P, D])
        self.eps = sb("eps", [P, 2])

        self.sorted = nc.dram_tensor("sorted_tokens", [SLOT_ROWS + 2 * TILES * P, D], F32, kind="Internal").ap()
        self.sorted_zeroed = nc.alloc_semaphore(name="sorted_zeroed")
        self.stage_sems = []

    def sem(self, name):
        self.n += 1
        self.stage_sems.append(self.nc.alloc_semaphore(name=f"{name}_{self.n}"))
        return self.stage_sems[-1]

    def end_stage(self):
        self.nc.clear_and_free_semaphores(self.stage_sems)
        self.nc.all_engine_barrier()
        self.stage_sems = []


def batch_cols(b):
    return bass.ds(b * S, S)


def load_stage(nc, C):
    zeros_made = C.sem("zeros_made")
    loaded, made, memset_done = C.sem("loaded"), C.sem("made"), C.sem("memset")
    with nc.Block() as block:
        @block.sync
        def _(sp):
            sp.dma_start(C.x[:], C.dram["x"].rearrange("b (t p) d -> p (b t) d", p=P)).then_inc(loaded, 16)
            sp.dma_start(C.ctxT[:], C.dram["ctx_T"].rearrange("(k p) t -> p k t", p=P)).then_inc(loaded, 16)
            sp.wait_ge(zeros_made, 1)
            sp.dma_start(C.sorted[:SLOT_ROWS, :].rearrange("(n p) d -> p n d", p=P),
                         C.zeros[:].unsqueeze(1).broadcast_to([P, SLOT_ROWS // P, D])).then_inc(C.sorted_zeroed, 16)
            sp.wait_ge(loaded, 32)

        @block.gpsimd
        def _(pool):
            nc.gpsimd.memset(C.zeros[:], 0.0).then_inc(zeros_made, 1)
            nc.gpsimd.memset(C.ones[:], 1.0).then_inc(memset_done, 1)
            nc.gpsimd.memset(C.eps[:, 0:1], LN_EPS).then_inc(made, 1)
            nc.gpsimd.memset(C.eps[:, 1:2], RMS_EPS).then_inc(made, 1)
            pool.wait_ge(memset_done, 1)
            nc.gpsimd.affine_select(out=C.ident[:], in_=C.ones[:], compare_op=ALU.is_equal, fill=0.0, base=0,
                                    pattern=[[-1, P]], channel_multiplier=1).then_inc(made, 1)
    C.end_stage()


def norm_stage(nc, C, keep=None, gain=None, layer=True, src=None):
    src = C.x if src is None else src
    uid = C.n
    with ExitStack() as ctx:
        def sb(name, shape, dt=F32):
            return ctx.enter_context(nc.sbuf_tensor(f"{name}_{uid}", shape, dt))

        stats, mv8 = sb("stats", [P, 8, 6]), sb("mean_var_8", [P, 8, 2])
        mv = sb("mean_var", [P, TILES, 2])
        std, rstd = sb("std", [P, TILES]), sb("rstd", [P, TILES])
        sq = sb("mean_square", [P, TILES])
        normed = sb("normed", [P, 2, QT, D])
        gain_row = sb("gain_row", [P, D])
        turned = [ctx.enter_context(nc.psum_tensor(f"turned{i}_{uid}", [P, S], F32)) for i in range(2 * DK)]
        gain_loaded, var_ready, std_ready = C.sem("gain_loaded"), C.sem("var_ready"), C.sem("std_ready")
        normed_ready, turned_ready, copied = C.sem("normed_ready"), C.sem("turned_ready"), C.sem("copied")
        norms = int(layer) + int(gain is not None)

        with nc.Block() as block:
            if gain is not None:
                @block.sync
                def _(sp):
                    sp.dma_start(gain_row[:], gain.partition_broadcast(P)).then_inc(gain_loaded, 16)

            @block.vector
            def _(dve):
                if gain is not None:
                    dve.wait_ge(gain_loaded, 16)

                def moments(of):
                    with dve.Fori(0, TILES // 8) as g:
                        for t in range(8):
                            nc.vector.bn_stats(stats[:, t, :], of[:, g * 8 + t, :])
                        dve.drain()
                        for t in range(8):
                            nc.vector.bn_aggr(mv8[:, t, :], stats[:, t, :])
                        dve.drain()
                        nc.vector.tensor_copy(mv[:, bass.ds(g * 8, 8), :], mv8[:])
                    dve.drain()

                def batches(normalise):
                    with dve.Fori(0, B // 2) as pair:
                        for u in range(2):
                            b = pair * 2 + u
                            if gain is None or normalise is rms:
                                dve.wait_ge(turned_ready, pair * 2)
                            for t in range(QT):
                                ins = normalise(b * QT + t, normed[:, u, t, :])
                            if gain is None or normalise is rms:
                                ins.then_inc(normed_ready, 1)

                def centre(tile, to):
                    to = to if keep is None else keep[:, tile, :]
                    return nc.vector.tensor_scalar(to, src[:, tile, :], mv[:, bass.ds(tile, 1), 0], rstd[:, bass.ds(tile, 1)],
                                                   ALU.subtract, ALU.mult)

                def rms(tile, to):
                    return nc.vector.scalar_tensor_tensor(out=to, in0=(keep if layer else src)[:, tile, :],
                                                          scalar=rstd[:, bass.ds(tile, 1)], in1=gain_row[:],
                                                          op0=ALU.mult, op1=ALU.mult)

                if layer:
                    moments(src)
                    nc.vector.tensor_copy(sq[:], mv[:, :, 1]).then_inc(var_ready, 1)
                    dve.wait_ge(std_ready, 1)
                    nc.vector.reciprocal(rstd[:], std[:])
                    dve.drain()
                    batches(centre)
                    dve.drain()
                if gain is not None:
                    moments(keep if layer else src)
                    nc.vector.tensor_tensor(sq[:], mv[:, :, 0], mv[:, :, 0], ALU.mult)
                    dve.drain()
                    nc.vector.tensor_tensor(sq[:], sq[:], mv[:, :, 1], ALU.add).then_inc(var_ready, 1)
                    dve.wait_ge(std_ready, norms)
                    nc.vector.reciprocal(rstd[:], std[:])
                    dve.drain()
                    batches(rms)

            @block.tensor
            def _(pe):
                with pe.Fori(0, B // 2) as pair:
                    for u in range(2):
                        b = pair * 2 + u
                        pe.wait_ge(normed_ready, b + 1)
                        pe.wait_ge(copied, pair * 2)
                        for k in range(DK):
                            for t in range(QT):
                                ins = nc.tensor.transpose(turned[2 * u + k][:, t * P:(t + 1) * P],
                                                          normed[:, u, t, k * P:(k + 1) * P], C.ident[:])
                        ins.then_inc(turned_ready, 1)

            @block.scalar
            def _(act):
                for n in range(norms):
                    rms = gain is not None and n == norms - 1
                    act.wait_ge(var_ready, n + 1)
                    nc.scalar.activation(std[:], sq[:], ACT.Sqrt, bias=C.eps[:, int(rms):int(rms) + 1]).then_inc(std_ready, 1)
                with act.Fori(0, B // 2) as pair:
                    for u in range(2):
                        b = pair * 2 + u
                        act.wait_ge(turned_ready, b + 1)
                        for k in range(DK):
                            ins = nc.scalar.activation(C.nT[:, k, batch_cols(b)], turned[2 * u + k][:], ACT.Copy)
                        ins.then_inc(copied, 1)
    C.end_stage()


def store_stage(nc, C):
    stored = C.sem("stored")
    with nc.Block() as block:
        @block.sync
        def _(sp):
            sp.dma_start(C.dram["out"].rearrange("b (t p) d -> p (b t) d", p=P), C.x[:]).then_inc(stored, 16)
            sp.wait_ge(stored, 16)


def wide_attention_stage(nc, C, w):
    uid = C.n
    HD, HG = 64, 2
    G = H // HG
    U = HG * QT

    with ExitStack() as ctx:
        def sb(name, shape, dt=F32):
            return ctx.enter_context(nc.sbuf_tensor(f"{name}_{uid}", shape, dt))

        def psum(name, n):
            return [ctx.enter_context(nc.psum_tensor(f"{name}{i}_{uid}", [P, 512], F32)) for i in range(n)]

        w_all = {m: sb(f"w_{m}_all", [P, DK, H * HD]) for m in "qkv"}
        w_g = {m: sb(f"w_{m}_group", [P, DK, P]) for m in "qk"}
        wo = sb("w_o", [P, G, D])
        kv_chunk = sb("kv_chunk", [P, DK, S])
        q, k = [sb(f"q{u}", [P, S]) for u in range(2)], [sb(f"k{u}", [P, S]) for u in range(2)]
        v = [sb(f"v{u}", [P, QT, P]) for u in range(2)]
        probs = [sb(f"probs{i}", [P, S]) for i in range(4)]
        probsT = [sb(f"probsT{h}", [P, QT, S]) for h in range(HG)]
        neg_max, sums, recip = sb("neg_max", [P, 4]), sb("sums", [P, 4]), sb("recip", [P, 4])
        diag = [sb(f"diagonal{i}", [P, P]) for i in range(2)]
        headsT = sb("heads_out_T", [P, G, S])
        ps_p, ps_s, ps_t = psum("ps_proj", 2), psum("ps_scores", 2), psum("ps_turned", 2)
        ps_v, ps_o = psum("ps_values", 1)[0], psum("ps_out", 1)[0]

        weights, kv_staged, w_staged = C.sem("weights"), C.sem("kv_staged"), C.sem("w_staged")
        projected, v_projected = C.sem("projected"), C.sem("v_projected")
        qk_ready, v_ready = C.sem("qk_ready"), C.sem("v_ready")
        scored, maxed, exp_done = C.sem("scored"), C.sem("maxed"), C.sem("exp_done")
        diag_ready, turned, copied = C.sem("diag_ready"), C.sem("turned"), C.sem("copied")
        summed, heads_copied = C.sem("summed"), C.sem("heads_copied")
        out_ready, out_taken = C.sem("out_ready"), C.sem("out_taken")

        def steps(eng, project, first, second, group, output, vector=False, pairs=False):
            project(0, 0, 0)
            for s in range(2):
                first(0, 0, 0, s)

            def units(b, g, u, following):
                for s in range(0, U, 2):
                    if s == U - 2 and following is not None and not vector:
                        project(*following, 1 - u)

                    def ahead(s):
                        if s < U - 2:
                            first(b, g, u, s + 2)
                        elif following is not None:
                            first(*following, 1 - u, s + 2 - U)

                    if vector:
                        calls = ((second, s), (ahead, s), (second, s + 1), (ahead, s + 1))
                    elif pairs:
                        calls = ((ahead, s), (ahead, s + 1), (second, s), (second, s + 1))
                    else:
                        calls = ((ahead, s), (second, s), (ahead, s + 1), (second, s + 1))
                    for call, i in calls:
                        if call is second:
                            second(b, g, u, i)
                        else:
                            ahead(i)
                if vector and following is not None:
                    project(*following, 1 - u)
                group(b, g, u)

            def batch(b, last):
                with eng.Fori(0, G // 2 - 1) as pair:
                    for u in range(2):
                        units(b, pair * 2 + u, u, (b, pair * 2 + (u + 1)))
                units(b, G - 2, 0, (b, G - 1))
                units(b, G - 1, 1, None if last else (b + 1, 0))
                output(b)

            with eng.Fori(0, B - 1) as b:
                batch(b, False)
            batch(B - 1, True)

        none = lambda *a: None
        with nc.Block() as block:
            @block.sync
            def _(sp):
                for m in "qkv":
                    sp.dma_start(w_all[m][:], w[m].rearrange("(c p) n -> p c n", p=P)).then_inc(weights, 16)
                sp.dma_start(wo[:], w["o"].rearrange("(c p) n -> p c n", p=P)).then_inc(weights, 16)

            @block.gpsimd
            def _(pool):
                pool.wait_ge(weights, 64)
                with pool.Fori(0, B) as b:
                    pool.wait_ge(v_projected, b * G)
                    nc.gpsimd.tensor_copy(kv_chunk[:], C.ctxT[:, :, batch_cols(b)]).then_inc(kv_staged, 1)
                    with pool.Fori(0, G) as g:
                        pool.wait_ge(projected, b * G + g)
                        for m in "qk":
                            nc.gpsimd.tensor_copy(w_g[m][:], w_all[m][:, :, bass.ds(g * P, P)]).then_inc(w_staged, 1)

            @block.tensor
            def _(pe):
                pe.wait_ge(weights, 64)

                def project(b, g, u):
                    n = b * G + g
                    pe.wait_ge(w_staged, (n + 1) * 2)
                    pe.wait_ge(qk_ready, n)
                    if not isinstance(b, int) or b:
                        pe.wait_ge(out_taken, (b - 1 if isinstance(g, int) and g == 0 else b) * QT)
                    pe.wait_ge(kv_staged, b + 1)
                    for i in range(DK):
                        nc.tensor.matmul(ps_p[0][:], w_g["q"][:, i, :], C.nT[:, i, batch_cols(b)], start=(i == 0),
                                         stop=(i == DK - 1))
                    for i in range(DK):
                        ins = nc.tensor.matmul(ps_p[1][:], w_g["k"][:, i, :], kv_chunk[:, i, :], start=(i == 0),
                                               stop=(i == DK - 1))
                    ins.then_inc(projected, 1)
                    pe.wait_ge(v_ready, n)
                    for t in range(QT):
                        for i in range(DK):
                            ins = nc.tensor.matmul(ps_v[:, t * P:(t + 1) * P], kv_chunk[:, i, t * P:(t + 1) * P],
                                                   w_all["v"][:, i, bass.ds(g * P, P)], start=(i == 0), stop=(i == DK - 1))
                    ins.then_inc(v_projected, 1)

                def first(b, g, u, s):
                    n = b * G + g
                    h, t = s % HG, s // HG
                    own = slice(h * HD, (h + 1) * HD)
                    if s == 0:
                        pe.wait_ge(qk_ready, n + 1)
                    pe.wait_ge(exp_done, n * U + (s - 1) if s else n * U)
                    nc.tensor.matmul(ps_s[s % 2][:], q[u][own, t * P:(t + 1) * P], k[u][own, :], start=True,
                                     stop=True).then_inc(scored, 1)

                def second(b, g, u, s):
                    n = b * G + g
                    pe.wait_ge(diag_ready, n * U + s + 1)
                    pe.wait_ge(copied, n * U + max(s - 1, 0))
                    for c in range(QT):
                        ins = nc.tensor.matmul(ps_t[s % 2][:, c * P:(c + 1) * P], probs[s % 4][:, c * P:(c + 1) * P],
                                               diag[s % 2][:], start=True, stop=True)
                    ins.then_inc(turned, 1)

                def group(b, g, u):
                    n = b * G + g
                    pe.wait_ge(copied, (n + 1) * U)
                    pe.wait_ge(v_ready, n + 1)
                    pe.wait_ge(heads_copied, n)
                    for i in range(QT):
                        for h in range(HG):
                            ins = nc.tensor.matmul(ps_o[h * HD:(h + 1) * HD, :], v[u][:, i, h * HD:(h + 1) * HD],
                                                   probsT[h][:, i, :], start=(i == 0), stop=(i == QT - 1))
                    ins.then_inc(summed, 1)

                def output(b):
                    pe.wait_ge(heads_copied, (b + 1) * G)
                    pe.wait_ge(qk_ready, (b + 1) * G + (0 if isinstance(b, int) else 1))
                    for t in range(QT):
                        pe.wait_ge(out_taken, b * QT + max(t - 1, 0))
                        for c in range(G):
                            ins = nc.tensor.matmul(ps_p[t % 2][:, :D], headsT[:, c, t * P:(t + 1) * P], wo[:, c, :],
                                                   start=(c == 0), stop=(c == G - 1))
                        ins.then_inc(out_ready, 1)

                steps(pe, project, first, second, group, output, pairs=True)

            @block.scalar
            def _(act):
                def project(b, g, u):
                    act.wait_ge(projected, b * G + g + 1)
                    nc.scalar.activation(q[u][:], ps_p[0][:], ACT.Copy, scale=float(HD) ** -0.5)
                    nc.scalar.activation(k[u][:], ps_p[1][:], ACT.Copy)
                    act.drain().then_inc(qk_ready, 1)

                def first(b, g, u, s):
                    n = b * G + g
                    act.wait_ge(maxed, n * U + s + 1)
                    nc.scalar.activation(probs[s % 4][:], ps_s[s % 2][:], ACT.Exp, bias=neg_max[:, s % 4:s % 4 + 1],
                                         accum_out=sums[:, s % 4:s % 4 + 1]).then_inc(exp_done, 1)

                def second(b, g, u, s):
                    n = b * G + g
                    h, t = s % HG, s // HG
                    act.wait_ge(turned, n * U + s + 1)
                    act.wait_ge(summed, n)
                    nc.scalar.activation(probsT[h][:, :, t * P:(t + 1) * P],
                                         ps_t[s % 2][:].rearrange("p (c q) -> p c q", c=QT), ACT.Copy).then_inc(copied, 1)

                def group(b, g, u):
                    n = b * G + g
                    act.wait_ge(summed, n + 1)
                    nc.scalar.activation(headsT[:, bass.ds(g, 1), :].rearrange("p g t -> p (g t)") if not isinstance(g, int)
                                         else headsT[:, g, :], ps_o[:], ACT.Copy).then_inc(heads_copied, 1)

                steps(act, project, first, second, group, none)

            @block.vector
            def _(dve):
                def project(b, g, u):
                    dve.wait_ge(v_projected, b * G + g + 1)
                    nc.vector.tensor_copy(v[u][:], ps_v[:].rearrange("p (t c) -> p t c", t=QT)).then_inc(v_ready, 1)

                def first(b, g, u, s):
                    n = b * G + g
                    dve.wait_ge(scored, n * U + s + 1)
                    nc.vector.tensor_reduce(neg_max[:, s % 4:s % 4 + 1], ps_s[s % 2][:], AX_X, ALU.max,
                                            negate=True).then_inc(maxed, 1)

                def second(b, g, u, s):
                    n = b * G + g
                    dve.wait_ge(exp_done, n * U + s + 1)
                    nc.vector.reciprocal(recip[:, s % 4:s % 4 + 1], sums[:, s % 4:s % 4 + 1])
                    dve.drain()
                    dve.wait_ge(turned, n * U + max(s - 1, 0))
                    nc.vector.tensor_scalar(diag[s % 2][:], C.ident[:], recip[:, s % 4:s % 4 + 1], None, ALU.mult) \
                        .then_inc(diag_ready, 1)

                def output(b):
                    for t in range(QT):
                        dve.wait_ge(out_ready, b * QT + t + 1)
                        x_tile = C.x[:, b * QT + t, :]
                        nc.vector.tensor_tensor(x_tile, x_tile, ps_p[t % 2][:, :D], ALU.add).then_inc(out_taken, 1)

                steps(dve, project, first, second, none, output, vector=True)
    C.end_stage()


def stage_tensors(nc, ctx, uid):
    def sb(name, shape, dt=F32):
        return ctx.enter_context(nc.sbuf_tensor(f"{name}_{uid}", shape, dt))

    def psum(name, n, dt=F32):
        return [ctx.enter_context(nc.psum_tensor(f"{name}{i}_{uid}", [P, 2048 // mybir.dt.size(dt)], dt)) for i in range(n)]

    return sb, psum


def channel_mix_stage(nc, C, w):
    with ExitStack() as ctx:
        sb, psum = stage_tensors(nc, ctx, C.n)
        wr, wk, wv = (sb(n, [P, DK, D]) for n in ("w_r", "w_k", "w_v"))
        mu, rest = sb("mu", [P, 2, DK]), sb("one_less_mu", [P, 2, DK])
        earlier = sb("earlier", [P, S])
        mixed = [sb(f"mixed{u}", [P, 2, DK, S]) for u in range(2)]
        k_act = [sb(f"k_act{u}", [P, DK, S]) for u in range(2)]
        gate, gated = sb("gate", [P, 2, D]), sb("gated", [P, D])
        ps_k, ps_o = psum("ps_k", 2 * DK), psum("ps_rv", QT)
        weights, mixed_ready, k_ready = C.sem("weights"), C.sem("mixed_ready"), C.sem("k_ready")
        k_acted, out_ready, gate_ready, out_taken = C.sem("k_acted"), C.sem("out_ready"), C.sem("gate_ready"), C.sem("out_taken")

        with nc.Block() as block:
            @block.sync
            def _(sp):
                for to, of in ((wr, w["r"]), (wk, w["k"]), (wv, w["v"])):
                    sp.dma_start(to[:], of.rearrange("(c p) n -> p c n", p=P)).then_inc(weights, 16)
                sp.dma_start(mu[:], w["mu"]).then_inc(weights, 16)

            @block.vector
            def _(dve):
                dve.wait_ge(weights, 64)
                nc.vector.tensor_scalar(rest[:], mu[:], -1.0, 1.0, ALU.mult, ALU.add)
                nc.vector.memset(earlier[:, 0:1], 0.0)
                dve.drain()
                with dve.Fori(0, B // 2) as pair:
                    for u in range(2):
                        b = pair * 2 + u
                        dve.wait_ge(out_ready, pair * 2 * QT)
                        for i in range(2):
                            for c in range(DK):
                                nc.vector.tensor_scalar(earlier[:, 1:], C.nT[:, c, bass.ds(b * S, S - 1)],
                                                        rest[:, i, c:c + 1], None, ALU.mult)
                                dve.drain()
                                nc.vector.scalar_tensor_tensor(out=mixed[u][:, i, c, :], in0=C.nT[:, c, batch_cols(b)],
                                                               scalar=mu[:, i, c:c + 1], in1=earlier[:],
                                                               op0=ALU.mult, op1=ALU.add)
                                dve.drain()
                        dve.sem_inc(mixed_ready, 1)
                        for c in range(DK):
                            dve.wait_ge(k_ready, b * DK + c + 1)
                            bank = ps_k[u * DK + c]
                            ins = nc.vector.tensor_scalar(k_act[u][:, c, :], bank[:], 0.0, None, ALU.max)
                            dve.drain()
                            ins = nc.vector.tensor_tensor(k_act[u][:, c, :], k_act[u][:, c, :], k_act[u][:, c, :], ALU.mult)
                            ins.then_inc(k_acted, 1)
                        for t in range(QT):
                            dve.wait_ge(gate_ready, b * QT + t + 1)
                            nc.vector.tensor_tensor(gated[:], gate[:, t % 2, :], ps_o[t][:, D:], ALU.mult).then_inc(out_taken, 1)
                            dve.drain()
                            x_tile = C.x[:, b * QT + t, :]
                            nc.vector.tensor_tensor(x_tile, x_tile, gated[:], ALU.add)
                            dve.drain()

            @block.tensor
            def _(pe):
                pe.wait_ge(weights, 64)
                with pe.Fori(0, B // 2) as pair:
                    for u in range(2):
                        b = pair * 2 + u
                        pe.wait_ge(mixed_ready, b + 1)
                        pe.wait_ge(k_acted, pair * 2 * DK)
                        for m in range(DK):
                            for c in range(DK):
                                ins = nc.tensor.matmul(ps_k[u * DK + m][:], wk[:, c, m * P:(m + 1) * P],
                                                       mixed[u][:, 1, c, :], start=(c == 0), stop=(c == DK - 1))
                            ins.then_inc(k_ready, 1)
                        for t in range(QT):
                            pe.wait_ge(out_taken, b * QT)
                            for c in range(DK):
                                nc.tensor.matmul(ps_o[t][:, :D], mixed[u][:, 0, c, t * P:(t + 1) * P], wr[:, c, :],
                                                 start=(c == 0), stop=(c == DK - 1))
                            pe.wait_ge(k_acted, (b + 1) * DK)
                            for c in range(DK):
                                ins = nc.tensor.matmul(ps_o[t][:, D:], k_act[u][:, c, t * P:(t + 1) * P], wv[:, c, :],
                                                       start=(c == 0), stop=(c == DK - 1))
                            ins.then_inc(out_ready, 1)

            @block.scalar
            def _(act):
                with act.Fori(0, B // 2) as pair:
                    for u in range(2):
                        b = pair * 2 + u
                        for t in range(QT):
                            act.wait_ge(out_ready, b * QT + t + 1)
                            if t >= 2:
                                act.wait_ge(out_taken, b * QT + t - 1)
                            else:
                                act.wait_ge(out_taken, b * QT)
                            nc.scalar.activation(gate[:, t % 2, :], ps_o[t][:, :D], ACT.Sigmoid).then_inc(gate_ready, 1)
    C.end_stage()


def router_stage(nc, C, w, experts, share, capacity=None, add=None):
    E, N = experts, TILES * experts
    BITS = 30
    with ExitStack() as ctx:
        sb, psum = stage_tensors(nc, ctx, C.n)
        wr = sb("w_router", [P, DK, E])
        first = sb("first_rank", [P, E])
        logitsT = sb("logits_T", [P, 2, S])
        logits = sb("logits", [P, TILES, E])
        probs = sb("probs", [P, TILES, E])
        left, ranked, chosen = sb("left", [P, TILES, E]), sb("ranked", [P, TILES, E]), sb("chosen", [P, TILES, E])
        best = sb("best", [P, TILES])
        if capacity:
            bits, bit, trial = sb("threshold_bits", [P, E], I32), sb("bit", [P, E], I32), sb("trial_bits", [P, E], I32)
            enough = sb("enough", [P, E], I32)
            counts, room = sb("counts", [P, E]), sb("room", [P, E])
            over = sb("over", [P, TILES, E])
            equal = sb("equal", [P, E, TILES])
            before, zeros = sb("before", [P, E, TILES]), sb("zeros", [P, TILES])
            lower = sb("lower", [P, P])
        ps_l, ps_t, ps_c, ps_e = psum("ps_logits", 2), psum("ps_turned", 2), psum("ps_counts", 1), psum("ps_equal", 2)
        weights, logitsT_ready, logitsT_copied = C.sem("weights"), C.sem("logitsT_ready"), C.sem("logitsT_copied")
        turned, taken, less_max, exp_ready = C.sem("turned"), C.sem("taken"), C.sem("less_max"), C.sem("exp_ready")
        counts_ready, counted, zeroed = C.sem("counts_ready"), C.sem("counted"), C.sem("zeroed")
        loads = [(wr, w["router"].rearrange("(c p) e -> p c e", p=P)), (first, w["first"].partition_broadcast(P))]
        if capacity:
            loads.append((lower, w["lower"]))

        def each(row):
            return row[:].unsqueeze(2).broadcast_to([P, TILES, E])

        def per_expert(col):
            return col.unsqueeze(1).broadcast_to([P, TILES, E])

        with nc.Block() as block:
            @block.sync
            def _(sp):
                for to, of in loads:
                    sp.dma_start(to[:], of).then_inc(weights, 16)

            @block.gpsimd
            def _(pool):
                nc.gpsimd.memset(logitsT[:], 0.0).then_inc(zeroed, 1)

            @block.scalar
            def _(act):
                act.wait_ge(zeroed, 1)
                with act.Fori(0, B // 2) as pair:
                    for u in range(2):
                        b = pair * 2 + u
                        act.wait_ge(logitsT_ready, b + 1)
                        nc.scalar.activation(logitsT[:E, u, :], ps_l[u][:E, :], ACT.Copy).then_inc(logitsT_copied, 1)
                act.wait_ge(less_max, 1)
                nc.scalar.activation(probs[:], probs[:], ACT.Exp).then_inc(exp_ready, 1)

            @block.tensor
            def _(pe):
                pe.wait_ge(weights, 16 * len(loads))
                with pe.Fori(0, B // 2) as pair:
                    for u in range(2):
                        b = pair * 2 + u
                        pe.wait_ge(logitsT_copied, pair * 2)
                        for c in range(DK):
                            ins = nc.tensor.matmul(ps_l[u][:E, :], wr[:, c, :], C.nT[:, c, batch_cols(b)],
                                                   start=(c == 0), stop=(c == DK - 1))
                        ins.then_inc(logitsT_ready, 1)
                        pe.wait_ge(logitsT_copied, b + 1)
                        pe.wait_ge(taken, pair * 2)
                        for t in range(QT):
                            ins = nc.tensor.transpose(ps_t[u][:, t * P:(t + 1) * P], logitsT[:, u, t * P:(t + 1) * P],
                                                      C.ident[:])
                        ins.then_inc(turned, 1)
                if capacity:
                    with pe.Fori(0, BITS) as i:
                        pe.wait_ge(counts_ready, i + 1)
                        nc.tensor.matmul(ps_c[0][:, :E], C.ones[:], counts[:], start=True, stop=True).then_inc(counted, 1)
                    pe.wait_ge(counts_ready, BITS + 1)
                    nc.tensor.matmul(ps_c[0][:, :E], C.ones[:], counts[:], start=True, stop=True)
                    nc.tensor.matmul(ps_e[0][:, :N], lower[:], equal[:], start=True, stop=True)
                    nc.tensor.matmul(ps_e[1][:, :N], C.ones[:], equal[:], start=True, stop=True).then_inc(counted, 1)

            @block.vector
            def _(dve):
                dve.wait_ge(weights, 16 * len(loads))
                with dve.Fori(0, B // 2) as pair:
                    for u in range(2):
                        b = pair * 2 + u
                        dve.wait_ge(turned, b + 1)
                        nc.vector.tensor_copy(logits[:, bass.ds(b * QT, QT), :],
                                              ps_t[u][:].rearrange("p (t e) -> p t e", t=QT)[:, :, :E]).then_inc(taken, 1)
                dve.drain()
                nc.vector.tensor_reduce(best[:], logits[:], AX_X, ALU.max)
                dve.drain()
                nc.vector.tensor_tensor(probs[:], logits[:], each(best), ALU.subtract)
                dve.drain().then_inc(less_max, 1)

                def first_best(of, marks):
                    nc.vector.tensor_reduce(best[:], of[:], AX_X, ALU.max)
                    dve.drain()
                    nc.vector.tensor_tensor(ranked[:], of[:], each(best), ALU.is_equal)
                    dve.drain()
                    nc.vector.tensor_tensor(ranked[:], ranked[:], per_expert(first[:]), ALU.mult)
                    dve.drain()
                    nc.vector.tensor_reduce(best[:], ranked[:], AX_X, ALU.max)
                    dve.drain()
                    nc.vector.tensor_tensor(marks[:], ranked[:], each(best), ALU.is_equal)
                    dve.drain()

                if not capacity:
                    first_best(logits, chosen)
                dve.wait_ge(exp_ready, 1)
                nc.vector.tensor_reduce(best[:], probs[:], AX_X, ALU.add)
                dve.drain()
                nc.vector.reciprocal(best[:], best[:])
                dve.drain()
                nc.vector.tensor_tensor(probs[:], probs[:], each(best), ALU.mult)
                dve.drain()
                if capacity:
                    first_best(probs, chosen)
                    nc.vector.scalar_tensor_tensor(out=left[:], in0=chosen[:], scalar=-2.0, in1=probs[:],
                                                   op0=ALU.mult, op1=ALU.add)
                    dve.drain()
                    first_best(left, left)
                    nc.vector.tensor_tensor(chosen[:], chosen[:], left[:], ALU.add)
                    dve.drain()
                nc.vector.tensor_tensor(share[:], probs[:], chosen[:], ALU.mult)
                dve.drain()
                if capacity:
                    nc.vector.memset(bits[:], 0)
                    nc.vector.memset(trial[:], 1 << (BITS - 1))
                    nc.vector.memset(bit[:], 1 << (BITS - 1))
                    dve.drain()
                    with dve.Fori(0, BITS) as i:
                        nc.vector.tensor_tensor(over[:], share[:], per_expert(trial[:].bitcast(F32)), ALU.is_ge)
                        dve.drain()
                        nc.vector.tensor_reduce(counts[:], over[:].rearrange("p t e -> p e t"), AX_X, ALU.add)
                        dve.drain().then_inc(counts_ready, 1)
                        dve.wait_ge(counted, i + 1)
                        nc.vector.tensor_scalar(enough[:], ps_c[0][:, :E], float(capacity), -1.0, ALU.is_ge, ALU.mult)
                        dve.drain()
                        nc.vector.tensor_tensor(enough[:], enough[:], bit[:], ALU.bitwise_and)
                        dve.drain()
                        nc.vector.tensor_tensor(bits[:], bits[:], enough[:], ALU.bitwise_or)
                        nc.vector.tensor_scalar(bit[:], bit[:], 1, None, ALU.logical_shift_right)
                        dve.drain()
                        nc.vector.tensor_tensor(trial[:], bits[:], bit[:], ALU.bitwise_or)
                        dve.drain()
                    threshold = per_expert(bits[:].bitcast(F32))
                    nc.vector.tensor_tensor(over[:], share[:], threshold, ALU.is_gt)
                    nc.vector.tensor_tensor(equal[:].rearrange("p e t -> p t e"), share[:], threshold, ALU.is_equal)
                    nc.vector.memset(zeros[:], 0.0)
                    dve.drain()
                    nc.vector.tensor_reduce(counts[:], over[:].rearrange("p t e -> p e t"), AX_X, ALU.add)
                    dve.drain().then_inc(counts_ready, 1)
                    dve.wait_ge(counted, BITS + 1)
                    nc.vector.tensor_scalar(room[:], ps_c[0][:, :E], -1.0, float(capacity), ALU.mult, ALU.add)
                    totals = ps_e[1][:, :N].rearrange("p (e t) -> p e t", e=E)
                    nc.vector.memset(before[:, :, 0:1], 0.0)
                    for e in range(E):
                        nc.vector.tensor_tensor_scan(before[:, e, 1:], totals[:, e, :TILES - 1], zeros[:, :TILES - 1],
                                                     0.0, ALU.add, ALU.add)
                    dve.drain()
                    nc.vector.tensor_tensor(before[:], before[:], ps_e[0][:, :N].rearrange("p (e t) -> p e t", e=E), ALU.add)
                    dve.drain()
                    nc.vector.tensor_tensor(before[:], before[:], room[:].unsqueeze(2).broadcast_to([P, E, TILES]), ALU.is_lt)
                    dve.drain()
                    nc.vector.tensor_tensor(before[:], before[:], equal[:], ALU.mult)
                    dve.drain()
                    nc.vector.tensor_tensor(over[:], over[:], before[:].rearrange("p e t -> p t e"), ALU.add)
                    dve.drain()
                    nc.vector.tensor_tensor(share[:], share[:], over[:], ALU.mult)
                if add is not None:
                    nc.vector.tensor_tensor(C.x[:], C.x[:], add[:], ALU.add)
    C.end_stage()


def quantised_stage(nc, C, w):
    F = 1024
    FK = F // P
    with ExitStack() as ctx:
        sb, psum = stage_tensors(nc, ctx, C.n)
        w1, w2 = sb("w1", [P, FK, D]), sb("w2", [P, DK, F])
        w1q, w2q = sb("w1_int", [P, FK, D], BF16), sb("w2_int", [P, DK, F], BF16)
        w1T, w2T = sb("w1_int_T", [P, DK, F], BF16), sb("w2_int_T", [P, FK, D], BF16)
        s1, r1 = sb("w1_scale", [P, FK]), sb("w1_inverse", [P, FK])
        s2, r2 = sb("w2_scale", [P, DK]), sb("w2_inverse", [P, DK])
        b1, b2 = sb("b1", [P, FK]), sb("b2", [P, DK])
        tmp1, tmp2 = sb("tmp1", [P, FK]), sb("tmp2", [P, DK])
        top = sb("top", [P, 1])
        top_all = sb("top_all", [P, 2])
        s_in, r_in = sb("in_scale", [P, 2]), sb("in_inverse", [P, 2])
        f_scale, f_inv = sb("f_scale", [P, FK]), sb("f_inverse", [P, FK])
        d_scale, d_inv = sb("d_scale", [P, DK]), sb("d_inverse", [P, DK])
        q_scale, q_bias = sb("q_scale", [P, FK]), sb("q_bias", [P, FK])
        diag = sb("diagonals", [P, 2, DK, P])
        rows = sb("scale_and_bias_rows", [P, 2, D])
        most = sb("most", [P, FK, B])
        ident16 = sb("ident16", [P, P], BF16)
        relu_n = sb("relu_n", [P, 2, S])
        nq = sb("n_int", [P, DK, B * S], BF16)
        relu_h = sb("relu_h", [P, 2, S])
        hq = [sb(f"hidden_int{u}", [P, FK, S], BF16) for u in range(2)]
        out = sb("out", [P, D])
        ps_w = psum("ps_weights", 1, BF16)
        ps_r = psum("ps_rows", 1)
        ps_h, ps_o = psum("ps_hidden", 4), psum("ps_out", 2)
        loaded, w_ready, w_turned, w_copied = C.sem("loaded"), C.sem("w_ready"), C.sem("w_turned"), C.sem("w_copied")
        top_ready, top_reduced, n_scaled = C.sem("top_ready"), C.sem("top_reduced"), C.sem("in_scale_ready")
        relu_ready, n_ready = C.sem("relu_ready"), C.sem("n_ready")
        hid_ready, hid_maxed, diag_ready, rows_ready = C.sem("hid_ready"), C.sem("hid_maxed"), C.sem("diag_ready"), C.sem("rows_ready")
        scales_ready, hid2_ready, relu2_ready = C.sem("scales_ready"), C.sem("hid2_ready"), C.sem("relu2_ready")
        hq_ready, out_ready, out_taken = C.sem("hq_ready"), C.sem("out_ready"), C.sem("out_taken")

        def largest_to_scale(dve, i):
            nc.vector.tensor_scalar(s_in[:, i:i + 1], top_all[:, i:i + 1], 1e-8, 1.0 / 255.0, ALU.max, ALU.mult)
            dve.drain()
            nc.vector.reciprocal(r_in[:, i:i + 1], s_in[:, i:i + 1])
            dve.drain()

        def bias(dve, b, scale, inv, tmp):
            nc.vector.reciprocal(inv[:], scale[:])
            dve.drain()
            nc.vector.tensor_tensor(tmp[:], b[:], inv[:], ALU.mult)
            dve.drain()
            nc.vector.tensor_scalar(tmp[:], tmp[:], ROUND, -ROUND, ALU.add, ALU.add)
            dve.drain()
            nc.vector.tensor_tensor(b[:], tmp[:], scale[:], ALU.mult)
            dve.drain()

        with nc.Block() as block:
            @block.sync
            def _(sp):
                sp.dma_start(w1[:], w["w1"].rearrange("(c p) d -> p c d", p=P)).then_inc(loaded, 16)
                sp.dma_start(w2[:], w["w2"].rearrange("(c p) f -> p c f", p=P)).then_inc(loaded, 16)
                sp.dma_start(b1[:], w["b1"]).then_inc(loaded, 16)
                sp.dma_start(b2[:], w["b2"]).then_inc(loaded, 16)

            @block.gpsimd
            def _(pool):
                for i in range(2):
                    pool.wait_ge(top_ready, i + 1)
                    nc.gpsimd.partition_all_reduce(top_all[:, i:i + 1], top[:], P, bass.bass_isa.ReduceOp.max) \
                        .then_inc(top_reduced, 1)

            @block.vector
            def _(dve):
                dve.wait_ge(loaded, 64)
                nc.vector.tensor_copy(ident16[:], C.ident[:])
                for wt, s, r, n in ((w1, s1, r1, FK), (w2, s2, r2, DK)):
                    nc.vector.tensor_reduce(s[:], wt[:], AX_X, ALU.max, apply_absolute_value=True)
                    dve.drain()
                    nc.vector.tensor_scalar(s[:], s[:], 1e-8, 1.0 / 127.0, ALU.max, ALU.mult)
                    dve.drain()
                    nc.vector.reciprocal(r[:], s[:])
                    dve.drain()
                for wt, wq, r, n in ((w1, w1q, r1, FK), (w2, w2q, r2, DK)):
                    for i in range(n):
                        nc.vector.tensor_scalar(wt[:, i, :], wt[:, i, :], r[:, i:i + 1], ROUND, ALU.mult, ALU.add)
                    dve.drain()
                    nc.vector.tensor_scalar(wt[:], wt[:], -ROUND, 127.0, ALU.add, ALU.min)
                    dve.drain()
                    nc.vector.tensor_scalar(wq[:], wt[:], -128.0, None, ALU.max)
                dve.drain().then_inc(w_ready, 1)
                nc.vector.tensor_reduce(top[:], C.nT[:].rearrange("p c t -> p (c t)"), AX_X, ALU.max).then_inc(top_ready, 1)
                dve.wait_ge(top_reduced, 1)
                largest_to_scale(dve, 0)
                dve.sem_inc(n_scaled, 1)
                for c in range(DK):
                    with dve.Fori(0, B // 2) as pair:
                        for u in range(2):
                            b = pair * 2 + u
                            dve.wait_ge(relu_ready, b + (c * B + 1))
                            nc.vector.tensor_scalar(nq[:, c, batch_cols(b)], relu_n[:, u, :], ROUND, -ROUND,
                                                    ALU.add, ALU.add).then_inc(n_ready, 1)
                nc.vector.tensor_scalar(f_scale[:], s1[:], s_in[:, 0:1], None, ALU.mult)
                dve.drain()
                bias(dve, b1, f_scale, f_inv, tmp1)
                with dve.Fori(0, B) as b:
                    for f in range(FK):
                        dve.wait_ge(hid_ready, b * FK + f + 1)
                        nc.vector.tensor_reduce(most[:, f, bass.ds(b, 1)], ps_h[f % 4][:], AX_X, ALU.max).then_inc(hid_maxed, 1)
                dve.drain()
                nc.vector.tensor_reduce(tmp1[:], most[:], AX_X, ALU.max)
                dve.drain()
                nc.vector.tensor_tensor(tmp1[:], tmp1[:], f_scale[:], ALU.mult)
                dve.drain()
                nc.vector.tensor_tensor(tmp1[:], tmp1[:], b1[:], ALU.add)
                dve.drain()
                nc.vector.tensor_reduce(top[:], tmp1[:], AX_X, ALU.max)
                dve.drain()
                nc.vector.tensor_scalar(top[:], top[:], 0.0, None, ALU.max).then_inc(top_ready, 1)
                dve.wait_ge(top_reduced, 2)
                largest_to_scale(dve, 1)
                nc.vector.tensor_scalar(q_scale[:], f_scale[:], r_in[:, 1:2], None, ALU.mult)
                nc.vector.tensor_scalar(q_bias[:], b1[:], r_in[:, 1:2], None, ALU.mult)
                nc.vector.tensor_scalar(d_scale[:], s2[:], s_in[:, 1:2], None, ALU.mult)
                dve.drain().then_inc(scales_ready, 1)
                bias(dve, b2, d_scale, d_inv, tmp2)
                for c in range(DK):
                    nc.vector.tensor_scalar(diag[:, 0, c, :], C.ident[:], d_scale[:, c:c + 1], None, ALU.mult)
                    nc.vector.tensor_scalar(diag[:, 1, c, :], C.ident[:], b2[:, c:c + 1], None, ALU.mult)
                dve.drain().then_inc(diag_ready, 1)
                dve.wait_ge(rows_ready, 1)
                nc.vector.tensor_copy(rows[:].rearrange("p a d -> p (a d)"), ps_r[0][:])
                dve.drain()
                with dve.Fori(0, B // 2) as pair:
                    for u in range(2):
                        b = pair * 2 + u
                        for f in range(FK):
                            dve.wait_ge(relu2_ready, b * FK + f + 1)
                            dve.wait_ge(out_ready, pair * 2 * QT)
                            nc.vector.tensor_scalar(hq[u][:, f, :], relu_h[:, f % 2, :], ROUND, -ROUND,
                                                    ALU.add, ALU.add).then_inc(hq_ready, 1)
                        for t in range(QT):
                            dve.wait_ge(out_ready, b * QT + t + 1)
                            nc.vector.tensor_tensor(out[:], ps_o[t % 2][:, :D], rows[:, 0, :], ALU.mult).then_inc(out_taken, 1)
                            dve.drain()
                            nc.vector.tensor_tensor(out[:], out[:], rows[:, 1, :], ALU.add)
                            dve.drain()
                            x_tile = C.x[:, b * QT + t, :]
                            nc.vector.tensor_tensor(x_tile, x_tile, out[:], ALU.add)
                            dve.drain()

            @block.scalar
            def _(act):
                act.wait_ge(w_turned, 1)
                nc.scalar.activation(w1T[:, 0, :], ps_w[0][:], ACT.Copy).then_inc(w_copied, 1)
                act.wait_ge(w_turned, 2)
                nc.scalar.activation(w1T[:, 1, :], ps_w[0][:], ACT.Copy).then_inc(w_copied, 1)
                for i in range(2):
                    act.wait_ge(w_turned, 3 + i)
                    nc.scalar.activation(w2T[:, 4 * i:4 * i + 4, :].rearrange("p c d -> p (c d)"), ps_w[0][:],
                                         ACT.Copy).then_inc(w_copied, 1)
                act.wait_ge(n_scaled, 1)
                for c in range(DK):
                    with act.Fori(0, B // 2) as pair:
                        for u in range(2):
                            b = pair * 2 + u
                            act.wait_ge(n_ready, pair * 2 + c * B)
                            nc.scalar.activation(relu_n[:, u, :], C.nT[:, c, batch_cols(b)], ACT.Relu,
                                                 scale=r_in[:, 0:1]).then_inc(relu_ready, 1)
                act.wait_ge(scales_ready, 1)
                with act.Fori(0, B) as b:
                    for f in range(FK):
                        act.wait_ge(hid2_ready, b * FK + f + 1)
                        if f >= 2:
                            act.wait_ge(hq_ready, b * FK + f - 1)
                        else:
                            act.wait_ge(hq_ready, b * FK)
                        nc.scalar.activation(relu_h[:, f % 2, :], ps_h[f % 4][:], ACT.Relu, scale=q_scale[:, f:f + 1],
                                             bias=q_bias[:, f:f + 1]).then_inc(relu2_ready, 1)

            @block.tensor
            def _(pe):
                pe.wait_ge(w_ready, 1)
                for c in range(DK):
                    if c:
                        pe.wait_ge(w_copied, c)
                    for f in range(FK):
                        ins = nc.tensor.transpose(ps_w[0][:, f * P:(f + 1) * P], w1q[:, f, c * P:(c + 1) * P], ident16[:])
                    ins.then_inc(w_turned, 1)
                for i in range(2):
                    pe.wait_ge(w_copied, 2 + i)
                    for f in range(4):
                        for c in range(DK):
                            ins = nc.tensor.transpose(ps_w[0][:, f * D + c * P:f * D + (c + 1) * P],
                                                      w2q[:, c, (4 * i + f) * P:(4 * i + f + 1) * P], ident16[:])
                    ins.then_inc(w_turned, 1)
                pe.wait_ge(w_copied, 4)
                pe.wait_ge(n_ready, DK * B)

                def hidden(b, f, ready):
                    for c in range(DK):
                        ins = nc.tensor.matmul(ps_h[f % 4][:], w1T[:, c, f * P:(f + 1) * P], nq[:, c, batch_cols(b)],
                                               start=(c == 0), stop=(c == DK - 1))
                    ins.then_inc(ready, 1)

                with pe.Fori(0, B) as b:
                    for f in range(FK):
                        if f >= 4:
                            pe.wait_ge(hid_maxed, b * FK + f - 3)
                        else:
                            pe.wait_ge(hid_maxed, b * FK)
                        hidden(b, f, hid_ready)
                pe.wait_ge(diag_ready, 1)
                for a in range(2):
                    for c in range(DK):
                        ins = nc.tensor.matmul(ps_r[0][:, a * D + c * P:a * D + (c + 1) * P], C.ones[:], diag[:, a, c, :],
                                               start=True, stop=True)
                ins.then_inc(rows_ready, 1)
                with pe.Fori(0, B // 2) as pair:
                    for u in range(2):
                        b = pair * 2 + u
                        for f in range(FK):
                            if f >= 4:
                                pe.wait_ge(relu2_ready, b * FK + f - 3)
                            else:
                                pe.wait_ge(relu2_ready, b * FK)
                                pe.wait_ge(hid_maxed, B * FK)
                            hidden(b, f, hid2_ready)
                        for t in range(QT):
                            pe.wait_ge(hq_ready, (b + 1) * FK)
                            pe.wait_ge(out_taken, b * QT + max(t - 1, 0))
                            for f in range(FK):
                                ins = nc.tensor.matmul(ps_o[t % 2][:, :D], hq[u][:, f, t * P:(t + 1) * P], w2T[:, f, :],
                                                       start=(f == 0), stop=(f == FK - 1))
                            ins.then_inc(out_ready, 1)
    C.end_stage()




def deformable_stage(nc, C, w):
    HD, ROWS = D // H, S + 1
    N = H * NK
    HALF = H // 2
    NH = HALF * NK
    PAIR = 4 * HD
    with ExitStack() as ctx:
        sb, psum = stage_tensors(nc, ctx, C.n)
        table = [nc.dram_tensor(f"kv_table{u}", [H * ROWS, PAIR], F32, kind="Internal").ap() for u in range(2)]
        wkv, wq, wo = sb("w_kv", [P, DK, 2 * D]), sb("w_q", [P, DK, D]), sb("w_o", [P, DK, D])
        woff = sb("w_off", [P, DK, N])
        bkv, bq, bo = sb("b_kv", [P, 2 * D]), sb("b_q", [P, D]), sb("b_o", [P, D])
        bq_col, boff = sb("b_q_col", [P, DK]), sb("b_off", [P, N])
        shift, row = sb("shift", [P, N]), sb("row", [P, N])
        mask_in, unmasked = sb("mask_in", [P, B, QT], I32), sb("unmasked", [P, B, QT])
        places = sb("places", [P, QT])
        length, inv_length, neg_length = sb("length", [P, B]), sb("inv_length", [P, B]), sb("neg_length", [P, B])
        n_chunk, kv_chunk = sb("n_chunk", [P, DK, S]), sb("kv_chunk", [P, DK, S])
        qT = sb("q_T", [P, DK, S])
        kv = [sb(f"kv{u}", [P, QT, 2 * D]) for u in range(2)]
        q = [sb(f"q{u}", [P, QT, D]) for u in range(2)]
        pos, whole, over = sb("pos", [P, QT, N]), sb("whole", [P, QT, N]), sb("over", [P, QT, N])
        w_hi = [sb(f"w_hi{u}", [P, QT, N]) for u in range(2)]
        w_lo = [sb(f"w_lo{u}", [P, QT, N]) for u in range(2)]
        index = sb("index", [P, QT, N], U32)
        index_tile = [sb(f"index_tile{i}", [P, N], U32) for i in range(2)]
        got = [sb(f"gathered{i}", [P, NH, PAIR]) for i in range(2)]
        lo, hi = sb("lo", [P, NH, 2 * HD]), sb("hi", [P, NH, 2 * HD])
        prod = sb("prod", [P, NH, HD])
        score, top = sb("score", [P, HALF, NK]), sb("top", [P, HALF])
        zeros = sb("zeros", [H, PAIR])
        heads, headsT = sb("heads_out", [P, QT, D]), sb("heads_out_T", [P, DK, S])
        added = sb("added", [P, D])
        ps_kv, ps_q, ps_qT = psum("ps_kv", 2), psum("ps_q", 2), psum("ps_qT", 2)
        ps_off, ps_o = psum("ps_off", 1), psum("ps_out", 1)
        loaded, zeroed, staged = C.sem("loaded"), C.sem("zeroed"), C.sem("staged")
        gathers_begun = C.sem("gathers_begun")
        parts_ready, length_ready = C.sem("parts_ready"), C.sem("length_ready")
        places_ready, borders = C.sem("places_ready"), C.sem("borders")
        kv_ready, kv_taken, q_ready, q_taken = C.sem("kv_ready"), C.sem("kv_taken"), C.sem("q_ready"), C.sem("q_taken")
        qT_ready, qT_taken, off_ready, off_taken = C.sem("qT_ready"), C.sem("qT_taken"), C.sem("off_ready"), C.sem("off_taken")
        table_written = [C.sem(f"table_written{u}") for u in range(2)]
        index_ready, index_used = C.sem("index_ready"), C.sem("index_used")
        gathered = [C.sem(f"gathered{i}") for i in range(2)]
        got_used = [C.sem(f"got_used{i}") for i in range(2)]
        shifted, exp_ready, sampled = C.sem("shifted"), C.sem("exp_ready"), C.sem("sampled")
        headsT_turned, headsT_copied = C.sem("headsT_turned"), C.sem("headsT_copied")
        out_ready, out_taken = C.sem("out_ready"), C.sem("out_taken")
        loads = [(wkv, w["wkv"].rearrange("(c p) n -> p c n", p=P)), (wq, w["wq"].rearrange("(c p) n -> p c n", p=P)),
                 (wo, w["wo"].rearrange("(c p) n -> p c n", p=P)), (woff, w["woff"].rearrange("(c p) n -> p c n", p=P)),
                 (bq_col, w["bq_col"]), (mask_in, w["mask"])]
        loads += [(to, w[n].partition_broadcast(P)) for to, n in (
            (bkv, "bkv"), (bq, "bq"), (bo, "bo"), (boff, "boff"), (shift, "shift"), (row, "row"))]

        def table_of(u, ahead):
            rows = table[u].rearrange("(h r) c -> r h c", h=H)
            return rows[1:, :, :2 * HD] if ahead == 0 else rows[:S, :, 2 * HD:]

        with nc.Block() as block:
            @block.sync
            def _(sp):
                for to, of in loads:
                    sp.dma_start(to[:], of).then_inc(loaded, 16)
                sp.wait_ge(zeroed, 1)
                for u in range(2):
                    rows = table[u].rearrange("(h r) c -> h r c", h=H)
                    sp.dma_start(rows[:, 0, :2 * HD], zeros[:, :2 * HD]).then_inc(borders, 16)
                    sp.dma_start(rows[:, S, 2 * HD:], zeros[:, 2 * HD:]).then_inc(borders, 16)
                with sp.Fori(0, B // 2) as pair:
                    for u in range(2):
                        b = pair * 2 + u
                        sp.wait_ge(kv_taken, (b + 1) * QT)
                        for t in range(QT):
                            for ahead in range(2):
                                sp.dma_start(table_of(u, ahead)[t * P:(t + 1) * P],
                                             kv[u][:, t, :].rearrange("p (h c) -> p h c", h=H)).then_inc(table_written[u], 16)
                sp.wait_ge(table_written[0], B // 2 * 32 * QT)
                sp.wait_ge(table_written[1], B // 2 * 32 * QT)

            @block.gpsimd
            def _(pool):
                nc.gpsimd.memset(zeros[:], 0.0).then_inc(zeroed, 1)
                nc.gpsimd.iota(places[:], [[P, QT]], base=0, channel_multiplier=1,
                               allow_small_or_imprecise_dtypes=True).then_inc(places_ready, 1)
                with pool.Fori(0, B // 2) as pair:
                    for u in range(2):
                        with pool.Fori(0, QT // 2) as tpair:
                            for v in range(2):
                                tile = (pair * 2 + u) * QT + tpair * 2 + v
                                pool.wait_ge(table_written[u], (pair + 1) * (32 * QT))
                                pool.wait_ge(index_ready, tile + 1)
                                for half in range(2):
                                    pool.wait_ge(got_used[half], tile)
                                    pool.wait_ge(borders, 64)
                                    pool.sem_inc(gathers_begun, 1)
                                    for c in range(NH):
                                        n = half * NH + c
                                        nc.gpsimd.indirect_dma_start(
                                            got[half][:, c, :], None, table[u],
                                            bass.IndirectOffsetOnAxis(ap=index_tile[v][:, n:n + 1], axis=0)) \
                                            .then_inc(gathered[half], 16)

            @block.scalar
            def _(act):
                act.wait_ge(loaded, 16 * len(loads))

                def prepare(b):
                    act.wait_ge(q_ready, b * QT)
                    act.wait_ge(kv_ready, b * QT)
                    nc.scalar.activation(kv_chunk[:], C.ctxT[:, :, batch_cols(b)], ACT.Copy)
                    nc.scalar.activation(n_chunk[:], C.nT[:, :, batch_cols(b)], ACT.Copy)
                    act.drain().then_inc(staged, 1)
                    for c in range(DK):
                        act.wait_ge(qT_ready, b * DK + c + 1)
                        nc.scalar.activation(qT[:, c, :], ps_qT[c][:], ACT.Identity, bias=bq_col[:, c:c + 1]) \
                            .then_inc(qT_taken, 1)

                def batch(b, more):
                    for half in range(2 * QT):
                        act.wait_ge(shifted, b * (2 * QT) + half + 1)
                        nc.scalar.activation(score[:], score[:], ACT.Exp).then_inc(exp_ready, 1)
                        if more and half == QT - 1:
                            prepare(b + 1)

                prepare(0)
                with act.Fori(0, B - 1) as b:
                    batch(b, True)
                batch(B - 1, False)

            @block.tensor
            def _(pe):
                pe.wait_ge(loaded, 16 * len(loads))
                pe.wait_ge(parts_ready, 1)
                nc.tensor.matmul(ps_off[0][:, :B], C.ones[:], length[:], start=True, stop=True).then_inc(length_ready, 1)
                pe.wait_ge(parts_ready, 2)
                def headsT_before(b):
                    return 0 if isinstance(b, int) and b == 0 else (b - 1) * DK

                def prepare(b):
                    for c in range(DK):
                        pe.wait_ge(staged, b + 1)
                        pe.wait_ge(qT_taken, b * DK)
                        pe.wait_ge(headsT_copied, headsT_before(b))
                        for i in range(DK):
                            ins = nc.tensor.matmul(ps_qT[c][:], wq[:, i, c * P:(c + 1) * P], n_chunk[:, i, :],
                                                   start=(i == 0), stop=(i == DK - 1))
                        ins.then_inc(qT_ready, 1)
                    for t in range(QT):
                        if t >= 2:
                            pe.wait_ge(kv_taken, b * QT + t - 1)
                            pe.wait_ge(q_taken, b * QT + t - 1)
                        else:
                            pe.wait_ge(kv_taken, b * QT)
                            pe.wait_ge(q_taken, b * QT)
                        for i in range(DK):
                            ins = nc.tensor.matmul(ps_kv[t % 2][:], kv_chunk[:, i, t * P:(t + 1) * P], wkv[:, i, :],
                                                   start=(i == 0), stop=(i == DK - 1))
                        ins.then_inc(kv_ready, 1)
                        for i in range(DK):
                            ins = nc.tensor.matmul(ps_q[t % 2][:, :D], n_chunk[:, i, t * P:(t + 1) * P], wq[:, i, :],
                                                   start=(i == 0), stop=(i == DK - 1))
                        ins.then_inc(q_ready, 1)
                    pe.wait_ge(qT_taken, (b + 1) * DK)
                    pe.wait_ge(off_taken, b)
                    for t in range(QT):
                        for i in range(DK):
                            ins = nc.tensor.matmul(ps_off[0][:, t * N:(t + 1) * N], qT[:, i, t * P:(t + 1) * P],
                                                   woff[:, i, :], start=(i == 0), stop=(i == DK - 1))
                    ins.then_inc(off_ready, 1)

                def output(b):
                    for c in range(DK):
                        pe.wait_ge(sampled, b + 1)
                        for t in range(QT):
                            ins = nc.tensor.transpose(ps_qT[c][:, t * P:(t + 1) * P], heads[:, t, c * P:(c + 1) * P],
                                                      C.ident[:])
                        ins.then_inc(headsT_turned, 1)
                    for t in range(QT):
                        pe.wait_ge(headsT_copied, (b + 1) * DK)
                        pe.wait_ge(out_taken, b * QT + t)
                        for c in range(DK):
                            ins = nc.tensor.matmul(ps_o[0][:, :D], headsT[:, c, t * P:(t + 1) * P], wo[:, c, :],
                                                   start=(c == 0), stop=(c == DK - 1))
                        ins.then_inc(out_ready, 1)

                prepare(0)
                with pe.Fori(0, B - 1) as b:
                    prepare(b + 1)
                    output(b)
                output(B - 1)

            @block.vector
            def _(dve):
                dve.wait_ge(loaded, 16 * len(loads))
                dve.wait_ge(places_ready, 1)
                nc.vector.tensor_scalar(unmasked[:], mask_in[:], -1.0, 1.0, ALU.mult, ALU.add)
                dve.drain()
                nc.vector.tensor_reduce(length[:], unmasked[:], AX_X, ALU.add)
                dve.drain().then_inc(parts_ready, 1)
                dve.wait_ge(length_ready, 1)
                nc.vector.tensor_scalar(length[:], ps_off[0][:, :B], -1.0, None, ALU.add)
                dve.drain()
                nc.vector.reciprocal(inv_length[:], length[:])
                nc.vector.tensor_scalar(neg_length[:], length[:], -1.0, None, ALU.mult)
                dve.drain().then_inc(parts_ready, 1)
                def prepare(b, u, n):
                    now = bass.ds(b, 1)
                    dve.wait_ge(table_written[u], n * (32 * QT))
                    for t in range(QT):
                        dve.wait_ge(kv_ready, b * QT + t + 1)
                        nc.vector.tensor_tensor(kv[u][:, t, :], ps_kv[t % 2][:], bkv[:], ALU.add).then_inc(kv_taken, 1)
                        dve.wait_ge(q_ready, b * QT + t + 1)
                        nc.vector.tensor_tensor(q[u][:, t, :], ps_q[t % 2][:, :D], bq[:], ALU.add).then_inc(q_taken, 1)
                    dve.drain()
                    nc.vector.tensor_scalar(q[u][:], q[u][:], float(HD) ** -0.5, None, ALU.mult)
                    dve.wait_ge(off_ready, b + 1)
                    by_tile = lambda r: r[:].unsqueeze(1).broadcast_to([P, QT, N])
                    nc.vector.tensor_tensor(pos[:], ps_off[0][:, :QT * N].rearrange("p (t n) -> p t n", t=QT),
                                            by_tile(boff), ALU.add).then_inc(off_taken, 1)
                    dve.drain()
                    nc.vector.tensor_tensor(pos[:], pos[:], by_tile(shift), ALU.add)
                    dve.drain()
                    nc.vector.tensor_tensor(pos[:], pos[:], places[:].unsqueeze(2).broadcast_to([P, QT, N]), ALU.add)
                    dve.drain()
                    nc.vector.tensor_scalar(whole[:], pos[:], inv_length[:, now], ROUND, ALU.mult, ALU.add)
                    dve.drain()
                    nc.vector.tensor_scalar(whole[:], whole[:], -ROUND, neg_length[:, now], ALU.add, ALU.mult)
                    dve.drain()
                    nc.vector.tensor_tensor(pos[:], pos[:], whole[:], ALU.add)
                    dve.drain()
                    nc.vector.tensor_scalar(over[:], pos[:], 0.0, length[:, now], ALU.is_lt, ALU.mult)
                    dve.drain()
                    nc.vector.tensor_tensor(pos[:], pos[:], over[:], ALU.add)
                    dve.drain()
                    nc.vector.tensor_scalar(pos[:], pos[:], S / (S - 1.0), -0.5, ALU.mult, ALU.add)
                    dve.drain()
                    nc.vector.tensor_scalar(whole[:], pos[:], ROUND, -ROUND, ALU.add, ALU.add)
                    dve.drain()
                    nc.vector.tensor_tensor(over[:], whole[:], pos[:], ALU.is_gt)
                    dve.drain()
                    nc.vector.tensor_tensor(whole[:], whole[:], over[:], ALU.subtract)
                    dve.drain()
                    nc.vector.tensor_tensor(pos[:], pos[:], whole[:], ALU.subtract)
                    nc.vector.tensor_scalar(whole[:], whole[:], -1.0, S - 1.0, ALU.max, ALU.min)
                    dve.drain()
                    nc.vector.tensor_scalar(w_hi[u][:], pos[:], 0.5, None, ALU.mult)
                    nc.vector.tensor_scalar(w_lo[u][:], pos[:], -0.5, 0.5, ALU.mult, ALU.add)
                    nc.vector.tensor_tensor(index[:], whole[:], by_tile(row), ALU.add)
                    dve.drain()

                def batch(b, u, n, more):
                    for t in range(QT):
                        tile = b * QT + t
                        for half in range(2):
                            own = slice(half * NH, (half + 1) * NH)
                            dve.wait_ge(gathered[half], (tile + 1) * (16 * NH))
                            pairs = got[half][:]
                            by = lambda m: m[u][:, t, own].unsqueeze(2).broadcast_to([P, NH, 2 * HD])
                            nc.vector.tensor_tensor(lo[:], pairs[:, :, :2 * HD], by(w_lo), ALU.mult)
                            nc.vector.tensor_tensor(hi[:], pairs[:, :, 2 * HD:], by(w_hi), ALU.mult)
                            dve.drain().then_inc(got_used[half], 1)
                            nc.vector.tensor_tensor(lo[:], lo[:], hi[:], ALU.add)
                            dve.drain()
                            by_head = lo[:].rearrange("p (h k) c -> p h k c", h=HALF)
                            prods = prod[:].rearrange("p (h k) c -> p h k c", h=HALF)
                            query = q[u][:, t, half * (D // 2):(half + 1) * (D // 2)] \
                                .rearrange("p (h c) -> p h c", h=HALF).unsqueeze(2).broadcast_to([P, HALF, NK, HD])
                            nc.vector.tensor_tensor(prods, by_head[:, :, :, :HD], query, ALU.mult)
                            dve.drain()
                            nc.vector.tensor_reduce(score[:], prods, AX_X, ALU.add)
                            dve.drain()
                            per_head = top[:].unsqueeze(2).broadcast_to([P, HALF, NK])
                            nc.vector.tensor_reduce(top[:], score[:], AX_X, ALU.max)
                            dve.drain()
                            nc.vector.tensor_tensor(score[:], score[:], per_head, ALU.subtract)
                            dve.drain().then_inc(shifted, 1)
                            dve.wait_ge(exp_ready, tile * 2 + half + 1)
                            nc.vector.tensor_reduce(top[:], score[:], AX_X, ALU.add)
                            dve.drain()
                            nc.vector.reciprocal(top[:], top[:])
                            dve.drain()
                            nc.vector.tensor_tensor(score[:], score[:], per_head, ALU.mult)
                            dve.drain()
                            nc.vector.tensor_tensor(prods, by_head[:, :, :, HD:],
                                                    score[:].unsqueeze(3).broadcast_to([P, HALF, NK, HD]), ALU.mult)
                            dve.drain()
                            nc.vector.tensor_reduce(
                                heads[:, t, half * (D // 2):(half + 1) * (D // 2)].rearrange("p (h c) -> p h c", h=HALF),
                                prod[:].rearrange("p (h k) c -> p h c k", h=HALF), AX_X, ALU.add)
                            dve.drain()
                        if t + 2 < QT or more:
                            nc.vector.tensor_copy(index_tile[t % 2][:], index[:, (t + 2) % QT, :]).then_inc(index_ready, 1)
                        if t == 1 and more:
                            dve.drain()
                            prepare(b + 1, 1 - u, n + u)
                    dve.sem_inc(sampled, 1)
                    for c in range(DK):
                        dve.wait_ge(headsT_turned, b * DK + c + 1)
                        nc.vector.tensor_copy(headsT[:, c, :], ps_qT[c][:]).then_inc(headsT_copied, 1)
                    for t in range(QT):
                        dve.wait_ge(out_ready, b * QT + t + 1)
                        nc.vector.tensor_tensor(added[:], ps_o[0][:, :D], bo[:], ALU.add).then_inc(out_taken, 1)
                        dve.drain()
                        x_tile = C.x[:, b * QT + t, :]
                        nc.vector.tensor_tensor(x_tile, x_tile, added[:], ALU.add)
                        dve.drain()

                prepare(0, 0, 0)
                for t in range(2):
                    nc.vector.tensor_copy(index_tile[t][:], index[:, t, :]).then_inc(index_ready, 1)
                with dve.Fori(0, B // 2 - 1) as pair:
                    for u in range(2):
                        batch(pair * 2 + u, u, pair, True)
                batch(B - 2, 0, B // 2 - 1, True)
                batch(B - 1, 1, B // 2 - 1, False)
    C.end_stage()




def stacked_attention_stage(nc, C, w, cross=True, causal=False, rope=False, biased=False, masked=False, res=None):
    res = C.x if res is None else res
    uid = C.n
    HD = D // H
    HH, HQ = H // DK, H // DK // 2
    U = HQ * QT
    BLOCKS = {"q": ((0, 0, 3, True), (3, 1, 2, True), (5, 2, 1, True)),
              "k": ((0, 0, 3, False), (3, 0, 2, False), (5, 0, 1, False))}
    MAX_PARTS = 2
    MAX_ROW = 6 * HD + int(masked)
    ROWS = MAX_ROW + MAX_PARTS
    VW = SLOT
    scale = float(HD) ** -0.5
    kvT = C.ctxT if cross else C.nT
    USES0, USES1 = (3, 2) if rope else (2, 1)
    STACKS = 6 + int(masked)

    with ExitStack() as ctx:
        sb, psum = stage_tensors(nc, ctx, uid)
        names = ["q", "k", "v"] + (["q_swap", "k_swap"] if rope else [])
        W = {m: sb(f"w_{m}", [P, DK, D]) for m in names}
        wo = sb("w_o", [P, DK, D])
        kv_chunk = sb("kv_chunk", [P, DK, S])
        full = {m: sb(f"{m}_full", [P, S]) for m in "qk"}
        rest = sb("rest", [P, S])
        parts = {m: sb(f"{m}_parts", [P, 3, S], BF16) for m in "qk"}
        stack = {m: [sb(f"{m}_stack{c}", [P, HH, S], BF16) for c in range(DK)] for m in "qk"}
        v = [sb(f"v{c}", [P, QT, HH, VW]) for c in range(DK)]
        parts_dram = {m: [nc.dram_tensor(f"{m}_parts_dram{c}_{uid}", [3, HD, HH, S], BF16, kind="Internal").ap()
                          for c in range(DK)] for m in "qk"}
        row_of_ones = sb("row_of_ones", [4, P], BF16)
        neg_max = [sb(f"neg_max{x}", [P, P]) for x in range(2)]
        max_parts = [sb(f"max_parts{x}", [U, MAX_PARTS, P], BF16) for x in range(2)]
        exps = [sb(f"exps{i}", [P, HQ, S]) for i in range(2)]
        outs = sb("outputs", [P, S])
        recip = sb("recip", [P, QT, HQ])
        heads, headsT = sb("heads_out", [P, QT, D]), sb("heads_out_T", [P, DK, S])
        added = sb("added", [P, D])
        if rope:
            cos, sin = sb("cos", [P, S]), sb("sin", [P, S])
            turn = sb("turn", [P, S])
        if biased:
            bq, bk = sb("b_q", [P, DK]), sb("b_k", [P, DK])
            bv, bo = sb("b_v", [P, D]), sb("b_o", [P, D])
        if masked:
            mask_in = sb("mask_in", [1, B * S], mybir.dt.uint8)
            mask = sb("mask_bias", [1, B * S], BF16)
        if causal:
            future = sb("future", [P, 2, P])
            future16, ident16 = sb("future16", [P, 2, P], BF16), sb("ident16", [P, P], BF16)
        ps_p, ps_s, ps_t = psum("ps_proj", 2), psum("ps_scores", 2), psum("ps_scores_T", 2)
        ps_m, ps_o = psum("ps_max", 1)[0], psum("ps_out", 1)[0]

        weights, prepared, cleared = C.sem("weights"), C.sem("prepared"), C.sem("cleared")
        kv_staged, ones_made, ones_in = C.sem("kv_staged"), C.sem("ones_made"), C.sem("ones_in")
        q_projected, k_projected, v_projected = C.sem("q_projected"), C.sem("k_projected"), C.sem("v_projected")
        taken0, taken1, v_ready = C.sem("bank0_taken"), C.sem("bank1_taken"), C.sem("v_ready")
        full_ready, q_split, k_split = C.sem("full_ready"), C.sem("q_split"), C.sem("k_split")
        written = [C.sem(f"parts_written{c}") for c in range(DK)]
        stacked = [C.sem(f"stacked{g}") for g in range(4)]
        scored, maxed, max_turned, max_split = C.sem("scored"), C.sem("maxed"), C.sem("max_turned"), C.sem("max_split")
        max_stacked = [C.sem(f"max_stacked{x}") for x in range(2)]
        scored_T, exp_done, roped = C.sem("scored_T"), C.sem("exp_done"), C.sem("roped")
        summed, copied = C.sem("summed"), C.sem("copied")
        outs_turned, normalised = C.sem("outs_turned"), C.sem("normalised")
        turned, headsT_ready, out_ready = C.sem("turned"), C.sem("headsT_ready"), C.sem("out_ready")

        loads = [(W[m], w[m].rearrange("(c p) n -> p c n", p=P)) for m in names]
        loads += [(wo, w["o"].rearrange("(c p) n -> p c n", p=P))]
        if rope:
            loads += [(cos, w["cos"]), (sin, w["sin"])]
        if biased:
            loads += [(bq, w["bq"]), (bk, w["bk"]),
                      (bv, w["bv"].partition_broadcast(P)), (bo, w["bo"].partition_broadcast(P))]
        if masked:
            loads += [(mask_in, w["mask"])]
        if causal:
            loads += [(future, w["future"])]

        def keys(t):
            return (t + 1) * P if causal else S

        def first_query(t):
            return t * P if causal else 0

        def turns(b, g):
            return min(b * 4 + g + 3, B * 4) if isinstance(b, int) else b * 4 + g + 3

        def steps(eng, project, values, quad, output):
            for c in range(DK):
                project(0, c, USES0 * c, USES1 * c)
                values(0, c, USES0 * c)
            quad(None, (0, 0))
            quad(None, (0, 1))

            def batch(b, last):
                more = 0 if last else 1
                per0, per1 = DK * USES0 + 3, DK * USES1 + 3
                at0, at1 = DK * USES0 + b * per0, DK * USES1 + b * per1
                for c in range(DK):
                    if more:
                        project(b + 1, c, at0 + c * USES0, at1 + c * USES1)
                    for x in range(2):
                        g = 2 * c + x
                        ahead = (b, g + 2) if g < 2 else ((b + 1, g - 2) if more else None)
                        quad((b, g), ahead)
                    if more:
                        values(b + 1, c, at0 + c * USES0)
                output(b, at0 + more * DK * USES0, at1 + more * DK * USES1)

            with eng.Fori(0, B - 1) as b:
                batch(b, False)
            batch(B - 1, True)

        with nc.Block() as block:
            @block.sync
            def _(sp):
                for to, of in loads:
                    sp.dma_start(to[:], of).then_inc(weights, 16)
                sp.wait_ge(ones_made, 1)
                for m in "qk":
                    for c in range(DK):
                        sp.dma_start(stack[m][c][6 * HD:6 * HD + 4].rearrange("r h (a t) -> r (h a) t", t=P),
                                     row_of_ones[:].unsqueeze(1).broadcast_to([4, HH * QT, P])) \
                            .then_inc(ones_in, 16)
                sp.wait_ge(ones_in, 64)
                if masked:
                    sp.wait_ge(prepared, 1)

                def project(b, c, at0, at1):
                    before = sp.to_reg(b * (16 * STACKS))
                    halves = sp.to_reg(b * DK + c + 1)
                    sp.wait_ge(q_split, halves)
                    if not (isinstance(b, int) and b == 0):
                        sp.wait_ge(stacked[2 * c], before)
                        sp.wait_ge(stacked[2 * c + 1], before)
                    for m in "qk":
                        if m == "k":
                            sp.wait_ge(k_split, halves)
                        for i in range(3):
                            sp.dma_start(parts_dram[m][c][i].rearrange("d h t -> h d t"), parts[m][:, i, :]) \
                                .then_inc(written[c], 16)

                def stack_quad(b, g, writes):
                    c, x = g // 2, g % 2
                    own = slice(x * HQ, (x + 1) * HQ)
                    sp.wait_ge(written[c], writes)
                    for m in "qk":
                        for row, part, n, over in BLOCKS[m]:
                            rows = stack[m][c][row * HD:(row + n) * HD, own, :]
                            of = parts_dram[m][c][part:part + n if not over else part + 1, :, own, :] \
                                .rearrange("i d h t -> i d (h t)")
                            if over:
                                of = of.broadcast_to([n, HD, HQ * S])
                            sp.dma_start(rows, of).then_inc(stacked[g], 16)
                    if masked:
                        sp.dma_start(stack["k"][c][6 * HD:6 * HD + 1, own, :],
                                     mask[:, batch_cols(b)].unsqueeze(1).broadcast_to([1, HQ, S])).then_inc(stacked[g], 16)

                def quad(now, ahead):
                    if now is not None:
                        done = sp.snap((now[0] * 4 + now[1] + 1) * U)
                        writes = sp.snap((now[0] + 2) * 96)
                    if ahead is not None:
                        quads = sp.snap(ahead[0] * 4 + ahead[1] + 1)
                    if now is None:
                        stack_quad(0, ahead[1], 96)
                        stack_quad(0, ahead[1] + 2, 96)
                    elif not (isinstance(now[0], int) and now[0] == B - 1):
                        sp.wait_ge(scored_T, done)
                        stack_quad(now[0] + 1, now[1], writes)
                    if ahead is not None:
                        c, x = ahead[1] // 2, ahead[1] % 2
                        sp.wait_ge(max_split, quads)
                        for i in range(MAX_PARTS):
                            sp.dma_start(stack["q"][c][MAX_ROW + i:MAX_ROW + i + 1, x * HQ:(x + 1) * HQ, :],
                                         max_parts[x][:, i, :]).then_inc(max_stacked[x], 16)

                none = lambda *a: None
                steps(sp, project, none, quad, none)

            @block.gpsimd
            def _(pool):
                pool.wait_ge(weights, 16 * len(loads))

                def project(b, c, at0, at1):
                    if c == 0:
                        pool.wait_ge(v_projected, b * DK)
                        nc.gpsimd.tensor_copy(kv_chunk[:], kvT[:, :, batch_cols(b)]).then_inc(kv_staged, 1)
                    n = b * DK + c
                    for m, split in (("q", q_split), ("k", k_split)):
                        pool.wait_ge(full_ready, 2 * n + (1 if m == "q" else 2))
                        nc.gpsimd.tensor_tensor(rest[:], full[m][:], parts[m][:, 0, :], ALU.subtract)
                        pool.drain()
                        nc.gpsimd.tensor_copy(parts[m][:, 1, :], rest[:])
                        pool.drain()
                        nc.gpsimd.tensor_tensor(parts[m][:, 2, :], rest[:], parts[m][:, 1, :], ALU.subtract)
                        pool.drain().then_inc(split, 1)

                none = lambda *a: None
                steps(pool, project, none, none, none)

            @block.tensor
            def _(pe):
                pe.wait_ge(weights, 16 * len(loads))
                pe.wait_ge(prepared, 1)
                pe.wait_ge(cleared, 6)
                pe.wait_ge(ones_in, 64)
                pe.sem_inc(summed, 1)

                def matmuls(bank, m, c, rhs, done):
                    for i in range(DK):
                        ins = nc.tensor.matmul(bank[:], W[m][:, i, c * P:(c + 1) * P], rhs(i), start=(i == 0),
                                               stop=(i == DK - 1))
                    if done is not None:
                        ins.then_inc(done, 1)

                def project(b, c, at0, at1):
                    of_n = lambda i: C.nT[:, i, batch_cols(b)]
                    of_kv = lambda i: kvT[:, i, batch_cols(b)]
                    pe.wait_ge(taken0, at0)
                    if rope:
                        pe.wait_ge(taken1, at1)
                        matmuls(ps_p[0], "q", c, of_n, None)
                        matmuls(ps_p[1], "q_swap", c, of_n, q_projected)
                        pe.wait_ge(taken0, at0 + 1)
                        pe.wait_ge(taken1, at1 + 1)
                        matmuls(ps_p[0], "k", c, of_kv, None)
                        matmuls(ps_p[1], "k_swap", c, of_kv, k_projected)
                    else:
                        matmuls(ps_p[0], "q", c, of_n, q_projected)
                        pe.wait_ge(taken1, at1)
                        matmuls(ps_p[1], "k", c, of_kv, k_projected)

                def values(b, c, at0):
                    pe.wait_ge(taken0, at0 + USES0 - 1)
                    pe.wait_ge(kv_staged, b + 1)
                    for t in range(QT):
                        for i in range(DK):
                            ins = nc.tensor.matmul(ps_p[0][:, t * P:(t + 1) * P], kv_chunk[:, i, t * P:(t + 1) * P],
                                                   W["v"][:, i, c * P:(c + 1) * P], start=(i == 0), stop=(i == DK - 1))
                    ins.then_inc(v_projected, 1)

                def scores(b, g, u):
                    h, t = u // QT, u % QT
                    c, hh = g // 2, (g % 2) * HQ + h
                    pe.wait_ge(maxed, (b * 4 + g) * U + u)
                    if u == 0:
                        pe.wait_ge(stacked[g], (b + 1) * (16 * STACKS))
                    ins = nc.tensor.matmul(ps_s[u % 2][:, :keys(t)], stack["q"][c][:MAX_ROW, hh, t * P:(t + 1) * P],
                                           stack["k"][c][:MAX_ROW, hh, :keys(t)], start=True, stop=not causal)
                    if causal:
                        ins = nc.tensor.matmul(ps_s[u % 2][:, t * P:keys(t)], ident16[:], future16[:, 0, :],
                                               start=False, stop=True)
                    ins.then_inc(scored, 1)

                def scores_T(b, g, u):
                    i, h = u // HQ, u % HQ
                    c, x, hh = g // 2, g % 2, (g % 2) * HQ + h
                    pe.wait_ge(exp_done, (b * 4 + g) * U + u)
                    if u == 0:
                        pe.wait_ge(max_stacked[x], (b * DK + c + 1) * (16 * MAX_PARTS))
                    q0 = first_query(i)
                    ins = nc.tensor.matmul(ps_t[u % 2][:, q0:], stack["k"][c][:ROWS, hh, i * P:(i + 1) * P],
                                           stack["q"][c][:ROWS, hh, q0:], start=True, stop=not causal)
                    if causal:
                        ins = nc.tensor.matmul(ps_t[u % 2][:, q0:q0 + P], ident16[:], future16[:, 1, :],
                                               start=False, stop=True)
                    ins.then_inc(scored_T, 1)

                def sums(b, g, i):
                    c, m = g // 2, b * 4 + g
                    if i == 0:
                        pe.wait_ge(copied, m)
                        pe.wait_ge(v_ready, b * DK + c + 1)
                    pe.wait_ge(exp_done, m * U + (i + 1) * HQ + 1)
                    q0 = first_query(i)
                    for h in range(HQ):
                        ins = nc.tensor.matmul(ps_o[h * VW:(h + 1) * VW, q0:], v[c][:, i, (g % 2) * HQ + h, :],
                                               exps[i % 2][:, h, q0:], start=(i == 0), stop=(i == QT - 1))
                    ins.then_inc(summed, 1)

                def turn_outputs(b, g):
                    m = b * 4 + g
                    pe.wait_ge(copied, m + 1)
                    pe.wait_ge(max_split, turns(b, g))
                    pe.wait_ge(normalised, m)
                    for t in range(QT):
                        ins = nc.tensor.transpose(ps_m[:, t * P:(t + 1) * P], outs[:, t * P:(t + 1) * P], C.ident[:])
                    ins.then_inc(outs_turned, 1)

                def quad(now, ahead):
                    for u in range(U):
                        if now is not None:
                            scores_T(*now, u)
                        if ahead is not None:
                            scores(*ahead, u)
                        if now is not None and u == HQ - 1 and now[1]:
                            turn_outputs(now[0], now[1] - 1)
                        if now is not None and u % HQ == 1 and u > HQ:
                            sums(*now, u // HQ - 1)
                    if ahead is not None:
                        m = ahead[0] * 4 + ahead[1]
                        pe.wait_ge(maxed, (m + 1) * U + 1)
                        if now is not None:
                            pe.wait_ge(normalised, now[0] * 4 + now[1])
                        pe.wait_ge(max_split, m)
                        nc.tensor.transpose(ps_m[:, :P], neg_max[ahead[1] % 2][:], C.ident[:]).then_inc(max_turned, 1)
                    if now is not None:
                        sums(*now, QT - 1)

                def output(b, at0, at1):
                    taken = (taken0, taken1)
                    turn_outputs(b, 3)
                    for c in range(DK):
                        pe.wait_ge(taken[c], (at0, at1)[c])
                        pe.wait_ge(normalised, (b + 1) * 4)
                        for t in range(QT):
                            ins = nc.tensor.transpose(ps_p[c][:, t * P:(t + 1) * P], heads[:, t, c * P:(c + 1) * P],
                                                      C.ident[:])
                        ins.then_inc(turned, 1)
                    for t in range(QT):
                        pe.wait_ge(headsT_ready, b + 1)
                        pe.wait_ge(taken[t % 2], (at0, at1)[t % 2] + 1 + t // 2)
                        for c in range(DK):
                            ins = nc.tensor.matmul(ps_p[t % 2][:, :D], headsT[:, c, t * P:(t + 1) * P], wo[:, c, :],
                                                   start=(c == 0), stop=(c == DK - 1))
                        ins.then_inc(out_ready, 1)

                none = lambda *a: None
                steps(pe, project, values, quad, output)

            @block.scalar
            def _(act):
                act.wait_ge(prepared, 1)
                act.sem_inc(exp_done, 1)

                def project(b, c, at0, at1):
                    n = b * DK + c
                    for i, (m, ready, by, bank, taken) in enumerate((("q", q_projected, scale, 0, taken0),
                                                                     ("k", k_projected, 1.0, 1, taken1))):
                        split = q_split if m == "q" else k_split
                        act.wait_ge(split, n)
                        if c or not (isinstance(b, int) and b == 0):
                            act.wait_ge(written[1 - c], (b + c) * 96)
                        if rope:
                            act.wait_ge(roped, 2 * n + i + 1)
                            nc.scalar.activation(parts[m][:, 0, :], full[m][:], ACT.Copy).then_inc(full_ready, 1)
                        else:
                            act.wait_ge(ready, n + 1)
                            args = dict(scale=by, bias=(bq if m == "q" else bk)[:, c:c + 1] if biased else 0.0)
                            nc.scalar.activation(full[m][:], ps_p[bank][:], ACT.Identity, **args)
                            nc.scalar.activation(parts[m][:, 0, :], ps_p[bank][:], ACT.Identity, **args).then_inc(taken, 1)
                            act.drain().then_inc(full_ready, 1)

                def copy_outputs(b, g):
                    act.wait_ge(summed, (b * 4 + g + 1) * QT + 1)
                    act.wait_ge(outs_turned, b * 4 + g)
                    nc.scalar.activation(outs[:], ps_o[:], ACT.Copy).then_inc(copied, 1)

                def quad(now, ahead):
                    if now is None:
                        return
                    b, g = now
                    m = b * 4 + g
                    for u in range(U):
                        i, h = u // HQ, u % HQ
                        act.wait_ge(scored_T, m * U + u + 1)
                        if h == 0:
                            act.wait_ge(summed, m * QT + i)
                        q0 = first_query(i)
                        nc.scalar.activation(exps[i % 2][:, h, q0:], ps_t[u % 2][:, q0:], ACT.Exp).then_inc(exp_done, 1)
                        if u == HQ - 1 and g:
                            copy_outputs(b, g - 1)

                def output(b, at0, at1):
                    copy_outputs(b, 3)
                    for c in range(DK):
                        act.wait_ge(turned, b * DK + c + 1)
                        nc.scalar.activation(headsT[:, c, :], ps_p[c][:], ACT.Copy).then_inc((taken0, taken1)[c], 1)
                    act.drain().then_inc(headsT_ready, 1)

                none = lambda *a: None
                steps(act, project, none, quad, output)

            @block.vector
            def _(dve):
                dve.wait_ge(weights, 16 * len(loads))
                if masked:
                    nc.vector.tensor_scalar(mask[:], mask_in[:], 1.0, -NEG, ALU.subtract, ALU.mult)
                if biased:
                    nc.vector.tensor_scalar(bq[:], bq[:], scale, None, ALU.mult)
                if causal:
                    nc.vector.tensor_copy(future16[:], future[:])
                    nc.vector.tensor_copy(ident16[:], C.ident[:])
                dve.drain().then_inc(prepared, 2)
                nc.vector.memset(row_of_ones[:], 1.0).then_inc(ones_made, 1)
                for c in range(DK):
                    nc.vector.memset(v[c][:, :, :, HD + 1:], 0.0).then_inc(cleared, 1)
                    nc.vector.memset(v[c][:, :, :, HD:HD + 1], 1.0).then_inc(cleared, 1)
                    nc.vector.memset(neg_max[c][:], 0.0).then_inc(cleared, 1)
                dve.drain()
                dve.sem_inc(maxed, 1)

                def project(b, c, at0, at1):
                    if rope:
                        n = b * DK + c
                        for i, (m, ready, by) in enumerate((("q", q_projected, scale), ("k", k_projected, 1.0))):
                            dve.wait_ge(ready, n + 1)
                            dve.wait_ge(q_split if m == "q" else k_split, n)
                            nc.vector.scalar_tensor_tensor(out=full[m][:], in0=ps_p[0][:], scalar=by, in1=cos[:],
                                                           op0=ALU.mult, op1=ALU.mult).then_inc(taken0, 1)
                            nc.vector.scalar_tensor_tensor(out=turn[:], in0=ps_p[1][:], scalar=by, in1=sin[:],
                                                           op0=ALU.mult, op1=ALU.mult).then_inc(taken1, 1)
                            dve.drain()
                            nc.vector.tensor_tensor(full[m][:], full[m][:], turn[:], ALU.add).then_inc(roped, 1)
                            dve.drain()

                def values(b, c, at0):
                    dve.wait_ge(v_projected, b * DK + c + 1)
                    of = ps_p[0][:].rearrange("p (t h d) -> p t h d", t=QT, h=HH)
                    if biased:
                        by = bv[:, c * P:(c + 1) * P].rearrange("p (h d) -> p h d", h=HH).unsqueeze(1) \
                            .broadcast_to([P, QT, HH, HD])
                        nc.vector.tensor_tensor(v[c][:, :, :, :HD], of, by, ALU.add).then_inc(v_ready, 1)
                    else:
                        nc.vector.tensor_copy(v[c][:, :, :, :HD], of).then_inc(v_ready, 1)
                    dve.drain().then_inc(taken0, 1)

                def normalise(b, g):
                    dve.wait_ge(outs_turned, b * 4 + g + 1)
                    of = ps_m[:].rearrange("p (t h w) -> p t h w", h=HQ, t=QT)
                    nc.vector.reciprocal(recip[:], of[:, :, :, HD])
                    dve.drain()
                    to = heads[:, :, g * HQ * HD:(g + 1) * HQ * HD].rearrange("p t (h d) -> p t h d", h=HQ)
                    nc.vector.tensor_tensor(to, of[:, :, :, :HD], recip[:].unsqueeze(3).broadcast_to([P, QT, HQ, HD]),
                                            ALU.mult).then_inc(normalised, 1)

                def quad(now, ahead):
                    if now is not None and now[1] and ahead is None:
                        normalise(now[0], now[1] - 1)
                    if ahead is not None:
                        b, g = ahead
                        m, x = b * 4 + g, g % 2
                        for h in range(HQ):
                            for t in range(QT):
                                dve.wait_ge(scored, m * U + h * QT + t + 1)
                                nc.vector.tensor_reduce(neg_max[x][:, h * QT + t:h * QT + t + 1],
                                                        ps_s[t % 2][:, :keys(t)], AX_X, ALU.max, negate=True).then_inc(maxed, 1)
                            if h == 1 and now is not None and now[1]:
                                normalise(now[0], now[1] - 1)
                        dve.wait_ge(max_turned, m + 1)
                        dve.wait_ge(max_stacked[x], (b * DK + g // 2) * (16 * MAX_PARTS))
                        nc.vector.tensor_copy(max_parts[x][:, 0, :], ps_m[:U, :P])
                        dve.drain()
                        nc.vector.tensor_tensor(max_parts[x][:, 1, :], ps_m[:U, :P], max_parts[x][:, 0, :], ALU.subtract)
                        dve.drain().then_inc(max_split, 1)

                def output(b, at0, at1):
                    normalise(b, 3)
                    for t in range(QT):
                        dve.wait_ge(out_ready, b * QT + t + 1)
                        x_tile = res[:, b * QT + t, :]
                        taken = (taken0, taken1)[t % 2]
                        if biased:
                            nc.vector.tensor_tensor(added[:], ps_p[t % 2][:, :D], bo[:], ALU.add).then_inc(taken, 1)
                            dve.drain()
                            nc.vector.tensor_tensor(x_tile, x_tile, added[:], ALU.add)
                            dve.drain()
                        else:
                            nc.vector.tensor_tensor(x_tile, x_tile, ps_p[t % 2][:, :D], ALU.add).then_inc(taken, 1)

                steps(dve, project, values, quad, output)
    C.end_stage()


def sparse_experts_stage(nc, C, weights, experts, share, func, R, SLOTS, picks, lower, b2=None):
    E, FK = experts, FFN // P
    N = TILES * E
    R_ROWS = R * P
    ROWS = SLOTS * R_ROWS
    W1, W2 = DK * FFN, FK * D
    WIDTH = W1 + W2 + (FK if b2 is not None else 0)
    with ExitStack() as ctx:
        sb, psum = stage_tensors(nc, ctx, C.n)
        results = nc.dram_tensor(f"expert_results_{C.n}", [ROWS, D], F32, kind="Internal").ap()
        below = sb("below", [P, P])
        marks, marks_pos = sb("marks", [P, E, TILES]), sb("marks_pos", [P, E, TILES])
        same = sb("same", [P, E, TILES])
        zeros = sb("zeros", [P, TILES])
        number, slots, ends, base = sb("number", [P, E]), sb("slots", [P, E]), sb("ends", [P, E]), sb("base", [P, E])
        row_of = sb("row_of", [P, picks, TILES])
        gate = sb("gate", [P, picks, TILES])
        spare, own = sb("spare", [P, picks, TILES]), sb("own_spare_row", [P, picks, TILES])
        to_row, from_row = sb("to_row", [P, picks, TILES], U32), sb("from_row", [P, picks, TILES], U32)
        idx = [sb(f"idx{u}", [P, picks, QT], U32) for u in range(2)]
        w_idx = [sb(f"w_idx{u}", [P, 2], U32) for u in range(2)]
        partition, slot_no = sb("partition", [P, 1]), sb("slot_no", [P, SLOTS])
        passed, expert_of = sb("passed", [P, SLOTS, E]), sb("expert_of", [P, SLOTS])
        w_row, b2_row = sb("w_row", [P, SLOTS], U32), sb("b2_row", [P, SLOTS], U32)
        chunk = [sb(f"chunk{u}", [P, DK, S]) for u in range(2)]
        rows = [sb(f"rows{u}", [P, QT, D]) for u in range(2)]
        w_e = [sb(f"expert_weights{u}", [P, WIDTH]) for u in range(2)]
        b2_e = [sb(f"b2_{u}", [P, D]) for u in range(2)] if b2 is not None else None
        slot_in, slot_T = [sb(f"slot_in{u}", [P, R, D]) for u in range(2)], [sb(f"slot_T{u}", [P, DK, R_ROWS]) for u in range(2)]
        hidden = [sb(f"hidden{u}", [P, FK, R_ROWS]) for u in range(2)]
        slot_out = [sb(f"slot_out{u}", [P, R, D]) for u in range(2)]
        result = [sb(f"result{u}", [P, QT, picks, D]) for u in range(2)]
        ps_x, ps_h, ps_y = psum("ps_turned", 2), psum("ps_hidden", FK), psum("ps_out", 2)

        loaded, numbered = C.sem("loaded"), C.sem("numbered")
        marked, counted, placed = C.sem("marked"), C.sem("counted"), C.sem("placed")
        turned, copied, idx_ready = C.sem("turned"), C.sem("copied"), C.sem("idx_ready")
        scattered = [C.sem(f"scattered{u}") for u in range(2)]
        chunk_ready = C.sem("chunk_ready")
        begun = C.sem("begun")
        w_got, in_got, out_stored = ([C.sem(f"{n}{u}") for u in range(2)] for n in ("weights_got", "slot_loaded", "slot_stored"))
        in_turned, in_copied, hid_ready, hid_acted = C.sem("in_turned"), C.sem("in_copied"), C.sem("hid_ready"), C.sem("hid_acted")
        out_ready, out_taken = C.sem("out_ready"), C.sem("out_taken")
        added = C.sem("added")
        result_got = [C.sem(f"result_got{u}") for u in range(2)]
        PER_W = 16 * (2 if b2 is not None else 1)
        HALF_SLOTS = SLOTS // 2

        def col(a, n):
            return a[:].unsqueeze(2).broadcast_to([P, E, n])

        with nc.Block() as block:
            @block.sync
            def _(sp):
                sp.dma_start(below[:], lower).then_inc(loaded, 16)
                for u in range(2):
                    sp.wait_ge(scattered[u], B // 2 * 16 * QT * picks)

                def load(s, u):
                    sp.dma_start(slot_in[u][:], C.sorted[bass.ds(s * R_ROWS, R_ROWS), :].rearrange("(r p) d -> p r d", p=P)) \
                        .then_inc(in_got[u], 16)

                def store(s, u):
                    sp.wait_ge(out_taken, (s + 1) * R)
                    sp.dma_start(results[bass.ds(s * R_ROWS, R_ROWS), :].rearrange("(r p) d -> p r d", p=P), slot_out[u][:]) \
                        .then_inc(out_stored[u], 16)

                load(0, 0)
                load(1, 1)
                with sp.Fori(0, HALF_SLOTS - 1) as pair:
                    for u in range(2):
                        store(pair * 2 + u, u)
                        sp.wait_ge(in_turned, pair * 2 + (u + 1))
                        load(pair * 2 + (u + 2), u)
                store(SLOTS - 2, 0)
                store(SLOTS - 1, 1)

            @block.gpsimd
            def _(pool):
                nc.gpsimd.iota(partition[:], [[0, 1]], base=0, channel_multiplier=1,
                               allow_small_or_imprecise_dtypes=True).then_inc(numbered, 1)
                nc.gpsimd.iota(own[:], [[P * TILES, picks], [P, TILES]], base=ROWS + 1, channel_multiplier=1,
                               allow_small_or_imprecise_dtypes=True).then_inc(numbered, 1)
                nc.gpsimd.iota(slot_no[:], [[1, SLOTS]], base=0, channel_multiplier=0,
                               allow_small_or_imprecise_dtypes=True).then_inc(numbered, 1)
                pool.wait_ge(C.sorted_zeroed, 16)
                with pool.Fori(0, B // 2) as pair:
                    for u in range(2):
                        b = pair * 2 + u
                        pool.wait_ge(idx_ready, 1)
                        pool.wait_ge(scattered[u], pair * (16 * QT * picks))
                        nc.gpsimd.tensor_copy(idx[u][:], to_row[:, :, bass.ds(b * QT, QT)])
                        pool.drain()
                        pool.wait_ge(copied, (b + 1) * QT)
                        pool.sem_inc(begun, 1)
                        for t in range(QT):
                            for k in range(picks):
                                nc.gpsimd.indirect_dma_start(
                                    C.sorted, bass.IndirectOffsetOnAxis(ap=idx[u][:, k, t:t + 1], axis=0),
                                    rows[u][:, t, :], None).then_inc(scattered[u], 16)
                def fetch(s, u):
                    nc.gpsimd.tensor_copy(w_idx[u][:, 0:1], w_row[:, bass.ds(s, 1)])
                    nc.gpsimd.tensor_copy(w_idx[u][:, 1:2], b2_row[:, bass.ds(s, 1)])
                    pool.drain()
                    nc.gpsimd.indirect_dma_start(w_e[u][:], None, weights,
                                                 bass.IndirectOffsetOnAxis(ap=w_idx[u][:, 0:1], axis=0)).then_inc(w_got[u], 16)
                    if b2 is not None:
                        nc.gpsimd.indirect_dma_start(b2_e[u][:], None, b2,
                                                     bass.IndirectOffsetOnAxis(ap=w_idx[u][:, 1:2], axis=0)).then_inc(w_got[u], 16)

                fetch(0, 0)
                fetch(1, 1)
                with pool.Fori(0, HALF_SLOTS - 1) as pair:
                    for u in range(2):
                        pool.wait_ge(out_taken, (pair * 2 + (u + 1)) * R)
                        pool.sem_inc(begun, 1)
                        fetch(pair * 2 + (u + 2), u)
                for u in range(2):
                    pool.wait_ge(out_stored[u], HALF_SLOTS * 16)
                with pool.Fori(0, B // 2) as pair:
                    for u in range(2):
                        b = pair * 2 + u
                        pool.wait_ge(added, b)
                        nc.gpsimd.tensor_copy(idx[u][:], from_row[:, :, bass.ds(b * QT, QT)])
                        pool.drain()
                        for t in range(QT):
                            for k in range(picks):
                                nc.gpsimd.indirect_dma_start(
                                    result[u][:, t, k, :], None, results,
                                    bass.IndirectOffsetOnAxis(ap=idx[u][:, k, t:t + 1], axis=0)).then_inc(result_got[u], 16)

            @block.tensor
            def _(pe):
                pe.wait_ge(loaded, 16)
                pe.wait_ge(marked, 1)
                of = marks[:].rearrange("p e t -> p (e t)")
                nc.tensor.matmul(ps_h[0][:, :N], below[:], of, start=True, stop=True)
                nc.tensor.matmul(ps_h[1][:, :N], C.ones[:], of, start=True, stop=True).then_inc(counted, 1)
                with pe.Fori(0, B // 2) as pair:
                    for u in range(2):
                        b = pair * 2 + u
                        for t in range(QT):
                            pe.wait_ge(chunk_ready, b + 1)
                            pe.wait_ge(copied, b * QT + max(t - 1, 0))
                            for c in range(DK):
                                ins = nc.tensor.transpose(ps_x[t % 2][:, c * P:(c + 1) * P], chunk[u][:, c, t * P:(t + 1) * P],
                                                          C.ident[:])
                            ins.then_inc(turned, 1)
                pe.wait_ge(copied, TILES)
                pe.wait_ge(placed, 1)

                def turn(s, u, n):
                    pe.wait_ge(in_got[u], (n + 1) * 16)
                    pe.wait_ge(in_copied, s * DK)
                    for c in range(DK):
                        for r in range(R):
                            ins = nc.tensor.transpose(ps_x[c][:, r * P:(r + 1) * P], slot_in[u][:, r, c * P:(c + 1) * P], C.ident[:])
                    ins.then_inc(in_turned, 1)

                def slot(s, u, n, more):
                    pe.wait_ge(w_got[u], (n + 1) * PER_W)
                    pe.wait_ge(in_copied, (s + 1) * DK)
                    pe.wait_ge(hid_acted, s * FK)
                    for f in range(FK):
                        for c in range(DK):
                            ins = nc.tensor.matmul(ps_h[f][:, :R_ROWS], w_e[u][:, c * FFN + f * P:c * FFN + (f + 1) * P],
                                                   slot_T[u][:, c, :], start=(c == 0), stop=(c == DK - 1))
                        ins.then_inc(hid_ready, 1)
                    if more:
                        turn(s + 1, 1 - u, n + u)
                    for r in range(R):
                        pe.wait_ge(hid_acted, (s + 1) * FK)
                        pe.wait_ge(out_taken, s * R + (r - 1 if u else max(r - 1, 0)))
                        for f in range(FK):
                            ins = nc.tensor.matmul(ps_y[(u * R + r) % 2][:, :D], hidden[u][:, f, r * P:(r + 1) * P],
                                                   w_e[u][:, W1 + f * D:W1 + (f + 1) * D], start=(f == 0), stop=(f == FK - 1))
                        ins.then_inc(out_ready, 1)

                turn(0, 0, 0)
                with pe.Fori(0, HALF_SLOTS - 1) as pair:
                    slot(pair * 2, 0, pair, True)
                    slot(pair * 2 + 1, 1, pair, True)
                slot(SLOTS - 2, 0, HALF_SLOTS - 1, True)
                slot(SLOTS - 1, 1, HALF_SLOTS - 1, False)

            @block.scalar
            def _(act):
                with act.Fori(0, B // 2) as pair:
                    for u in range(2):
                        b = pair * 2 + u
                        act.wait_ge(scattered[u], pair * (16 * QT * picks))
                        for t in range(QT):
                            act.wait_ge(turned, b * QT + t + 1)
                            nc.scalar.activation(rows[u][:, t, :], ps_x[t % 2][:, :D], ACT.Copy).then_inc(copied, 1)

                def copy_in(s, u):
                    act.wait_ge(in_turned, s + 1)
                    for c in range(DK):
                        nc.scalar.activation(slot_T[u][:, c, :], ps_x[c][:, :R_ROWS], ACT.Copy).then_inc(in_copied, 1)

                def slot(s, u, n, more):
                    act.wait_ge(w_got[u], (n + 1) * PER_W)
                    act.wait_ge(out_ready, n * (2 * R))
                    for f in range(FK):
                        act.wait_ge(hid_ready, s * FK + f + 1)
                        nc.scalar.activation(hidden[u][:, f, :], ps_h[f][:, :R_ROWS], func,
                                             bias=w_e[u][:, W1 + W2 + f:W1 + W2 + f + 1] if b2 is not None else 0.0) \
                            .then_inc(hid_acted, 1)
                    if more:
                        copy_in(s + 1, 1 - u)

                copy_in(0, 0)
                with act.Fori(0, HALF_SLOTS - 1) as pair:
                    slot(pair * 2, 0, pair, True)
                    slot(pair * 2 + 1, 1, pair, True)
                slot(SLOTS - 2, 0, HALF_SLOTS - 1, True)
                slot(SLOTS - 1, 1, HALF_SLOTS - 1, False)

            @block.vector
            def _(dve):
                nc.vector.tensor_scalar(marks[:].rearrange("p e t -> p t e"), share[:], 0.0, None, ALU.is_gt)
                nc.vector.memset(zeros[:], 0.0)
                dve.drain().then_inc(marked, 1)
                dve.wait_ge(counted, 1)
                totals = ps_h[1][:, :N].rearrange("p (e t) -> p e t", e=E)
                nc.vector.memset(marks_pos[:, :, 0:1], 0.0)
                for e in range(E):
                    nc.vector.tensor_tensor_scan(marks_pos[:, e, 1:], totals[:, e, :TILES - 1], zeros[:, :TILES - 1],
                                                 0.0, ALU.add, ALU.add)
                dve.drain()
                nc.vector.tensor_tensor(number[:], marks_pos[:, :, TILES - 1], totals[:, :, TILES - 1], ALU.add)
                dve.drain()
                nc.vector.tensor_tensor(marks_pos[:], marks_pos[:], ps_h[0][:, :N].rearrange("p (e t) -> p e t", e=E), ALU.add)
                dve.drain().then_inc(placed, 1)
                nc.vector.tensor_scalar(slots[:], number[:], (R_ROWS - 1) / 2, 1.0 / R_ROWS, ALU.add, ALU.mult)
                dve.drain()
                nc.vector.tensor_scalar(slots[:], slots[:], ROUND, -ROUND, ALU.add, ALU.add)
                dve.drain()
                nc.vector.tensor_tensor_scan(ends[:], slots[:], zeros[:, :E], 0.0, ALU.add, ALU.add)
                dve.drain()
                nc.vector.tensor_tensor(base[:], ends[:], slots[:], ALU.subtract)
                dve.drain()
                nc.vector.tensor_scalar(base[:], base[:], float(R_ROWS), 1.0, ALU.mult, ALU.add)
                dve.drain()
                nc.vector.tensor_tensor(marks_pos[:], marks_pos[:], col(base, TILES), ALU.add)
                dve.drain()
                nc.vector.tensor_tensor(marks_pos[:], marks_pos[:], marks[:], ALU.mult)
                dve.drain()
                for k in range(picks):
                    nc.vector.tensor_reduce(row_of[:, k, :], marks_pos[:].rearrange("p e t -> p t e"), AX_X, ALU.max)
                    dve.drain()
                    nc.vector.tensor_tensor(same[:], marks_pos[:], row_of[:, k, :].unsqueeze(1).broadcast_to([P, E, TILES]),
                                            ALU.is_equal)
                    dve.drain()
                    nc.vector.tensor_tensor(marks[:], same[:], share[:].rearrange("p t e -> p e t"), ALU.mult)
                    if k < picks - 1:
                        dve.drain()
                        nc.vector.tensor_tensor(same[:], same[:], marks_pos[:], ALU.mult)
                    dve.drain()
                    nc.vector.tensor_reduce(gate[:, k, :], marks[:].rearrange("p e t -> p t e"), AX_X, ALU.add)
                    if k < picks - 1:
                        nc.vector.tensor_tensor(marks_pos[:], marks_pos[:], same[:], ALU.subtract)
                    dve.drain()
                dve.wait_ge(numbered, 3)
                nc.vector.tensor_scalar(spare[:], row_of[:], 0.0, None, ALU.is_equal)
                nc.vector.scalar_tensor_tensor(out=gate[:], in0=row_of[:], scalar=0.0, in1=gate[:], op0=ALU.is_gt, op1=ALU.mult)
                dve.drain()
                nc.vector.tensor_tensor(spare[:], spare[:], own[:], ALU.mult)
                dve.drain()
                nc.vector.tensor_scalar(spare[:], spare[:], -1.0, None, ALU.add)
                dve.drain()
                nc.vector.tensor_tensor(to_row[:], row_of[:], spare[:], ALU.add)
                nc.vector.tensor_scalar(from_row[:], row_of[:], -1.0, 0.0, ALU.add, ALU.max)
                nc.vector.tensor_tensor(passed[:], ends[:].unsqueeze(1).broadcast_to([P, SLOTS, E]),
                                        slot_no[:].unsqueeze(2).broadcast_to([P, SLOTS, E]), ALU.is_le)
                dve.drain()
                nc.vector.tensor_reduce(expert_of[:], passed[:], AX_X, ALU.add)
                dve.drain()
                nc.vector.tensor_scalar(expert_of[:], expert_of[:], float(E - 1), None, ALU.min)
                dve.drain()
                nc.vector.tensor_copy(b2_row[:], expert_of[:])
                nc.vector.tensor_scalar(w_row[:], expert_of[:], float(P), partition[:], ALU.mult, ALU.add)
                dve.drain()

                dve.drain()
                dve.sem_inc(idx_ready, 1)
                with dve.Fori(0, B // 2) as pair:
                    for u in range(2):
                        b = pair * 2 + u
                        dve.wait_ge(turned, pair * (2 * QT))
                        nc.vector.tensor_copy(chunk[u][:], C.nT[:, :, batch_cols(b)]).then_inc(chunk_ready, 1)
                dve.sem_inc(added, 1)

                def slot(s, u, n):
                    for r in range(R):
                        dve.wait_ge(out_ready, s * R + r + 1)
                        if r == 0 and not (isinstance(n, int) and n == 0):
                            dve.wait_ge(out_stored[u], n * 16)
                        if b2 is not None:
                            nc.vector.tensor_tensor(slot_out[u][:, r, :], ps_y[(u * R + r) % 2][:, :D], b2_e[u][:], ALU.add).then_inc(out_taken, 1)
                        else:
                            nc.vector.tensor_copy(slot_out[u][:, r, :], ps_y[(u * R + r) % 2][:, :D]).then_inc(out_taken, 1)

                with dve.Fori(0, HALF_SLOTS - 1) as pair:
                    slot(pair * 2, 0, pair)
                    slot(pair * 2 + 1, 1, pair)
                slot(SLOTS - 2, 0, HALF_SLOTS - 1)
                slot(SLOTS - 1, 1, HALF_SLOTS - 1)
                with dve.Fori(0, B // 2) as pair:
                    for u in range(2):
                        b = pair * 2 + u
                        dve.wait_ge(result_got[u], (pair + 1) * (16 * QT * picks))
                        for k in range(picks):
                            for t in range(QT):
                                x_tile = C.x[:, b * QT + t, :]
                                nc.vector.scalar_tensor_tensor(out=x_tile, in0=result[u][:, t, k, :],
                                                               scalar=gate[:, k, bass.ds(b * QT + t, 1)], in1=x_tile,
                                                               op0=ALU.mult, op1=ALU.add)
                            dve.drain()
                        dve.sem_inc(added, 1)

    C.end_stage()


def build(nc, d, stages=None):
    with ExitStack() as ctx:
        C = Core(nc, ctx, d)
        share = ctx.enter_context(nc.sbuf_tensor("share", [P, TILES, E0], F32))
        share0, share3 = share, share[:, :, :E3]
        y = C.ctxT[:].rearrange("p c (t d) -> p (c t) d", d=D)

        def cross(l, **more):
            norm_stage(nc, C)
            w = {n: d[f"{l}_w{n}"] for n in "qkvo"}
            w.update({n: d[f"{l}_{n}"] for n in ("bq", "bk", "bv", "bo")})
            w["mask"] = d["mask"]
            stacked_attention_stage(nc, C, w, biased=True, **more)

        def ffn0():
            norm_stage(nc, C)
            router_stage(nc, C, dict(router=d["L0_router"], first=d["first0"]), E0, share0)
            sparse_experts_stage(nc, C, d["L0_experts"], E0, share0, ACT.Gelu, 2, SLOTS0, 1, d["lower"], d["L0_b2"])

        def ffn1():
            norm_stage(nc, C)
            quantised_stage(nc, C, dict(w1=d["L1_w1"], w2=d["L1_w2"], b1=d["L1_b1"], b2=d["L1_b2"]))

        def ffn2():
            norm_stage(nc, C)
            channel_mix_stage(nc, C, dict(r=d["L2_wr"], k=d["L2_wk2"], v=d["L2_wv2"], mu=d["L2_mu"]))

        def ffn3():
            norm_stage(nc, C, keep=y, gain=d["L3_g1"])
            stacked_attention_stage(nc, C, {n: d[f"L3f_{n}"] for n in ("q", "k", "q_swap", "k_swap", "v", "o", "cos", "sin", "future")},
                                    cross=False, causal=True, rope=True, res=y)
            norm_stage(nc, C, gain=d["L3_g2"], layer=False, src=y)
            router_stage(nc, C, dict(router=d["L3_router"], first=d["first3"], lower=d["lower"]), E3, share3,
                         capacity=CAP, add=y)
            sparse_experts_stage(nc, C, d["L3_experts"], E3, share3, ACT.Relu, 3, E3, 2, d["lower"])

        load_stage(nc, C)
        steps = {
            "L0x": lambda: (norm_stage(nc, C), deformable_stage(nc, C, {n: d[f"L0_{n}"] for n in (
                "wkv", "bkv", "wq", "bq", "bq_col", "woff", "boff", "shift", "wo", "bo", "mask", "row")})),
            "L0f": ffn0,
            "L1x": lambda: cross("L1"),
            "L1f": ffn1,
            "L2x": lambda: (norm_stage(nc, C), wide_attention_stage(nc, C, {n: d[f"L2_w{n}"] for n in "qkvo"})),
            "L2f": ffn2,
            "L3x": lambda: cross("L3", masked=True),
            "L3f": ffn3,
        }
        for name in stages or steps:
            steps[name]()
        store_stage(nc, C)


def lay_out(a):
    import numpy as np
    o = {"x": a["x"], "ctx_T": a["ctx_1024"].reshape(B * S, D).T}
    for l in ("L1", "L3"):
        o[f"{l}_wq"] = a[f"{l}_xattn_Wq"].T
        o[f"{l}_wk"] = a[f"{l}_xattn_Wk"].T
        o[f"{l}_wv"] = a[f"{l}_xattn_Wv"].T
        o[f"{l}_wo"] = a[f"{l}_xattn_Wo"].T
        o[f"{l}_bq"], o[f"{l}_bk"] = (a[f"{l}_xattn_b{n}"].reshape(DK, P).T for n in "qk")
        o[f"{l}_bv"], o[f"{l}_bo"] = a[f"{l}_xattn_bv"], a[f"{l}_xattn_bo"]
    for n in "qkvo":
        o[f"L2_w{n}"] = a[f"L2_xattn_W_{n.upper()}"]
    o["mask"] = a["mask_Bx1x1xS2_bf1"].reshape(1, B * S).view(np.uint8)
    o["L0_wkv"] = np.concatenate([a[f"L0_xattn_W{n}"].T.reshape(D, H, 16) for n in "kv"], axis=2).reshape(D, 2 * D)
    o["L0_bkv"] = np.concatenate([a[f"L0_xattn_b{n}"].reshape(H, 16) for n in "kv"], axis=1).reshape(2 * D)
    o["L0_wq"], o["L0_bq"] = a["L0_xattn_Wq"].T, a["L0_xattn_bq"]
    o["L0_bq_col"] = a["L0_xattn_bq"].reshape(DK, P).T
    o["L0_woff"], o["L0_boff"] = a["L0_xattn_Woff"].T, a["L0_xattn_boff"]
    o["L0_wo"], o["L0_bo"] = a["L0_xattn_Wo"].T, a["L0_xattn_bo"]
    o["L0_mask"] = a["mask_BxS2_if0"].reshape(B, QT, P).transpose(2, 0, 1)
    o["L0_shift"] = np.tile(np.arange(-NK // 2, NK + -NK // 2, dtype=np.float32), H)
    o["L0_row"] = (np.repeat(np.arange(H), NK) * (S + 1) + 1).astype(np.float32)
    o["L0_router"], o["L3_router"] = a["L0_ffn_router_w"], a["L3_ffn_w_router"]
    def by_partition(w):
        return w.reshape(w.shape[0], -1, P, w.shape[-1]).transpose(0, 2, 1, 3).reshape(w.shape[0] * P, -1)

    o["L0_experts"] = np.concatenate([by_partition(a["L0_ffn_w1"]), by_partition(a["L0_ffn_w2"]),
                                      by_partition(a["L0_ffn_b1"][:, :, None])], axis=1)
    o["L0_b2"] = a["L0_ffn_b2"]
    o["L1_w1"], o["L1_w2"] = a["L1_ffn_w1"], a["L1_ffn_w2"]
    o["L1_b1"], o["L1_b2"] = a["L1_ffn_b1"].reshape(-1, P).T, a["L1_ffn_b2"].reshape(-1, P).T
    o["L2_wr"], o["L2_wk2"], o["L2_wv2"] = (a[f"L2_ffn_W_{n}"].T for n in "rkv")
    o["L2_mu"] = np.stack([a[f"L2_ffn_mu_{n}"].reshape(DK, P).T for n in "rk"], axis=1)
    o["L3_g1"], o["L3_g2"] = a["L3_ffn_g1"], a["L3_ffn_g2"]
    q, k, v = np.split(a["L3_ffn_w_qkv"], 3, axis=1)
    swap = np.arange(D) ^ 1
    o["L3f_q"], o["L3f_k"], o["L3f_q_swap"], o["L3f_k_swap"] = q, k, q[:, swap], k[:, swap]
    o["L3f_v"], o["L3f_o"] = v, a["L3_ffn_w_o"]
    o["L3_experts"] = np.concatenate([by_partition(a["L3_ffn_w1"]), by_partition(a["L3_ffn_w2"])], axis=1)
    theta = np.float32(10000.0) ** (np.float32(-2.0) * (np.arange(8, dtype=np.float32) / np.float32(16)))
    angle = (np.arange(S, dtype=np.float32)[:, None] * theta[None, :]).astype(np.float32)
    feature = np.arange(P) % 16
    pair = feature // 2
    sign = np.where(feature % 2 == 0, -1.0, 1.0)[:, None]
    o["L3f_cos"] = (np.cos(angle).T[pair]).astype(np.float32)
    o["L3f_sin"] = (np.sin(angle).T[pair] * sign).astype(np.float32)
    later = np.triu(np.ones((P, P)), 1)
    o["L3f_future"] = (np.stack([later, later.T], axis=1) * NEG).astype(np.float32)
    o["lower"] = np.triu(np.ones((P, P), np.float32), 1)
    o["first0"], o["first3"] = np.arange(E0, 0, -1, dtype=np.float32), np.arange(E3, 0, -1, dtype=np.float32)
    return {k: np.ascontiguousarray(v) for k, v in o.items()}


def kernel(**inputs):
    import numpy as np
    import concourse.bacc as bacc
    from concourse.bass_utils import run_bass_kernel_spmd

    nc = bacc.Bacc("TRN2", target_bir_lowering=False, num_devices=1)
    arrays = {f"in_{k}": v for k, v in lay_out({k: np.asarray(v) for k, v in inputs.items()}).items()}
    d = {k[3:]: nc.dram_tensor(k, v.shape, mybir.dt.from_np(v.dtype), kind="ExternalInput").ap() for k, v in arrays.items()}
    d["out"] = nc.dram_tensor("out", (B, S, D), F32, kind="ExternalOutput").ap()
    build(nc, d)
    return run_bass_kernel_spmd(nc, [arrays], core_ids=[0]).results[0]["out"]
```
